# Optimizing a Trainium2 kernel written in Bass

```python
import numpy as np
import jax
import jax.numpy as jnp

def _softmax(x, axis=-1):
    return jax.nn.softmax(x, axis=axis)

def _gelu(x):
    return jax.nn.gelu(x, approximate=True)

def _silu(x):
    return jax.nn.silu(x)

def _sigmoid(x):
    return jax.nn.sigmoid(x)

def _layernorm(x, axis=-1, eps=1e-05):
    m = jnp.mean(x, axis=axis, keepdims=True)
    v = jnp.var(x, axis=axis, keepdims=True)
    return (x - m) / jnp.sqrt(v + eps)

def _scatter_add(tgt, idx, src, axis=0):
    return tgt.at[idx].add(src)

def _segment_sum(src, seg, n):
    return jax.ops.segment_sum(src, seg, n)
kernel_name = 'mk_lm_tower_d2_tok_ids256_r4_bf4333'

def setup_inputs(seed: int=0):
    np.random.seed(seed)
    _w = jnp.asarray

    def _rec_inputs():
        import jax
        import jax.numpy as jnp
        _rk = jax.random.key(seed)
        x = jax.random.randint(jax.random.fold_in(_rk, 1), (32, 512), 0, 64, jnp.int32)
        return x
    x = _rec_inputs()

    def _L0_tok_setup():
        import jax, jax.numpy as jnp
        import numpy as np
        BASE = 257
        HASH_MOD = 1024
        WINDOWS = (2, 4, 8, 16)
        MATCH_OFFSETS = (1, 2, 4, 8)
        CHUNK = 32
        EPS_LN = 1e-05

        def _shift_right(x, k):
            B, T = x.shape
            return jnp.concatenate([jnp.zeros((B, k), x.dtype), x[:, :T - k]], axis=1)

        def _rolling_hashes(chars):
            c = chars.astype(jnp.int32)
            hs = []
            for w in WINDOWS:
                acc = jnp.zeros_like(c)
                p = 1
                for j in range(w):
                    acc = acc + _shift_right(c, j) * p
                    p = p * BASE % HASH_MOD
                hs.append(acc % HASH_MOD)
            return jnp.stack(hs, axis=2)

        def _match_features(chars):
            feats = []
            for k in MATCH_OFFSETS:
                m = (chars == _shift_right(chars, k)).astype(jnp.float32)
                m = m.at[:, :k].set(0.0)
                feats.append(m)
            return jnp.stack(feats, axis=-1)

        def _layer_norm(x, g, b):
            mu = jnp.mean(x, axis=-1, keepdims=True)
            var = jnp.mean((x - mu) ** 2, axis=-1, keepdims=True)
            return (x - mu) * jax.lax.rsqrt(var + EPS_LN) * g + b

        def _forward(chars, emb_byte, hash_tables, Wq, bq, conv_w, conv_b, Win, b_in, Wg, bg, Wi, bi, Wo, bo, ln_g, ln_b, mlp_w, mlp_b, Wout, bout):
            B, T = chars.shape
            byte_emb = emb_byte[chars]
            hidx = _rolling_hashes(chars)
            scale_embeds = jnp.stack([hash_tables[s][hidx[:, :, s]] for s in range(len(WINDOWS))], axis=2)
            E = scale_embeds.shape[-1]
            q = byte_emb @ Wq + bq
            scores = jnp.einsum('bte,btse->bts', q, scale_embeds) / jnp.sqrt(jnp.float32(E))
            w = jax.nn.softmax(scores, axis=-1)
            hash_feat = jnp.einsum('bts,btse->bte', w, scale_embeds)
            C = hash_feat.shape[-1]
            kk = conv_w.shape[-1]
            ht = jnp.moveaxis(hash_feat, 1, 2)
            ht = jnp.pad(ht, ((0, 0), (0, 0), (kk - 1, 0)))
            ht = jax.lax.conv_general_dilated(ht, conv_w, window_strides=(1,), padding='VALID', dimension_numbers=('NCH', 'OIH', 'NCH'), feature_group_count=C)
            hash_feat = jax.nn.silu(jnp.moveaxis(ht + conv_b[None, :, None], 2, 1))
            mf = _match_features(chars)
            feat = jnp.concatenate([byte_emb, hash_feat, mf], axis=-1)
            h = jax.nn.silu(feat @ Win + b_in)
            gates = jax.nn.sigmoid(h @ Wg + bg)
            drive = (1.0 - gates) * (h @ Wi + bi)
            S = gates.shape[-1]
            nC = T // CHUNK
            g = gates.reshape(B, nC, CHUNK, S).transpose(1, 0, 2, 3)
            d = drive.reshape(B, nC, CHUNK, S).transpose(1, 0, 2, 3)

            def step(hc, ab):
                a, b = ab
                log_a = jnp.log(jnp.maximum(a, 1e-06))
                cum_a = jnp.exp(jnp.cumsum(log_a, axis=1))
                inv = 1.0 / jnp.maximum(cum_a, 1e-08)
                cum_wb = jnp.cumsum(b * inv, axis=1)
                out = cum_a * (hc[:, None, :] + cum_wb)
                return (out[:, -1], out)
            _, states = jax.lax.scan(step, jnp.zeros((B, S), h.dtype), (g, d))
            states = states.transpose(1, 0, 2, 3).reshape(B, T, S)
            h = _layer_norm(h + states @ Wo + bo, ln_g, ln_b)
            for l in range(mlp_w.shape[0]):
                h = h + jax.nn.silu(h @ mlp_w[l] + mlp_b[l])
            return h @ Wout + bout
        key = jax.random.key(seed)
        ks = jax.random.split(key, 12)
        B, T, V = (8, 2048, 64)
        EB, E, H, SS, KC, NM, NR = (64, 64, 128, 32, 4, 4, 3)
        feat = EB + E + NM

        def lin(k, i, o):
            return (jax.random.normal(k, (i, o), jnp.float32) / np.sqrt(i)).astype(jnp.float32)
        return {'chars': jax.random.randint(ks[0], (B, T), 0, V), 'emb_byte': jax.random.normal(ks[1], (V, EB), jnp.float32) * 0.02, 'hash_tables': jax.random.normal(ks[2], (len(WINDOWS), HASH_MOD, E), jnp.float32) * 0.02, 'Wq': lin(ks[3], EB, E), 'bq': jnp.zeros((E,), jnp.float32), 'conv_w': jax.random.normal(ks[4], (E, 1, KC), jnp.float32) * 0.2, 'conv_b': jnp.zeros((E,), jnp.float32), 'Win': lin(ks[5], feat, H), 'b_in': jnp.zeros((H,), jnp.float32), 'Wg': lin(ks[6], H, SS), 'bg': jnp.zeros((SS,), jnp.float32), 'Wi': lin(ks[7], H, SS), 'bi': jnp.zeros((SS,), jnp.float32), 'Wo': lin(ks[8], SS, H), 'bo': jnp.zeros((H,), jnp.float32), 'ln_g': jnp.ones((H,), jnp.float32), 'ln_b': jnp.zeros((H,), jnp.float32), 'mlp_w': jax.random.normal(ks[9], (NR, H, H), jnp.float32) / np.sqrt(H), 'mlp_b': jnp.zeros((NR, H), jnp.float32), 'Wout': lin(ks[10], H, V), 'bout': jnp.zeros((V,), jnp.float32)}
    _L0_tok_all = _L0_tok_setup()
    _L0_tok_in = {k: v for k, v in _L0_tok_all.items() if k in ('emb_byte', 'hash_tables', 'Wq', 'bq', 'conv_w', 'conv_b', 'Win', 'b_in', 'Wg', 'bg', 'Wi', 'bi', 'Wo', 'bo', 'ln_g', 'ln_b', 'mlp_w', 'mlp_b', 'Wout', 'bout')}
    del _L0_tok_all

    def _L0_attn_setup():
        import jax, jax.numpy as jnp
        import numpy as np
        B, N, C, H = (4, 256, 64, 8)
        HD = C // H
        BN_EPS = 1e-05
        key = jax.random.key(seed)
        ks = jax.random.split(key, 6)

        def w(k, shape, sc=0.02):
            return jax.random.normal(k, shape, jnp.float32) * sc
        return {'x': jax.random.normal(ks[0], (B, N, C), jnp.float32), 'w_qkv': w(ks[1], (3 * C, C)), 'b_qkv': jnp.zeros((3 * C,), jnp.float32), 'w_proj': w(ks[2], (C, C)), 'b_proj': jnp.zeros((C,), jnp.float32), 'scale': jnp.float32(HD ** (-0.5)), 'riem_scale': jnp.float32(HD ** (-0.5)), 'grassman_scale': jnp.float32(HD ** (-0.5)), 'bn_gamma': jnp.ones((3 * H,), jnp.float32), 'bn_beta': jnp.zeros((3 * H,), jnp.float32), 'bn_mean': jnp.zeros((3 * H,), jnp.float32), 'bn_var': jnp.ones((3 * H,), jnp.float32), 'conv_w': w(ks[3], (H, 3 * H)), 'conv_b': jnp.zeros((H,), jnp.float32)}
    _L0_attn_all = _L0_attn_setup()
    _L0_attn_in = {k: v for k, v in _L0_attn_all.items() if k in ('w_qkv', 'b_qkv', 'w_proj', 'b_proj', 'scale', 'riem_scale', 'grassman_scale', 'bn_gamma', 'bn_beta', 'bn_mean', 'bn_var', 'conv_w', 'conv_b')}
    del _L0_attn_all

    def _L0_ffn_setup():
        import jax, jax.numpy as jnp
        import numpy as np
        B, S, D, E, H, K = (4, 1024, 64, 8, 128, 2)
        key = jax.random.key(seed)
        ks = jax.random.split(key, 6)
        x = jax.random.normal(ks[0], (B, S, D), jnp.float32)
        Wg = jax.random.normal(ks[1], (D, E), jnp.float32) * 0.02
        bg = jnp.zeros((E,), jnp.float32)
        W1 = jax.random.normal(ks[2], (E, D, H), jnp.float32) * 0.02
        b1 = jnp.zeros((E, H), jnp.float32)
        W2 = jax.random.normal(ks[3], (E, H, D), jnp.float32) * 0.02
        b2 = jnp.zeros((E, D), jnp.float32)
        return {'x': x, 'Wg': Wg, 'bg': bg, 'W1': W1, 'b1': b1, 'W2': W2, 'b2': b2}
    _L0_ffn_all = _L0_ffn_setup()
    _L0_ffn_in = {k: v for k, v in _L0_ffn_all.items() if k in ('Wg', 'bg', 'W1', 'b1', 'W2', 'b2')}
    del _L0_ffn_all

    def _L1_attn_setup():
        import jax, jax.numpy as jnp
        import numpy as np
        B_SZ, L, H, P = (16, 1024, 64, 64)
        STEP_SCALE = 1.0
        key = jax.random.key(seed)
        ks = jax.random.split(key, 8)
        x = jax.random.normal(ks[0], (B_SZ, L, H), jnp.float32)
        Lambda_re = jax.random.uniform(ks[1], (P,), jnp.float32, 0.2, 1.0)
        Lambda_im = jax.random.normal(ks[2], (P,), jnp.float32) * np.float32(np.pi)
        B_re = jax.random.normal(ks[3], (P, H), jnp.float32) / np.float32(np.sqrt(H))
        B_im = jax.random.normal(ks[4], (P, H), jnp.float32) / np.float32(np.sqrt(H))
        C_re = jax.random.normal(ks[5], (H, P), jnp.float32) / np.float32(np.sqrt(P))
        C_im = jax.random.normal(ks[6], (H, P), jnp.float32) / np.float32(np.sqrt(P))
        log_step = jax.random.uniform(ks[7], (P,), jnp.float32, np.float32(np.log(0.001)), np.float32(np.log(0.1)))
        return {'x': x, 'Lambda_re': Lambda_re, 'Lambda_im': Lambda_im, 'B_re': B_re, 'B_im': B_im, 'C_re': C_re, 'C_im': C_im, 'log_step': log_step}
    _L1_attn_all = _L1_attn_setup()
    _L1_attn_in = {k: v for k, v in _L1_attn_all.items() if k in ('Lambda_re', 'Lambda_im', 'B_re', 'B_im', 'C_re', 'C_im', 'log_step')}
    del _L1_attn_all

    def _L1_ffn_setup():
        import jax, jax.numpy as jnp
        import numpy as np
        B, T, C = (64, 96, 64)
        NH, NKV = (4, 2)
        HD = C // NH
        NREP = NH // NKV
        NE, TOPK = (8, 2)
        HID = int(8 / 3 * C)
        EPS_RMS = 1e-06

        def _rope_tables(t_len):
            inv_freq = 1.0 / 10000.0 ** (np.arange(0, HD, 2, dtype=np.float32) / HD)
            t = np.arange(t_len, dtype=np.float32)
            freqs = np.outer(t, inv_freq)
            emb = np.concatenate([freqs, freqs], axis=-1)
            return (jnp.asarray(np.cos(emb)), jnp.asarray(np.sin(emb)))

        def _rotate_half(x):
            h = x.shape[-1] // 2
            return jnp.concatenate([-x[..., h:], x[..., :h]], axis=-1)

        def _rmsnorm(v, w):
            return v * jax.lax.rsqrt(jnp.mean(v * v, axis=-1, keepdims=True) + EPS_RMS) * w
        key = jax.random.key(seed)
        ks = jax.random.split(key, 10)
        s = lambda k, shape: jax.random.normal(k, shape, jnp.float32) * 0.02
        return {'x': jax.random.normal(ks[0], (B, T, C), jnp.float32), 'ln1_w': jnp.ones((C,), jnp.float32), 'ln2_w': jnp.ones((C,), jnp.float32), 'wq': s(ks[1], (NH * HD, C)), 'wk': s(ks[2], (NKV * HD, C)), 'wv': s(ks[3], (NKV * HD, C)), 'wo': s(ks[4], (C, C)), 'router_w': s(ks[5], (NE, C)), 'w1': s(ks[6], (NE, HID, C)), 'w2': s(ks[7], (NE, C, HID)), 'w3': s(ks[8], (NE, HID, C))}
    _L1_ffn_all = _L1_ffn_setup()
    _L1_ffn_in = {k: v for k, v in _L1_ffn_all.items() if k in ('ln1_w', 'ln2_w', 'wq', 'wk', 'wv', 'wo', 'router_w', 'w1', 'w2', 'w3')}
    del _L1_ffn_all
    return {'x': x, 'L0_tok_emb_byte': _L0_tok_in['emb_byte'], 'L0_tok_hash_tables': _L0_tok_in['hash_tables'], 'L0_tok_Wq': _L0_tok_in['Wq'], 'L0_tok_bq': _L0_tok_in['bq'], 'L0_tok_conv_w': _L0_tok_in['conv_w'], 'L0_tok_conv_b': _L0_tok_in['conv_b'], 'L0_tok_Win': _L0_tok_in['Win'], 'L0_tok_b_in': _L0_tok_in['b_in'], 'L0_tok_Wg': _L0_tok_in['Wg'], 'L0_tok_bg': _L0_tok_in['bg'], 'L0_tok_Wi': _L0_tok_in['Wi'], 'L0_tok_bi': _L0_tok_in['bi'], 'L0_tok_Wo': _L0_tok_in['Wo'], 'L0_tok_bo': _L0_tok_in['bo'], 'L0_tok_ln_g': _L0_tok_in['ln_g'], 'L0_tok_ln_b': _L0_tok_in['ln_b'], 'L0_tok_mlp_w': _L0_tok_in['mlp_w'], 'L0_tok_mlp_b': _L0_tok_in['mlp_b'], 'L0_tok_Wout': _L0_tok_in['Wout'], 'L0_tok_bout': _L0_tok_in['bout'], 'L0_attn_w_qkv': _L0_attn_in['w_qkv'], 'L0_attn_b_qkv': _L0_attn_in['b_qkv'], 'L0_attn_w_proj': _L0_attn_in['w_proj'], 'L0_attn_b_proj': _L0_attn_in['b_proj'], 'L0_attn_scale': _L0_attn_in['scale'], 'L0_attn_riem_scale': _L0_attn_in['riem_scale'], 'L0_attn_grassman_scale': _L0_attn_in['grassman_scale'], 'L0_attn_bn_gamma': _L0_attn_in['bn_gamma'], 'L0_attn_bn_beta': _L0_attn_in['bn_beta'], 'L0_attn_bn_mean': _L0_attn_in['bn_mean'], 'L0_attn_bn_var': _L0_attn_in['bn_var'], 'L0_attn_conv_w': _L0_attn_in['conv_w'], 'L0_attn_conv_b': _L0_attn_in['conv_b'], 'L0_ffn_Wg': _L0_ffn_in['Wg'], 'L0_ffn_bg': _L0_ffn_in['bg'], 'L0_ffn_W1': _L0_ffn_in['W1'], 'L0_ffn_b1': _L0_ffn_in['b1'], 'L0_ffn_W2': _L0_ffn_in['W2'], 'L0_ffn_b2': _L0_ffn_in['b2'], 'L1_attn_Lambda_re': _L1_attn_in['Lambda_re'], 'L1_attn_Lambda_im': _L1_attn_in['Lambda_im'], 'L1_attn_B_re': _L1_attn_in['B_re'], 'L1_attn_B_im': _L1_attn_in['B_im'], 'L1_attn_C_re': _L1_attn_in['C_re'], 'L1_attn_C_im': _L1_attn_in['C_im'], 'L1_attn_log_step': _L1_attn_in['log_step'], 'L1_ffn_ln1_w': _L1_ffn_in['ln1_w'], 'L1_ffn_ln2_w': _L1_ffn_in['ln2_w'], 'L1_ffn_wq': _L1_ffn_in['wq'], 'L1_ffn_wk': _L1_ffn_in['wk'], 'L1_ffn_wv': _L1_ffn_in['wv'], 'L1_ffn_wo': _L1_ffn_in['wo'], 'L1_ffn_router_w': _L1_ffn_in['router_w'], 'L1_ffn_w1': _L1_ffn_in['w1'], 'L1_ffn_w2': _L1_ffn_in['w2'], 'L1_ffn_w3': _L1_ffn_in['w3']}

def reference(x, L0_tok_emb_byte, L0_tok_hash_tables, L0_tok_Wq, L0_tok_bq, L0_tok_conv_w, L0_tok_conv_b, L0_tok_Win, L0_tok_b_in, L0_tok_Wg, L0_tok_bg, L0_tok_Wi, L0_tok_bi, L0_tok_Wo, L0_tok_bo, L0_tok_ln_g, L0_tok_ln_b, L0_tok_mlp_w, L0_tok_mlp_b, L0_tok_Wout, L0_tok_bout, L0_attn_w_qkv, L0_attn_b_qkv, L0_attn_w_proj, L0_attn_b_proj, L0_attn_scale, L0_attn_riem_scale, L0_attn_grassman_scale, L0_attn_bn_gamma, L0_attn_bn_beta, L0_attn_bn_mean, L0_attn_bn_var, L0_attn_conv_w, L0_attn_conv_b, L0_ffn_Wg, L0_ffn_bg, L0_ffn_W1, L0_ffn_b1, L0_ffn_W2, L0_ffn_b2, L1_attn_Lambda_re, L1_attn_Lambda_im, L1_attn_B_re, L1_attn_B_im, L1_attn_C_re, L1_attn_C_im, L1_attn_log_step, L1_ffn_ln1_w, L1_ffn_ln2_w, L1_ffn_wq, L1_ffn_wk, L1_ffn_wv, L1_ffn_wo, L1_ffn_router_w, L1_ffn_w1, L1_ffn_w2, L1_ffn_w3):
    import jax
    import jax.numpy as jnp

    def _L0_tok_ref(chars, emb_byte, hash_tables, Wq, bq, conv_w, conv_b, Win, b_in, Wg, bg, Wi, bi, Wo, bo, ln_g, ln_b, mlp_w, mlp_b, Wout, bout):
        import jax, jax.numpy as jnp
        import numpy as np
        BASE = 257
        HASH_MOD = 1024
        WINDOWS = (2, 4, 8, 16)
        MATCH_OFFSETS = (1, 2, 4, 8)
        CHUNK = 32
        EPS_LN = 1e-05

        def _shift_right(x, k):
            B, T = x.shape
            return jnp.concatenate([jnp.zeros((B, k), x.dtype), x[:, :T - k]], axis=1)

        def _rolling_hashes(chars):
            c = chars.astype(jnp.int32)
            hs = []
            for w in WINDOWS:
                acc = jnp.zeros_like(c)
                p = 1
                for j in range(w):
                    acc = acc + _shift_right(c, j) * p
                    p = p * BASE % HASH_MOD
                hs.append(acc % HASH_MOD)
            return jnp.stack(hs, axis=2)

        def _match_features(chars):
            feats = []
            for k in MATCH_OFFSETS:
                m = (chars == _shift_right(chars, k)).astype(jnp.float32)
                m = m.at[:, :k].set(0.0)
                feats.append(m)
            return jnp.stack(feats, axis=-1)

        def _layer_norm(x, g, b):
            mu = jnp.mean(x, axis=-1, keepdims=True)
            var = jnp.mean((x - mu) ** 2, axis=-1, keepdims=True)
            return (x - mu) * jax.lax.rsqrt(var + EPS_LN) * g + b

        def _forward(chars, emb_byte, hash_tables, Wq, bq, conv_w, conv_b, Win, b_in, Wg, bg, Wi, bi, Wo, bo, ln_g, ln_b, mlp_w, mlp_b, Wout, bout):
            B, T = chars.shape
            byte_emb = emb_byte[chars]
            hidx = _rolling_hashes(chars)
            scale_embeds = jnp.stack([hash_tables[s][hidx[:, :, s]] for s in range(len(WINDOWS))], axis=2)
            E = scale_embeds.shape[-1]
            q = byte_emb @ Wq + bq
            scores = jnp.einsum('bte,btse->bts', q, scale_embeds) / jnp.sqrt(jnp.float32(E))
            w = jax.nn.softmax(scores, axis=-1)
            hash_feat = jnp.einsum('bts,btse->bte', w, scale_embeds)
            C = hash_feat.shape[-1]
            kk = conv_w.shape[-1]
            ht = jnp.moveaxis(hash_feat, 1, 2)
            ht = jnp.pad(ht, ((0, 0), (0, 0), (kk - 1, 0)))
            ht = jax.lax.conv_general_dilated(ht, conv_w, window_strides=(1,), padding='VALID', dimension_numbers=('NCH', 'OIH', 'NCH'), feature_group_count=C)
            hash_feat = jax.nn.silu(jnp.moveaxis(ht + conv_b[None, :, None], 2, 1))
            mf = _match_features(chars)
            feat = jnp.concatenate([byte_emb, hash_feat, mf], axis=-1)
            h = jax.nn.silu(feat @ Win + b_in)
            gates = jax.nn.sigmoid(h @ Wg + bg)
            drive = (1.0 - gates) * (h @ Wi + bi)
            S = gates.shape[-1]
            nC = T // CHUNK
            g = gates.reshape(B, nC, CHUNK, S).transpose(1, 0, 2, 3)
            d = drive.reshape(B, nC, CHUNK, S).transpose(1, 0, 2, 3)

            def step(hc, ab):
                a, b = ab
                log_a = jnp.log(jnp.maximum(a, 1e-06))
                cum_a = jnp.exp(jnp.cumsum(log_a, axis=1))
                inv = 1.0 / jnp.maximum(cum_a, 1e-08)
                cum_wb = jnp.cumsum(b * inv, axis=1)
                out = cum_a * (hc[:, None, :] + cum_wb)
                return (out[:, -1], out)
            _, states = jax.lax.scan(step, jnp.zeros((B, S), h.dtype), (g, d))
            states = states.transpose(1, 0, 2, 3).reshape(B, T, S)
            h = _layer_norm(h + states @ Wo + bo, ln_g, ln_b)
            for l in range(mlp_w.shape[0]):
                h = h + jax.nn.silu(h @ mlp_w[l] + mlp_b[l])
            return h @ Wout + bout
        return _forward(chars, emb_byte, hash_tables, Wq, bq, conv_w, conv_b, Win, b_in, Wg, bg, Wi, bi, Wo, bo, ln_g, ln_b, mlp_w, mlp_b, Wout, bout)

    def _L0_attn_ref(x, w_qkv, b_qkv, w_proj, b_proj, scale, riem_scale, grassman_scale, bn_gamma, bn_beta, bn_mean, bn_var, conv_w, conv_b):
        import jax, jax.numpy as jnp
        import numpy as np
        B, N, C, H = (4, 256, 64, 8)
        HD = C // H
        BN_EPS = 1e-05
        b, n, c = x.shape
        h, hd = (H, c // H)
        qkv = (x @ w_qkv.T + b_qkv).reshape(b, n, 3, h, hd).transpose(2, 0, 3, 1, 4)
        q, k, v = (qkv[0], qkv[1], qkv[2])
        qgr, _ = jnp.linalg.qr(q)
        kgr, _ = jnp.linalg.qr(k)
        attn_grass = jnp.einsum('bhnd,bhmd->bhnm', qgr, kgr) ** 2 * grassman_scale
        dots = jnp.einsum('bhnd,bhmd->bhnm', q, k)
        attn_eucl = dots * scale
        attn_riem = dots ** 2 * riem_scale
        a = jnp.concatenate([attn_eucl, attn_riem, attn_grass], axis=1)
        inv = (bn_gamma * jax.lax.rsqrt(bn_var + BN_EPS))[:, None, None]
        a = (a - bn_mean[:, None, None]) * inv + bn_beta[:, None, None]
        a = jnp.einsum('oc,bcnm->bonm', conv_w, a) + conv_b[None, :, None, None]
        a = jax.nn.softmax(a, axis=-1)
        out = jnp.einsum('bhnm,bhmd->bhnd', a, v)
        out = out.transpose(0, 2, 1, 3).reshape(b, n, c)
        return out @ w_proj.T + b_proj

    def _L0_ffn_ref(x, Wg, bg, W1, b1, W2, b2):
        import jax, jax.numpy as jnp
        import numpy as np
        B, S, D, E, H, K = (4, 1024, 64, 8, 128, 2)
        Bv, Sv, Dv = x.shape
        gate_scores = x @ Wg + bg
        _, idx = jax.lax.top_k(gate_scores, K)
        mask = jax.nn.one_hot(idx, E, dtype=x.dtype).sum(axis=-2)
        xf = x.reshape(-1, Dv)
        mf = mask.reshape(-1, E)
        h = jax.nn.gelu(jnp.einsum('td,edh->teh', xf, W1) + b1[None], approximate=False)
        y = jnp.einsum('teh,ehd->ted', h, W2) + b2[None]
        out = jnp.einsum('ted,te->td', y, mf)
        return out.reshape(Bv, Sv, Dv)

    def _L1_attn_ref(x, Lambda_re, Lambda_im, B_re, B_im, C_re, C_im, log_step):
        import jax, jax.numpy as jnp
        import numpy as np
        B_SZ, L, H, P = (16, 1024, 64, 64)
        STEP_SCALE = 1.0
        step = STEP_SCALE * jnp.exp(log_step)
        Lam = -jnp.abs(Lambda_re) + 1j * Lambda_im
        Lam_bar = jnp.exp(Lam * step)
        gamma = (Lam_bar - 1.0) / Lam
        Bc = (B_re + 1j * B_im) * gamma[:, None]
        Bu = jnp.einsum('blh,ph->blp', x, Bc.real) + 1j * jnp.einsum('blh,ph->blp', x, Bc.imag)
        A_el = jnp.broadcast_to(Lam_bar, Bu.shape)

        def binop(a, b):
            Aa, ba = a
            Ab, bb = b
            return (Ab * Aa, Ab * ba + bb)
        _, states = jax.lax.associative_scan(binop, (A_el, Bu), axis=1)
        y = jnp.einsum('blp,hp->blh', states.real, C_re) - jnp.einsum('blp,hp->blh', states.imag, C_im)
        return jax.nn.relu(y) + x

    def _L1_ffn_ref(x, ln1_w, ln2_w, wq, wk, wv, wo, router_w, w1, w2, w3):
        import jax, jax.numpy as jnp
        import numpy as np
        B, T, C = (64, 96, 64)
        NH, NKV = (4, 2)
        HD = C // NH
        NREP = NH // NKV
        NE, TOPK = (8, 2)
        HID = int(8 / 3 * C)
        EPS_RMS = 1e-06

        def _rope_tables(t_len):
            inv_freq = 1.0 / 10000.0 ** (np.arange(0, HD, 2, dtype=np.float32) / HD)
            t = np.arange(t_len, dtype=np.float32)
            freqs = np.outer(t, inv_freq)
            emb = np.concatenate([freqs, freqs], axis=-1)
            return (jnp.asarray(np.cos(emb)), jnp.asarray(np.sin(emb)))

        def _rotate_half(x):
            h = x.shape[-1] // 2
            return jnp.concatenate([-x[..., h:], x[..., :h]], axis=-1)

        def _rmsnorm(v, w):
            return v * jax.lax.rsqrt(jnp.mean(v * v, axis=-1, keepdims=True) + EPS_RMS) * w
        Bx, Tx, Cx = x.shape
        h = _rmsnorm(x, ln1_w)
        q = (h @ wq.T).reshape(Bx, Tx, NH, HD).transpose(0, 2, 1, 3)
        k = (h @ wk.T).reshape(Bx, Tx, NKV, HD).transpose(0, 2, 1, 3)
        v = (h @ wv.T).reshape(Bx, Tx, NKV, HD).transpose(0, 2, 1, 3)
        cos, sin = _rope_tables(Tx)
        cos, sin = (cos[None, None], sin[None, None])
        q = q * cos + _rotate_half(q) * sin
        k = k * cos + _rotate_half(k) * sin
        k = jnp.repeat(k, NREP, axis=1)
        v = jnp.repeat(v, NREP, axis=1)
        scores = jnp.einsum('bhtd,bhsd->bhts', q, k) / jnp.sqrt(jnp.float32(HD))
        causal = jnp.tril(jnp.ones((Tx, Tx), dtype=bool))
        scores = jnp.where(causal[None, None], scores, jnp.float32(-1e+30))
        att = jax.nn.softmax(scores, axis=-1)
        y = jnp.einsum('bhts,bhsd->bhtd', att, v).transpose(0, 2, 1, 3).reshape(Bx, Tx, Cx)
        x = x + y @ wo.T
        flat = _rmsnorm(x, ln2_w).reshape(-1, Cx)
        probs = jax.nn.softmax(flat @ router_w.T, axis=-1)
        tp, ti = jax.lax.top_k(probs, TOPK)
        tp = tp / (jnp.sum(tp, axis=-1, keepdims=True) + 1e-09)
        weights = jnp.sum(tp[..., None] * jax.nn.one_hot(ti, NE, dtype=flat.dtype), axis=1)
        out = jnp.zeros_like(flat)
        for e in range(NE):
            hh = jax.nn.silu(flat @ w1[e].T) * (flat @ w3[e].T)
            out = out + weights[:, e:e + 1] * (hh @ w2[e].T)
        return x + out.reshape(Bx, Tx, Cx)
    h = _L0_tok_ref(x, L0_tok_emb_byte, L0_tok_hash_tables, L0_tok_Wq, L0_tok_bq, L0_tok_conv_w, L0_tok_conv_b, L0_tok_Win, L0_tok_b_in, L0_tok_Wg, L0_tok_bg, L0_tok_Wi, L0_tok_bi, L0_tok_Wo, L0_tok_bo, L0_tok_ln_g, L0_tok_ln_b, L0_tok_mlp_w, L0_tok_mlp_b, L0_tok_Wout, L0_tok_bout)
    h = h + _L0_attn_ref(_layernorm(h, axis=-1), L0_attn_w_qkv, L0_attn_b_qkv, L0_attn_w_proj, L0_attn_b_proj, L0_attn_scale, L0_attn_riem_scale, L0_attn_grassman_scale, L0_attn_bn_gamma, L0_attn_bn_beta, L0_attn_bn_mean, L0_attn_bn_var, L0_attn_conv_w, L0_attn_conv_b)
    h = h + _L0_ffn_ref(_layernorm(h, axis=-1), L0_ffn_Wg, L0_ffn_bg, L0_ffn_W1, L0_ffn_b1, L0_ffn_W2, L0_ffn_b2)
    h = h + _L1_attn_ref(_layernorm(h, axis=-1), L1_attn_Lambda_re, L1_attn_Lambda_im, L1_attn_B_re, L1_attn_B_im, L1_attn_C_re, L1_attn_C_im, L1_attn_log_step)
    h = h + _L1_ffn_ref(_layernorm(h, axis=-1), L1_ffn_ln1_w, L1_ffn_ln2_w, L1_ffn_wq, L1_ffn_wk, L1_ffn_wv, L1_ffn_wo, L1_ffn_router_w, L1_ffn_w1, L1_ffn_w2, L1_ffn_w3)
    return h

_drawn_inputs = setup_inputs


def setup_inputs(seed=0):
    import zlib

    import numpy as np

    out = dict(_drawn_inputs(seed))
    spreads = {'L0_tok_bq': (0.0, 0.8),
     'L0_tok_conv_b': (0.0, 0.1),
     'L0_tok_b_in': (0.0, 0.1),
     'L0_tok_bg': (0.0, 0.1),
     'L0_tok_bi': (0.0, 0.1),
     'L0_tok_bo': (0.0, 0.1),
     'L0_tok_ln_g': (1.0, 0.2),
     'L0_tok_ln_b': (0.0, 0.1),
     'L0_tok_mlp_b': (0.0, 0.1),
     'L0_tok_bout': (0.0, 0.1),
     'L0_attn_b_qkv': (0.0, 0.621),
     'L0_attn_b_proj': (0.0, 0.1),
     'L0_attn_bn_gamma': (1.0, 0.6),
     'L0_attn_bn_beta': (0.0, 0.8),
     'L0_attn_bn_mean': (0.0, 0.8),
     'L0_attn_bn_var': (1.0, 0.6),
     'L0_attn_conv_b': (0.0, 0.8),
     'L0_ffn_bg': (0.0, 0.306),
     'L0_ffn_b1': (0.0, 0.8),
     'L0_ffn_b2': (0.0, 0.1),
     'L1_ffn_ln1_w': (1.0, 0.6),
     'L1_ffn_ln2_w': (1.0, 0.6)}
    factors = {'L0_tok_hash_tables': 8.0,
     'L0_tok_Wq': 8.0,
     'L0_tok_conv_w': 8.0,
     'L0_attn_w_qkv': 4.265,
     'L0_attn_w_proj': 2.909,
     'L0_attn_conv_w': 8.0,
     'L0_ffn_W1': 4.403,
     'L0_ffn_W2': 3.41,
     'L1_ffn_wq': 8.0,
     'L1_ffn_wk': 8.0,
     'L1_ffn_wv': 6.882,
     'L1_ffn_wo': 8.0,
     'L1_ffn_router_w': 8.0,
     'L1_ffn_w1': 8.0,
     'L1_ffn_w2': 8.0,
     'L1_ffn_w3': 8.0}
    for name, (base, spread) in spreads.items():
        noise = np.random.default_rng([zlib.crc32(name.encode()), seed]).standard_normal(out[name].shape)
        drawn = base * np.exp(spread * noise) if base else spread * noise
        out[name] = jnp.asarray(drawn.astype(out[name].dtype))
    for name, factor in factors.items():
        out[name] = (out[name] * factor).astype(out[name].dtype)
    return out
```

```python
from contextlib import ExitStack

import numpy as np

import concourse.bass as bass
from concourse import mybir

F32 = mybir.dt.float32
I32 = mybir.dt.int32
U32 = mybir.dt.uint32
ALU = mybir.AluOpType
ACT = mybir.ActivationFunctionType
AX = mybir.AxisListType.X

P = 128
B = 32
T = 512
D = 64
TB = T // P
PAIRS = B // 2
STREAMS = (0, 1)
VOCAB = 64
NSCALE = 4
HASH_MOD = 1024
MATCH = (1, 2, 4, 8)
H = 128
SS = 32
CHUNK = 32
NMLP = 3
HEADS = 8
HD = D // HEADS
MONO = HD * (HD + 1) // 2
NQUAD = HEADS * MONO
NFEAT = NQUAD + D + 1
NE = 8
FH = 128
NH2, NKV2, HD2 = 4, 2, 16
HID = int(8 / 3 * D)
REST = HID - P


class Steps:

    def __init__(self, sem, names):
        self.sem, self.names, self.at = sem, names, 0

    def mark(self, name):
        assert self.names[self.at % len(self.names)] == name, (name, self.names[self.at % len(self.names)])
        self.at += 1
        return self.sem

    def now(self, i, name):
        return (i + 1) * len(self.names) + self.names.index(name) + 1

    def before(self, i, name):
        return i * len(self.names) + self.names.index(name) + 1


def wait_now(eng, steps, i, name):
    eng.wait_ge(steps.sem, steps.now(i, name))


def wait_before(eng, steps, i, name):
    eng.wait_ge(steps.sem, steps.before(i, name))


def wait_load(eng, sem, i, count=1):
    eng.wait_ge(sem, i * (16 * count) + 16 * count)



def mono_pairs():
    return [(i, i + r) for r in range(HD) for i in range(HD - r)]


def spec(stage):
    s = {
        "token": [("embT", D, P), ("wq", D, D), ("bq", P, D), ("win_e", D, H), ("w1a", P, H), ("w1b", P, H),
                  ("wmf", 4, H), ("b_in", H, 1), ("wg", H, SS), ("wi", H, SS), ("bg", 2 * SS, 1),
                  ("bi", 2 * SS, 1), ("woT", H, 2 * SS), ("bo", H, 1), ("ln_g", H, 1), ("ln_b", H, 1),
                  ("mlp_w", H, NMLP * H), ("mlp_b", H, NMLP), ("wout", H, D), ("bout", P, 1),
                  ("conv_w", P, 4), ("conv_b", P, 1), ("cen", P, P), ("avg", P, P), ("ident", P, P),
                  ("iota", P, 1), ("first", 2 * SS, T), ("rest", 2 * SS, T), ("eps", P, 1)],
        "qkv": [("cen2", P, P), ("avg2", P, P), ("wqkv", P, 3 * D), ("bqkv", P, 3 * D), ("eps", P, 1)],
        "qr": [("eye", P, 4 * HD * HD)],
        "attn": [("ident", P, P), ("convT", 3 * HEADS, HEADS), ("gamma", 3 * HEADS, 1), ("beta", 3 * HEADS, 1),
                 ("mean", 3 * HEADS, 1), ("var", 3 * HEADS, 1), ("scales", 3 * HEADS, 1),
                 ("conv_b", P, HEADS), ("sel_b", 3 * HEADS, 3 * P), ("sel_c", 3 * HEADS, 3 * P),
                 ("sel_1", 3 * HEADS, P), ("last", P, 1), ("wproj", D, P), ("bproj", P, 1),
                 ("eps", 3 * HEADS, 1)],
        "gelu": [("cen2", P, P), ("avg2", P, P), ("ident", P, P), ("wg", P, 2 * NE), ("bg", P, NE),
                 ("w1", P, NE * FH), ("b1", FH, NE), ("w2", FH, NE * D), ("b2", NE, D), ("tri", P, NE * NE),
                 ("eps", P, 1)],
        "ssm": [("cen2", P, P), ("avg2", P, P), ("lre", P, 1), ("lim", P, 1), ("lstep", P, 1), ("b_mine", P, D),
                ("b_other", P, D), ("sgn", P, 1), ("c1", P, D), ("c2", P, D), ("neg1", P, 1), ("neg2", P, 1),
                ("ident", P, P), ("eps", P, 1)],
        "norm": [("cen2", P, P), ("avg2", P, P), ("eps", P, 1)],
        "causal": [("avg2", P, P), ("ident", P, P), ("ln", P, 1), ("wq", P, P), ("wqr", P, P), ("wk", P, P),
                   ("wkr", P, P), ("wv", P, 2 * NKV2 * HD2), ("wo", D, P), ("cos", P, T), ("sin", P, T),
                   ("mask", P, P), ("eps", P, 1)],
        "swiglu": [("avg2", P, P), ("ident", P, P), ("ln", P, 1), ("router", P, 2 * NE), ("w1", P, 12 * P),
                   ("w3", P, 12 * P), ("w2", P, NE * D), ("w2r", P, NE * D), ("tri", P, NE * NE), ("eps", P, 1)],
    }[stage]
    at, out = 0, {}
    for name, rows, cols in s:
        out[name] = (rows, at, cols)
        at += cols
    return out, at


class Params:

    def __init__(self, tile, stage):
        self.tile, (self.parts, _) = tile, spec(stage)

    def __call__(self, name, r0=0, r1=None):
        rows, at, cols = self.parts[name]
        return self.tile[r0:rows if r1 is None else r1, at:at + cols]

    def cols(self, name, c0, c1, r0=0, r1=None):
        rows, at, _ = self.parts[name]
        return self.tile[r0:rows if r1 is None else r1, at + c0:at + c1]


STAGES = ("token", "qkv", "qr", "attn", "gelu", "ssm", "norm", "causal", "swiglu")


def load_params(nc, ctx, stage, dram):
    tile = ctx.enter_context(nc.sbuf_tensor(f"sb_params_{stage}", [P, spec(stage)[1]], F32))
    return tile, Params(tile, stage), nc.alloc_semaphore(f"params_{stage}_loaded")



def hash_stage(nc, dram):
    pad = 16
    with ExitStack() as ctx:
        def sb(name, shape, dt=F32):
            return ctx.enter_context(nc.sbuf_tensor(f"hash_{name}", shape, dt))

        chars_i = sb("chars_i", [B, T], I32)
        ident = sb("hash_ident", [P, P])
        win = [sb(f"window{s}", [B, pad + T]) for s in range(NSCALE + 1)]
        match = sb("match", [B, len(MATCH), T])
        index_i = sb("index_i", [P, NSCALE * TB * B], I32)
        index = sb("index", [P, PAIRS, NSCALE, TB, 2], I32)
        turned = ctx.enter_context(nc.psum_tensor("turned", [P, NSCALE, TB, B], F32))
        loaded, padded, windows, matched, transposed, indexed, stored = (
            ctx.enter_context(nc.semaphore(n)) for n in
            ("chars_loaded", "windows_padded", "windows_made", "match_made", "hashes_turned", "index_made",
             "hashes_stored"))
        block = ctx.enter_context(nc.Block())

        @block.sync
        def _(sp):
            sp.dma_start(chars_i[:, :], dram["x"]).then_inc(loaded, 16)
            parts, _ = spec("token")
            at = parts["ident"][1]
            sp.dma_start(ident[:, :], dram["params_token"][:, at:at + P]).then_inc(loaded, 16)
            sp.wait_ge(matched, 2)
            sp.dma_start(dram["match"], match[:, :, :]).then_inc(stored, 16)
            sp.wait_ge(indexed, 2)
            sp.dma_start(dram["index"], index[:, :, :, :, :].rearrange("p a b c d -> p (a b c d)")).then_inc(stored, 16)
            sp.wait_ge(stored, 32)

        @block.gpsimd
        def _(pool):
            for s in range(NSCALE + 1):
                last = nc.gpsimd.memset(win[s][:, 0:pad], 0.0)
            last.then_inc(padded, 1)

        @block.vector
        def _(dve):
            step = [0]

            def done(ins):
                step[0] += 1
                ins.then_inc(windows, 1)
                dve.wait_ge(windows, step[0])

            def ago(s, k):
                return win[s][:, pad - k:pad - k + T]

            dve.wait_ge(loaded, 32)
            dve.wait_ge(padded, 1)
            done(nc.vector.tensor_copy(ago(0, 0), chars_i[:, :]))
            done(nc.vector.scalar_tensor_tensor(ago(1, 0), ago(0, 1), 257.0, ago(0, 0), ALU.mult, ALU.add))
            done(nc.vector.scalar_tensor_tensor(ago(2, 0), ago(0, 2), 513.0, ago(1, 0), ALU.mult, ALU.add))
            done(nc.vector.scalar_tensor_tensor(ago(2, 0), ago(0, 3), 769.0, ago(2, 0), ALU.mult, ALU.add))
            done(nc.vector.tensor_tensor(ago(3, 0), ago(2, 0), ago(2, 4), ALU.add))
            done(nc.vector.tensor_tensor(ago(4, 0), ago(3, 0), ago(3, 8), ALU.add))
            for m, k in enumerate(MATCH):
                last = nc.vector.tensor_tensor(match[:, m, :], ago(0, 0), ago(0, k), ALU.is_equal)
            last.then_inc(matched, 1)
            dve.wait_ge(matched, 1)
            for m, k in enumerate(MATCH):
                last = nc.vector.memset(match[:, m, 0:k], 0.0)
            last.then_inc(matched, 1)
            dve.wait_ge(transposed, 1)
            nc.vector.tensor_copy(index_i[:, :], turned[:, :, :, :].rearrange("p a b c -> p (a b c)")).then_inc(indexed, 1)
            dve.wait_ge(indexed, 1)
            for s in range(NSCALE):
                src = index_i[:, s * TB * B:(s + 1) * TB * B].rearrange("p (t a q) -> p a t q", t=TB, q=2)
                last = nc.vector.tensor_scalar(index[:, :, s, :, :], src, HASH_MOD - 1, s * HASH_MOD,
                                               ALU.bitwise_and, ALU.bitwise_or)
            last.then_inc(indexed, 1)

        @block.tensor
        def _(pe):
            pe.wait_ge(loaded, 32)
            pe.wait_ge(windows, 6)
            for s in range(NSCALE):
                for t in range(TB):
                    last = nc.tensor.transpose(turned[:, s, t, :], win[s + 1][:, pad + t * P:pad + (t + 1) * P],
                                               ident[0:B, 0:B])
            last.then_inc(transposed, 1)


def token_stage(nc, dram):
    VS = ["onehot", "prod", "score", "smax", "sub", "sum", "rec", "weight", "wprod", "hsum",
          "conv0", "conv1", "conv2", "conv3", "gate", "d0", "d1", "clamped", "cum", "keep", "drive", "ratio",
          "fed", "states", "rstd", "norm", "res0", "res1", "res2"]
    SSN = ["exp", "hashT", "silu_hash", "h1", "tanh", "centered", "square", "std", "affine",
           "act0", "act1", "act2", "out"]
    TS = ["q", "hashT", "feat", "gates", "center", "var", "mlp0", "mlp1", "mlp2", "out"]
    with ExitStack() as ctx:
        def sb(name, shape, dt=F32):
            return [ctx.enter_context(nc.sbuf_tensor(f"token_{name}{s}", shape, dt)) for s in STREAMS]

        def one(name, shape, dt=F32):
            return ctx.enter_context(nc.sbuf_tensor(f"token_{name}", shape, dt))

        def sem(name):
            return nc.alloc_semaphore(f"token_{name}")

        params, par, params_loaded = load_params(nc, ctx, "token", dram)
        tq = one("tq", [P, D])
        w1b = one("w1b_sb", [P, H])
        wo_c = one("wo_c", [2 * SS, H])
        bo_c = one("bo_c", [P, 1])
        half_bg = one("half_bg", [2 * SS, 1])
        mark, carrier = sb("mark", [P, 1]), sb("carrier", [P, 1])
        index = sb("idx", [P, NSCALE * TB * 2], U32)
        xb = sb("xb", [P, T], I32)
        mf = sb("mf", [4, 2, T])
        feat = sb("feat", [P, 2, T])
        emb = sb("emb", [P, TB, 2, NSCALE, D])
        prod = sb("prod", [P, 2, TB, NSCALE, D])
        sc = sb("sc", [P, 2, TB, NSCALE])
        wt = sb("wt", [P, 2, TB, NSCALE])
        mx = sb("mx", [P, 2 * TB])
        hsum = sb("hsum", [P, TB, 2, D])
        hpad = sb("hpad", [P, 3 + T])
        conv = sb("conv", [P, T])
        h = sb("h", [P, 2, T])
        sq = sb("sq", [P, 2, T])
        xc = sb("xc", [P, 2, T])
        gate, clamped, d0, d1, cum, keep, fed, states = (
            sb(n, [2 * SS, T]) for n in ("gate", "clamped", "d0", "d1", "cum", "keep", "fed", "states"))
        ho = sb("ho", [P, T])
        ps = [[ctx.enter_context(nc.psum_tensor(f"token_ps{s}{k}", [P, T], F32)) for k in range(4)] for s in STREAMS]
        marked = [sem(f"round_open{s}") for s in STREAMS]
        x_in, idx_in, mf_in, gathered, stored = (
            [sem(f"{n}{s}") for s in STREAMS] for n in ("chars_in", "index_in", "match_in", "rows_gathered", "h_stored"))
        V = [Steps(sem(f"vector_steps{s}"), VS) for s in STREAMS]
        S = [Steps(sem(f"scalar_steps{s}"), SSN) for s in STREAMS]
        TE = [Steps(sem(f"tensor_steps{s}"), TS) for s in STREAMS]
        setup_pe, setup_v, pads = sem("setup_products"), sem("setup_weights"), sem("pads_cleared")
        block = ctx.enter_context(nc.Block())
        N = PAIRS // 2

        @block.sync
        def _(sp):
            sp.dma_start(params[:, :], dram["params_token"]).then_inc(params_loaded, 16)
            with sp.Fori(0, N) as i:
                for s in STREAMS:
                    seq = i * 4 + 2 * s
                    wait_before(sp, V[s], i, "onehot")
                    sp.dma_start(xb[s][0:D, :], dram["x"][bass.ds(seq + 1, 1), :].to_broadcast((D, T))).then_inc(x_in[s], 16)
                    sp.dma_start(xb[s][D:P, :], dram["x"][bass.ds(seq, 1), :].to_broadcast((D, T))).then_inc(x_in[s], 16)
                    wait_before(sp, TE[s], i, "feat")
                    sp.dma_start(mf[s][:, :, :], dram["match"][bass.ds(seq, 2), :, :].rearrange("q k t -> k q t")).then_inc(mf_in[s], 16)
                for s in STREAMS:
                    wait_now(sp, S[s], i, "out")
                    sp.dma_start(dram["h0"][bass.ds(i * 2 + s, 1), :, :].rearrange("a p t -> (a p) t"), ho[s][:, :]).then_inc(stored[s], 16)
            for s in STREAMS:
                sp.wait_ge(stored[s], 16 * N)

        @block.gpsimd
        def _(pool):
            for s in STREAMS:
                nc.gpsimd.memset(mark[s][:, :], 0.0)
                last = nc.gpsimd.memset(hpad[s][:, 0:3], 0.0)
            last.then_inc(pads, 1)
            pool.wait_ge(pads, 1)
            with pool.Fori(0, N) as i:
                for s in STREAMS:
                    pool.wait_ge(gathered[s], i * (16 * NSCALE * TB * 2))
                    pool.dma_start(index[s][:, :], dram["index"][:, bass.ds((i * 2 + s) * (NSCALE * TB * 2), NSCALE * TB * 2)]
                                   ).then_inc(idx_in[s], 16)
                for s in STREAMS:
                    pool.wait_ge(marked[s], i)
                    wait_before(pool, V[s], i, "wprod")
                    wait_load(pool, idx_in[s], i)
                    nc.gpsimd.tensor_tensor(carrier[s][:, :], mark[s][:, :], mark[s][:, :], ALU.mult).then_inc(marked[s], 1)
                    for c in range(NSCALE):
                        for t in range(TB):
                            for q in range(2):
                                k = (c * TB + t) * 2 + q
                                nc.gpsimd.indirect_dma_start(
                                    out=emb[s][:, t, q, c, :], out_offset=None, in_=dram["hash_tables"],
                                    in_offset=bass.IndirectOffsetOnAxis(ap=index[s][:, k:k + 1], axis=0),
                                ).then_inc(gathered[s], 16)

        @block.vector
        def _(dve):
            for s in STREAMS:
                nc.vector.sem_inc(V[s].sem, len(VS))
            dve.wait_ge(params_loaded, 16)
            dve.wait_ge(setup_pe, 1)
            nc.vector.tensor_tensor(tq[:, :], ps[0][0][:, 0:D], par("bq"), ALU.add)
            nc.vector.tensor_copy(par("w1a", D, P), ps[0][1][D:P, 0:H])
            nc.vector.tensor_copy(par("w1b", 0, D), ps[0][1][0:D, 0:H])
            nc.vector.tensor_copy(wo_c[:, :], ps[0][2][0:2 * SS, 0:H])
            nc.vector.tensor_copy(bo_c[:, :], ps[0][3][:, 0:1])
            nc.vector.tensor_scalar(half_bg[:, :], par("bg"), 0.5, None, ALU.mult).then_inc(setup_v, 1)
            with dve.Fori(0, N) as i:
                def hash_scores(s):
                    wait_load(dve, x_in[s], i, 2)
                    wait_before(dve, TE[s], i, "feat")
                    nc.vector.tensor_scalar(feat[s][D:P, 0, :], xb[s][D:P, :], par("iota", D, P), None, ALU.is_equal)
                    nc.vector.tensor_scalar(feat[s][0:D, 1, :], xb[s][0:D, :], par("iota", 0, D), None, ALU.is_equal
                                            ).then_inc(V[s].mark("onehot"), 1)

                def scores(s):
                    wait_load(dve, gathered[s], i, NSCALE * TB * 2)
                    wait_now(dve, TE[s], i, "q")
                    for q in range(2):
                        query = ps[s][q][:, 0:TB * D].rearrange("p (t o d) -> p t o d", t=TB, o=1).to_broadcast((P, TB, NSCALE, D))
                        last = nc.vector.tensor_tensor(prod[s][:, q], emb[s][:, :, q], query, ALU.mult)
                    last.then_inc(V[s].mark("prod"), 1)

                for s in STREAMS:
                    hash_scores(s)
                for s in STREAMS:
                    scores(s)
                for s in STREAMS:
                    wait_now(dve, V[s], i, "prod")
                    nc.vector.tensor_reduce(sc[s][:].rearrange("p q t c -> p (q t c)"), prod[s][:].rearrange("p q t c d -> p (q t c) d"), AX, ALU.add
                                            ).then_inc(V[s].mark("score"), 1)
                for s in STREAMS:
                    wait_now(dve, V[s], i, "score")
                    nc.vector.tensor_reduce(mx[s][:, :], sc[s][:].rearrange("p q t c -> p (q t) c"), AX, ALU.max
                                            ).then_inc(V[s].mark("smax"), 1)

                def across(tile):
                    return tile[:, :].rearrange("p (n o) -> p n o", o=1).to_broadcast((P, 2 * TB, NSCALE))

                def by_token(tile):
                    return tile[:].rearrange("p q t c -> p (q t) c")

                for s in STREAMS:
                    wait_now(dve, V[s], i, "smax")
                    nc.vector.tensor_tensor(by_token(sc[s]), by_token(sc[s]), across(mx[s]), ALU.subtract
                                            ).then_inc(V[s].mark("sub"), 1)
                for s in STREAMS:
                    wait_now(dve, S[s], i, "exp")
                    nc.vector.tensor_reduce(mx[s][:, :], by_token(wt[s]), AX, ALU.add).then_inc(V[s].mark("sum"), 1)
                for s in STREAMS:
                    wait_now(dve, V[s], i, "sum")
                    nc.vector.reciprocal(mx[s][:, :], mx[s][:, :]).then_inc(V[s].mark("rec"), 1)
                for s in STREAMS:
                    wait_now(dve, V[s], i, "rec")
                    nc.vector.tensor_tensor(by_token(wt[s]), by_token(wt[s]), across(mx[s]), ALU.mult
                                            ).then_inc(V[s].mark("weight"), 1)
                for s in STREAMS:
                    wait_now(dve, V[s], i, "weight")
                    for q in range(2):
                        w = wt[s][:, q].rearrange("p t (c o) -> p t c o", o=1).to_broadcast((P, TB, NSCALE, D))
                        last = nc.vector.tensor_tensor(prod[s][:, q], emb[s][:, :, q], w, ALU.mult)
                    last.then_inc(V[s].mark("wprod"), 1)
                for s in STREAMS:
                    wait_now(dve, V[s], i, "wprod")
                    wait_before(dve, TE[s], i, "hashT")
                    for q in range(2):
                        last = nc.vector.tensor_reduce(hsum[s][:, :, q, :], prod[s][:, q].rearrange("p t c d -> p t d c"), AX, ALU.add)
                    last.then_inc(V[s].mark("hsum"), 1)
                for k in range(4):
                    for s in STREAMS:
                        if k == 0:
                            wait_now(dve, S[s], i, "hashT")
                            nc.vector.tensor_scalar(conv[s][:, :], hpad[s][:, 0:T], par.cols("conv_w", 0, 1), par("conv_b"),
                                                    ALU.mult, ALU.add).then_inc(V[s].mark("conv0"), 1)
                        else:
                            wait_now(dve, V[s], i, f"conv{k - 1}")
                            nc.vector.scalar_tensor_tensor(conv[s][:, :], hpad[s][:, k:k + T], par.cols("conv_w", k, k + 1),
                                                           conv[s][:, :], ALU.mult, ALU.add).then_inc(V[s].mark(f"conv{k}"), 1)
                for s in STREAMS:
                    wait_now(dve, S[s], i, "tanh")
                    nc.vector.tensor_scalar(gate[s][:, :], keep[s][:, :], 0.5, 0.5, ALU.mult, ALU.add).then_inc(V[s].mark("gate"), 1)
                for s in STREAMS:
                    wait_now(dve, V[s], i, "gate")
                    nc.vector.scalar_tensor_tensor(d0[s][:, :], gate[s][:, :], 1e-6, par("rest"), ALU.max, ALU.mult).then_inc(V[s].mark("d0"), 1)
                    nc.vector.scalar_tensor_tensor(d1[s][:, :], gate[s][:, :], 1e-6, par("first"), ALU.max, ALU.mult).then_inc(V[s].mark("d1"), 1)
                    nc.vector.tensor_scalar(clamped[s][:, :], gate[s][:, :], 1e-6, None, ALU.max).then_inc(V[s].mark("clamped"), 1)
                for s in STREAMS:
                    wait_now(dve, V[s], i, "d1")
                    nc.vector.tensor_tensor_scan(cum[s][:, :], d0[s][:, :], d1[s][:, :], 0.0, ALU.mult, ALU.add).then_inc(V[s].mark("cum"), 1)
                    nc.vector.tensor_scalar(keep[s][:, :], keep[s][:, :], -0.5, 0.5, ALU.mult, ALU.add).then_inc(V[s].mark("keep"), 1)
                for s in STREAMS:
                    wait_now(dve, V[s], i, "keep")
                    nc.vector.scalar_tensor_tensor(fed[s][:, :], ps[s][3][0:2 * SS, :], par("bi"), keep[s][:, :], ALU.add, ALU.mult
                                                   ).then_inc(V[s].mark("drive"), 1)
                    nc.vector.tensor_scalar(cum[s][:, :], cum[s][:, :], 1e8, 1.0, ALU.mult, ALU.min).then_inc(V[s].mark("ratio"), 1)
                for s in STREAMS:
                    wait_now(dve, V[s], i, "ratio")
                    nc.vector.tensor_tensor(fed[s][:, :], fed[s][:, :], cum[s][:, :], ALU.mult).then_inc(V[s].mark("fed"), 1)
                for s in STREAMS:
                    wait_now(dve, V[s], i, "fed")
                    nc.vector.tensor_tensor_scan(states[s][:, :], clamped[s][:, :], fed[s][:, :], 0.0, ALU.mult, ALU.add
                                                 ).then_inc(V[s].mark("states"), 1)
                for s in STREAMS:
                    wait_now(dve, S[s], i, "std")
                    nc.vector.reciprocal(sq[s][:].rearrange("p a t -> p (a t)"), sq[s][:].rearrange("p a t -> p (a t)")).then_inc(V[s].mark("rstd"), 1)
                for s in STREAMS:
                    wait_now(dve, V[s], i, "rstd")
                    nc.vector.tensor_tensor(xc[s][:], xc[s][:], sq[s][:], ALU.mult).then_inc(V[s].mark("norm"), 1)
                for l in range(NMLP):
                    for s in STREAMS:
                        wait_now(dve, S[s], i, f"act{l}")
                        nc.vector.tensor_tensor(h[s][:], h[s][:], sq[s][:], ALU.add).then_inc(V[s].mark(f"res{l}"), 1)

        @block.scalar
        def _(act):
            for s in STREAMS:
                nc.scalar.sem_inc(S[s].sem, len(SSN))
            act.wait_ge(setup_v, 1)
            act.wait_ge(pads, 1)
            with act.Fori(0, N) as i:
                for s in STREAMS:
                    wait_now(act, V[s], i, "sub")
                    nc.scalar.activation(wt[s][:], sc[s][:], ACT.Exp, scale=D ** -0.5).then_inc(S[s].mark("exp"), 1)
                for s in STREAMS:
                    wait_now(act, TE[s], i, "hashT")
                    nc.scalar.activation(hpad[s][:, 3:3 + T], ps[s][2][:, :], ACT.Copy).then_inc(S[s].mark("hashT"), 1)
                for s in STREAMS:
                    wait_now(act, V[s], i, "conv3")
                    nc.scalar.activation(feat[s][0:D, 0, :], conv[s][0:D, :], ACT.Silu)
                    nc.scalar.activation(feat[s][D:P, 1, :], conv[s][D:P, :], ACT.Silu).then_inc(S[s].mark("silu_hash"), 1)
                for s in STREAMS:
                    wait_now(act, TE[s], i, "feat")
                    wait_before(act, TE[s], i, "out")
                    for q in range(2):
                        last = nc.scalar.activation(h[s][:, q, :], ps[s][q][:, :], ACT.Silu, bias=par("b_in"))
                    last.then_inc(S[s].mark("h1"), 1)
                for s in STREAMS:
                    wait_now(act, TE[s], i, "gates")
                    nc.scalar.activation(keep[s][:, :], ps[s][2][0:2 * SS, :], ACT.Tanh, bias=half_bg[:, :], scale=0.5
                                         ).then_inc(S[s].mark("tanh"), 1)
                for s in STREAMS:
                    wait_now(act, TE[s], i, "center")
                    for q in range(2):
                        last = nc.scalar.activation(xc[s][:, q, :], ps[s][q][:, :], ACT.Identity, bias=bo_c[:, :])
                    last.then_inc(S[s].mark("centered"), 1)
                    for q in range(2):
                        last = nc.scalar.activation(sq[s][:, q, :], ps[s][q][:, :], ACT.Square, bias=bo_c[:, :])
                    last.then_inc(S[s].mark("square"), 1)
                for s in STREAMS:
                    wait_now(act, TE[s], i, "var")
                    for q in range(2):
                        last = nc.scalar.activation(sq[s][:, q, :], ps[s][2 + q][:, :], ACT.Sqrt, bias=par("eps"))
                    last.then_inc(S[s].mark("std"), 1)
                for s in STREAMS:
                    wait_now(act, V[s], i, "norm")
                    for q in range(2):
                        last = nc.scalar.activation(h[s][:, q, :], xc[s][:, q, :], ACT.Identity, bias=par("ln_b"), scale=par("ln_g"))
                    last.then_inc(S[s].mark("affine"), 1)
                for l in range(NMLP):
                    for s in STREAMS:
                        wait_now(act, TE[s], i, f"mlp{l}")
                        wait_now(act, V[s], i, "norm" if l == 0 else f"res{l - 1}")
                        for q in range(2):
                            last = nc.scalar.activation(sq[s][:, q, :], ps[s][q][:, :], ACT.Silu, bias=par.cols("mlp_b", l, l + 1))
                        last.then_inc(S[s].mark(f"act{l}"), 1)
                for s in STREAMS:
                    wait_now(act, TE[s], i, "out")
                    act.wait_ge(stored[s], i * 16)
                    nc.scalar.activation(ho[s][:, :], ps[s][2][:, :], ACT.Identity, bias=par("bout")).then_inc(S[s].mark("out"), 1)

        @block.tensor
        def _(pe):
            for s in STREAMS:
                nc.tensor.sem_inc(TE[s].sem, len(TS))
            pe.wait_ge(params_loaded, 16)
            nc.tensor.matmul(ps[0][0][:, 0:D], par("embT"), par("wq"), start=True, stop=True)
            nc.tensor.matmul(ps[0][1][:, 0:H], par("embT"), par("win_e"), start=True, stop=True)
            nc.tensor.matmul(ps[0][2][0:2 * SS, 0:H], par("woT"), par("cen"), start=True, stop=True)
            nc.tensor.matmul(ps[0][3][:, 0:1], par("cen"), par("bo"), start=True, stop=True).then_inc(setup_pe, 1)
            pe.wait_ge(setup_v, 1)
            with pe.Fori(0, N) as i:
                for s in STREAMS:
                    wait_now(pe, V[s], i, "onehot")
                    wait_before(pe, S[s], i, "act2")
                    for t in range(TB):
                        nc.tensor.matmul(ps[s][0][:, t * D:(t + 1) * D], feat[s][D:P, 0, t * P:(t + 1) * P], tq[D:P, :], start=True, stop=True)
                        last = nc.tensor.matmul(ps[s][1][:, t * D:(t + 1) * D], feat[s][0:D, 1, t * P:(t + 1) * P], tq[0:D, :], start=True, stop=True)
                    last.then_inc(TE[s].mark("q"), 1)
                for s in STREAMS:
                    wait_now(pe, V[s], i, "hsum")
                    wait_before(pe, S[s], i, "out")
                    for t in range(TB):
                        last = nc.tensor.transpose(ps[s][2][:, t * P:(t + 1) * P], hsum[s][:, t].rearrange("p q d -> p (q d)"), par("ident"))
                    last.then_inc(TE[s].mark("hashT"), 1)
                for s in STREAMS:
                    wait_now(pe, S[s], i, "silu_hash")
                    wait_load(pe, mf_in[s], i)
                    for q, w in enumerate(("w1a", "w1b")):
                        nc.tensor.matmul(ps[s][q][:, :], par(w), feat[s][:, q, :], start=True, stop=False)
                        last = nc.tensor.matmul(ps[s][q][:, :], par("wmf"), mf[s][:, q, :], start=False, stop=True)
                    last.then_inc(TE[s].mark("feat"), 1)
                for s in STREAMS:
                    wait_now(pe, S[s], i, "h1")
                    for q in range(2):
                        nc.tensor.matmul(ps[s][2][SS * q:SS * (q + 1), :], par("wg"), h[s][:, q, :], start=True, stop=True)
                        last = nc.tensor.matmul(ps[s][3][SS * q:SS * (q + 1), :], par("wi"), h[s][:, q, :], start=True, stop=True)
                    last.then_inc(TE[s].mark("gates"), 1)
                for s in STREAMS:
                    wait_now(pe, V[s], i, "states")
                    for q in range(2):
                        nc.tensor.matmul(ps[s][q][:, :], par("cen"), h[s][:, q, :], start=True, stop=False)
                        last = nc.tensor.matmul(ps[s][q][:, :], wo_c[SS * q:SS * (q + 1), :], states[s][SS * q:SS * (q + 1), :], start=False, stop=True)
                    last.then_inc(TE[s].mark("center"), 1)
                for s in STREAMS:
                    wait_now(pe, S[s], i, "square")
                    for q in range(2):
                        last = nc.tensor.matmul(ps[s][2 + q][:, :], par("avg"), sq[s][:, q, :], start=True, stop=True)
                    last.then_inc(TE[s].mark("var"), 1)
                for l in range(NMLP):
                    for s in STREAMS:
                        if l == 0:
                            wait_now(pe, S[s], i, "affine")
                        else:
                            wait_now(pe, V[s], i, f"res{l - 1}")
                        for q in range(2):
                            last = nc.tensor.matmul(ps[s][q][:, :], par.cols("mlp_w", l * H, (l + 1) * H), h[s][:, q, :], start=True, stop=True)
                        last.then_inc(TE[s].mark(f"mlp{l}"), 1)
                for s in STREAMS:
                    wait_now(pe, V[s], i, "res2")
                    for q in range(2):
                        last = nc.tensor.matmul(ps[s][2][D * q:D * (q + 1), :], par("wout"), h[s][:, q, :], start=True, stop=True)
                    last.then_inc(TE[s].mark("out"), 1)



def qkv_stage(nc, dram):
    VS = ["norm", "bias0", "bias1", "bias2", "bias3"]
    SSN = ["square", "log", "rstd", "gram"]
    TS = ["center", "var", "qkv0", "qkv1", "qkv2", "qkv3", "gram"]
    with ExitStack() as ctx:
        def sb(name, shape, dt=F32):
            return [ctx.enter_context(nc.sbuf_tensor(f"qkv_{name}{s}", shape, dt)) for s in STREAMS]

        def sem(name):
            return nc.alloc_semaphore(f"qkv_{name}")

        params, par, params_loaded = load_params(nc, ctx, "qkv", dram)
        h, sq, xn = sb("h", [P, T]), sb("sq", [P, T]), sb("xn", [P, T])
        qkv = sb("qkv", [P, 2, TB, 3 * D])
        gram = sb("gram", [P, 2, P])
        ps = [[ctx.enter_context(nc.psum_tensor(f"qkv_ps{s}{k}", [P, T], F32)) for k in range(4)] for s in STREAMS]
        h_in, tok_out, gram_out = ([sem(f"{n}{s}") for s in STREAMS] for n in ("h_in", "tokens_stored", "gram_stored"))
        V = [Steps(sem(f"vector_steps{s}"), VS) for s in STREAMS]
        S = [Steps(sem(f"scalar_steps{s}"), SSN) for s in STREAMS]
        TE = [Steps(sem(f"tensor_steps{s}"), TS) for s in STREAMS]
        block = ctx.enter_context(nc.Block())
        N = PAIRS // 2

        @block.sync
        def _(sp):
            sp.dma_start(params[:, :], dram["params_qkv"]).then_inc(params_loaded, 16)
            with sp.Fori(0, N) as i:
                for s in STREAMS:
                    wait_before(sp, TE[s], i, "center")
                    sp.dma_start(h[s][:, :], dram["h0"][bass.ds(i * 2 + s, 1), :, :].rearrange("a p t -> (a p) t")).then_inc(h_in[s], 16)
                for s in STREAMS:
                    wait_now(sp, V[s], i, "bias3")
                    sp.dma_start(dram["tokens"][bass.ds(i * 4 + 2 * s, 2), :, :, :].rearrange("q p t c -> p q (t c)"),
                                 qkv[s][:].rearrange("p q t c -> p q (t c)")).then_inc(tok_out[s], 16)
                    wait_now(sp, S[s], i, "gram")
                    sp.dma_start(dram["gram"][bass.ds(i * 4 + 2 * s, 2), :, :].rearrange("q p c -> p q c"), gram[s][:]).then_inc(gram_out[s], 16)
            for s in STREAMS:
                sp.wait_ge(tok_out[s], 16 * N)
                sp.wait_ge(gram_out[s], 16 * N)

        @block.vector
        def _(dve):
            for s in STREAMS:
                nc.vector.sem_inc(V[s].sem, len(VS))
            dve.wait_ge(params_loaded, 16)
            with dve.Fori(0, N) as i:
                for s in STREAMS:
                    wait_now(dve, S[s], i, "rstd")
                    wait_before(dve, TE[s], i, "qkv3")
                    nc.vector.tensor_tensor(xn[s][:, :], ps[s][0][:, :], sq[s][:, :], ALU.mult).then_inc(V[s].mark("norm"), 1)
                bias = par("bqkv").rearrange("p (o c) -> p o c", o=1).to_broadcast((P, 2, 3 * D))
                for k in range(4):
                    for s in STREAMS:
                        if k == 0:
                            dve.wait_ge(tok_out[s], i * 16)
                        wait_now(dve, TE[s], i, f"qkv{k}")
                        nc.vector.tensor_tensor(qkv[s][:, k // 2, 2 * (k % 2):2 * (k % 2) + 2, :],
                                                ps[s][k][:, 0:6 * D].rearrange("p (t c) -> p t c", t=2), bias, ALU.add
                                                ).then_inc(V[s].mark(f"bias{k}"), 1)

        @block.scalar
        def _(act):
            for s in STREAMS:
                nc.scalar.sem_inc(S[s].sem, len(SSN))
            act.wait_ge(params_loaded, 16)
            with act.Fori(0, N) as i:
                for s in STREAMS:
                    wait_now(act, TE[s], i, "center")
                    nc.scalar.activation(sq[s][:, :], ps[s][0][:, :], ACT.Square).then_inc(S[s].mark("square"), 1)
                for s in STREAMS:
                    wait_now(act, TE[s], i, "var")
                    nc.scalar.activation(sq[s][:, :], ps[s][1][:, :], ACT.Ln, bias=par("eps")).then_inc(S[s].mark("log"), 1)
                for s in STREAMS:
                    wait_now(act, S[s], i, "log")
                    nc.scalar.activation(sq[s][:, :], sq[s][:, :], ACT.Exp, scale=-0.5).then_inc(S[s].mark("rstd"), 1)
                for s in STREAMS:
                    wait_now(act, TE[s], i, "gram")
                    act.wait_ge(gram_out[s], i * 16)
                    for q in range(2):
                        last = nc.scalar.activation(gram[s][:, q, :], ps[s][q][:, 384:384 + P], ACT.Copy)
                    last.then_inc(S[s].mark("gram"), 1)

        @block.tensor
        def _(pe):
            for s in STREAMS:
                nc.tensor.sem_inc(TE[s].sem, len(TS))
            pe.wait_ge(params_loaded, 16)
            with pe.Fori(0, N) as i:
                for s in STREAMS:
                    wait_load(pe, h_in[s], i)
                    wait_before(pe, S[s], i, "gram")
                    wait_before(pe, V[s], i, "bias1")
                    nc.tensor.matmul(ps[s][0][:, :], par("cen2"), h[s][:, :], start=True, stop=True).then_inc(TE[s].mark("center"), 1)
                for s in STREAMS:
                    wait_now(pe, S[s], i, "square")
                    nc.tensor.matmul(ps[s][1][:, :], par("avg2"), sq[s][:, :], start=True, stop=True).then_inc(TE[s].mark("var"), 1)
                for s in STREAMS:
                    wait_now(pe, V[s], i, "norm")
                    wait_before(pe, V[s], i, "bias3")
                    for k in range(4):
                        q = k // 2
                        for t in range(2):
                            tt = 2 * (k % 2) + t
                            last = nc.tensor.matmul(ps[s][k][:, t * 3 * D:(t + 1) * 3 * D], xn[s][D * q:D * (q + 1), tt * P:(tt + 1) * P],
                                                    par("wqkv", D * q, D * (q + 1)), start=True, stop=True)
                        last.then_inc(TE[s].mark(f"qkv{k}"), 1)
                for s in STREAMS:
                    wait_now(pe, V[s], i, "bias3")
                    for q in range(2):
                        for t in range(TB):
                            last = nc.tensor.matmul(ps[s][q][:, 384:384 + P], qkv[s][:, q, t, 0:P], qkv[s][:, q, t, 0:P],
                                                    start=(t == 0), stop=(t == TB - 1))
                    last.then_inc(TE[s].mark("gram"), 1)


def qr_stage(nc, dram):
    G = 4
    with ExitStack() as ctx:
        def sb(name, shape):
            return ctx.enter_context(nc.sbuf_tensor(f"qr_{name}", shape, F32))

        def sem(name):
            return nc.alloc_semaphore(f"qr_{name}")

        aug = sb("aug", [P, G, HD, 2 * HD])
        top = sb("top", [P, G, HD, HD])
        eye = sb("eye", [P, G * HD * HD])
        prod = sb("prod", [P, HD, HD, HD])
        outer = sb("outer", [P, G, HD, 2 * HD])
        factor = sb("factor", [P, G, HD])
        rec = sb("rec", [P, G])
        diag = sb("diag", [P, G, HD])
        root = sb("root", [P, G, HD])
        li = sb("li", [P, G, HD, HD])
        w = sb("w", [P, G, HD, HD])
        sign = sb("sign", [P, G, HD])
        both = sb("both", [P, 2, HD])
        lq = sb("lq", [P, 2, HD, HD])
        blocks = sb("blocks", [P, 2, HD, HD])
        zero = sb("zero", [P, B * D * D // P])
        loaded, cleared, zeroed, steps, rooted, pivots, made, stored = (
            sem(n) for n in ("loaded", "zero_made", "blocks_zeroed", "vector_steps", "roots", "pivots", "blocks_made", "stored"))
        block = ctx.enter_context(nc.Block())
        LOADS = 2 * G * 4 + 1

        @block.sync
        def _(sp):
            sp.dma_start(eye[:, :], dram["params_qr"]).then_inc(loaded, 16)
            for a in range(4):
                for g in range(G):
                    r = (g // 2) * D + (2 * a + g % 2) * HD
                    sp.dma_start(aug[32 * a:32 * a + 32, g, :, 0:HD], dram["gram"][:, r:r + HD, r:r + HD]).then_inc(loaded, 16)
                    sp.dma_start(top[32 * a:32 * a + 32, g, :, :], dram["tokens"][0:B, 0:HD, 0, r:r + HD]).then_inc(loaded, 16)
            sp.wait_ge(cleared, 1)
            sp.dma_start(dram["blocks"][0:B].rearrange("b r c -> (b r c)").rearrange("(p n) -> p n", p=P), zero[:, :]).then_inc(zeroed, 16)
            sp.wait_ge(made, 1)
            sp.wait_ge(zeroed, 16)
            for a in range(4):
                for k in range(2):
                    r = (2 * a + k) * HD
                    sp.dma_start(dram["blocks"][0:B, r:r + HD, r:r + HD], blocks[32 * a:32 * a + 32, k, :, :]).then_inc(stored, 16)
            sp.wait_ge(stored, 16 * 8)

        @block.gpsimd
        def _(pool):
            nc.gpsimd.memset(zero[:, :], 0.0).then_inc(cleared, 1)

        @block.scalar
        def _(act):
            act.wait_ge(pivots, 1)
            nc.scalar.activation(root[:, :, :], diag[:, :, :], ACT.Sqrt).then_inc(rooted, 1)

        @block.vector
        def _(dve):
            count = [0]

            def then(ins):
                count[0] += 1
                ins.then_inc(steps, 1)
                dve.wait_ge(steps, count[0])

            dve.wait_ge(loaded, 16 * LOADS)
            then(nc.vector.tensor_copy(aug[:, :, :, HD:2 * HD], eye[:, :].rearrange("p (g r c) -> p g r c", g=G, r=HD)))
            for j in range(HD):
                then(nc.vector.tensor_copy(diag[:, :, j], aug[:, :, j, j]))
                if j == HD - 1:
                    break
                n = HD - 1 - j
                then(nc.vector.reciprocal(rec[:, :], aug[:, :, j, j]))
                then(nc.vector.tensor_tensor(factor[:, :, 0:n], aug[:, :, j + 1:HD, j],
                                             rec[:, :].rearrange("p (g o) -> p g o", o=1).to_broadcast((P, G, n)), ALU.mult))
                then(nc.vector.tensor_tensor(
                    outer[:, :, 0:n, :], factor[:, :, 0:n].rearrange("p g (n o) -> p g n o", o=1).to_broadcast((P, G, n, 2 * HD)),
                    aug[:, :, j:j + 1, :].to_broadcast((P, G, n, 2 * HD)), ALU.mult))
                then(nc.vector.tensor_tensor(aug[:, :, j + 1:HD, :], aug[:, :, j + 1:HD, :], outer[:, :, 0:n, :], ALU.subtract))
            nc.vector.sem_inc(pivots, 1)
            dve.wait_ge(rooted, 1)
            then(nc.vector.reciprocal(root[:, :, :], root[:, :, :]))
            then(nc.vector.tensor_tensor(li[:, :, :, :], aug[:, :, :, HD:2 * HD],
                                         root[:, :, :].rearrange("p g (r o) -> p g r o", o=1).to_broadcast((P, G, HD, HD)), ALU.mult))
            for g in range(G):
                then(nc.vector.tensor_tensor(
                    prod[:, :, :, :], top[:, g, :, :].rearrange("p n (o j) -> p n o j", o=1).to_broadcast((P, HD, HD, HD)),
                    li[:, g:g + 1, :, :].to_broadcast((P, HD, HD, HD)), ALU.mult))
                then(nc.vector.tensor_reduce(w[:, g, :, :], prod[:, :, :, :], AX, ALU.add))
            for d in range(HD):
                then(nc.vector.tensor_scalar(sign[:, :, d], w[:, :, d, d], 0.0, None, ALU.is_ge))
                then(nc.vector.tensor_scalar(sign[:, :, d], sign[:, :, d], -2.0, 1.0, ALU.mult, ALU.add))
                if d == HD - 1:
                    break
                n = HD - 1 - d
                then(nc.vector.tensor_tensor(rec[:, :], w[:, :, d, d], sign[:, :, d], ALU.subtract))
                then(nc.vector.reciprocal(rec[:, :], rec[:, :]))
                then(nc.vector.tensor_tensor(factor[:, :, 0:n], w[:, :, d + 1:HD, d],
                                             rec[:, :].rearrange("p (g o) -> p g o", o=1).to_broadcast((P, G, n)), ALU.mult))
                then(nc.vector.tensor_tensor(
                    outer[:, :, 0:n, 0:n], factor[:, :, 0:n].rearrange("p g (n o) -> p g n o", o=1).to_broadcast((P, G, n, n)),
                    w[:, :, d:d + 1, d + 1:HD].to_broadcast((P, G, n, n)), ALU.mult))
                then(nc.vector.tensor_tensor(w[:, :, d + 1:HD, d + 1:HD], w[:, :, d + 1:HD, d + 1:HD], outer[:, :, 0:n, 0:n], ALU.subtract))
            then(nc.vector.tensor_tensor(both[:, :, :], sign[:, 0:2, :], sign[:, 2:4, :], ALU.mult))
            then(nc.vector.tensor_tensor(lq[:, :, :, :], li[:, 0:2, :, :],
                                         both[:, :, :].rearrange("p g (r o) -> p g r o", o=1).to_broadcast((P, 2, HD, HD)), ALU.mult))
            for k in range(2):
                then(nc.vector.tensor_tensor(
                    prod[:, :, :, :], li[:, 2 + k, :, :].rearrange("p d (j o) -> p j o d", o=1).to_broadcast((P, HD, HD, HD)),
                    lq[:, k, :, :].rearrange("p d (o i) -> p o i d", o=1).to_broadcast((P, HD, HD, HD)), ALU.mult))
                then(nc.vector.tensor_reduce(blocks[:, k, :, :], prod[:, :, :, :], AX, ALU.add))
            nc.vector.sem_inc(made, 1)


class Count:

    def __init__(self, sem, per_round):
        self.sem, self.per_round = sem, per_round

    def value(self, i, j):
        return i * self.per_round + (self.per_round + j + 1)


def attention_stage(nc, dram):
    R = 2 * HEADS
    NT = TB
    widths = [P, P, NFEAT - 2 * P]
    quads = [P, P, NQUAD - 2 * P]
    with ExitStack() as ctx:
        def one(name, shape, dt=F32):
            return ctx.enter_context(nc.sbuf_tensor(f"attn_{name}", shape, dt))

        def sb(name, shape, dt=F32):
            return [one(f"{name}{k}", shape, dt) for k in range(2)]

        def sem(name):
            return nc.alloc_semaphore(f"attn_{name}")

        def bank(name):
            return ctx.enter_context(nc.psum_tensor(f"attn_{name}", [P, T], F32))

        params, par, params_loaded = load_params(nc, ctx, "attn", dram)
        tok = sb("tok", [P, TB, 3 * D])
        blk = sb("blk", [P, D])
        resid = sb("resid", [D, T])
        kt_sb = one("kt", [P, T])
        k2 = one("k2", [P, TB, D])
        fq, fk, fk2 = one("fq", [P, TB, NFEAT]), one("fk", [P, TB, NFEAT]), one("fk2", [P, TB, NQUAD])
        fqt, fkt, fk2t = sb("fqt", [P, 3, T]), sb("fkt", [P, 3, T]), sb("fk2t", [P, 3, T])
        psi = sb("psi", [P, 3, T])
        prob = sb("prob", [P, NT, T])
        probt = sb("probt", [P, NT, T])
        nmax = one("nmax", [P, 2, NT])
        rsum = sb("rsum", [P, NT, HEADS])
        on = one("on", [P, NT, 2 * D])
        ot = one("ot", [D, T])
        hout = one("hout", [D, T])
        coef_b, coef_c = one("coef_b", [P, 3, HEADS]), one("coef_c", [P, 3, HEADS])
        bn = one("bn", [3 * HEADS, 4])
        cw = one("cw", [3 * HEADS, 2, HEADS])
        L = [bank(f"logits{k}") for k in range(NT)]
        PT = [bank(f"turned{k}") for k in range(2)]
        O, X = bank("values"), bank("features")

        tok_in = [sem(f"tokens_in{k}") for k in range(2)]
        blk_in = [sem(f"blocks_in{k}") for k in range(2)]
        res_in = [sem(f"residual_in{k}") for k in range(2)]
        stored, extra = sem("h_stored"), sem("extra_copied")
        setup_s, setup_v, setup_pe, ones_set = sem("setup_s"), sem("setup_v"), sem("setup_pe"), sem("ones_set")

        def count(name, per_round):
            return Count(sem(name), per_round)

        logits, maxes, exps = count("logits", R * NT), count("maxes", R * NT), count("exps", R * NT)
        turned, turned_sb = count("turned", R * NT), count("turned_sb", R * NT)
        values = count("values", R)
        psi_b, psi_all = count("psi_b", R), count("psi_all", R)
        kt_ps, kt_copied, k2_ps, k2_copied = (count(n, 2) for n in ("kt_ps", "kt_copied", "k2_ps", "k2_copied"))
        mono = count("mono", 6)
        feat_ps, feat_copied = count("feat_ps", 18), count("feat_copied", 18)
        normed, rsum_inv = count("normed", 2), count("rsum_inv", 2)
        ot_ps, ot_copied, proj_ps, resid_added = (count(n, 2) for n in ("ot_ps", "ot_copied", "proj_ps", "resid_added"))
        block = ctx.enter_context(nc.Block())
        N = B // 2
        h0, h1 = dram["h0"].rearrange("a (q d) t -> (a q) d t", q=2), dram["h1"].rearrange("a (q d) t -> (a q) d t", q=2)

        def wait(eng, c, i, j):
            eng.wait_ge(c.sem, c.value(i, j))

        def prime(eng, *counts):
            for c in counts:
                eng.sem_inc(c.sem, c.per_round)

        @block.sync
        def _(sp):
            sp.dma_start(params[:, :], dram["params_attn"]).then_inc(params_loaded, 16)
            sp.dma_start(dram["tokens"][B], dram["tokens"][0]).then_inc(extra, 16)
            sp.dma_start(dram["blocks"][B], dram["blocks"][0]).then_inc(extra, 16)
            sp.wait_ge(extra, 32)

            def load(i, n, seq):
                k = n % 2
                wait(sp, values, i, (n - 2) * HEADS + HEADS - 1)
                sp.dma_start(tok[k][:, :, :], dram["tokens"][bass.ds(seq, 1), :, :, :].rearrange("a p t c -> p (a t) c")).then_inc(tok_in[k], 16)
                wait(sp, k2_ps, i, n - 2)
                sp.dma_start(blk[k][D:P, :], dram["blocks"][bass.ds(seq, 1), :, :].rearrange("a r c -> (a r) c")).then_inc(blk_in[k], 16)

            load(0, 0, 0)
            with sp.Fori(0, N) as i:
                nexts = [sp.snap(i * 2 + 1), sp.snap(i * 2 + 2)]
                for n in range(2):
                    wait(sp, resid_added, i, n - 2)
                    sp.dma_start(resid[n][:, :], h0[bass.ds(i * 2 + n, 1), :, :].rearrange("a p t -> (a p) t")).then_inc(res_in[n], 16)
                    load(i, n + 1, nexts[n])
                    wait(sp, resid_added, i, n)
                    sp.dma_start(h1[bass.ds(i * 2 + n, 1), :, :].rearrange("a p t -> (a p) t"), hout[:, :]).then_inc(stored, 16)
            sp.wait_ge(stored, 16 * B)

        @block.gpsimd
        def _(pool):
            prime(nc.gpsimd, mono)
            nc.gpsimd.memset(on[:, :, D:2 * D], 0.0)
            nc.gpsimd.memset(fq[:, :, NFEAT - 1:NFEAT], 1.0)
            nc.gpsimd.memset(fk[:, :, NFEAT - 1:NFEAT], 1.0).then_inc(ones_set, 1)

            def products(dst, src, linear):
                at = 0
                quad = dst[:, :, 0:NQUAD].rearrange("p t (h m) -> p t h m", h=HEADS)
                x = src.rearrange("p t (h d) -> p t h d", h=HEADS)
                for r in range(HD):
                    last = nc.gpsimd.tensor_tensor(quad[:, :, :, at:at + HD - r], x[:, :, :, 0:HD - r], x[:, :, :, r:HD], ALU.mult)
                    at += HD - r
                if linear:
                    last = nc.gpsimd.tensor_copy(dst[:, :, NQUAD:NQUAD + D], src)
                last.then_inc(mono.sem, 1)

            def prepare(i, n):
                k = n % 2
                pool.wait_ge(tok_in[k], i * 16 + 16 * (n // 2 + 1))
                wait(pool, feat_ps, i, 9 * (n - 1) + 2)
                products(fq, tok[k][:, :, 0:D], True)
                wait(pool, feat_ps, i, 9 * (n - 1) + 5)
                products(fk, tok[k][:, :, D:2 * D], True)
                wait(pool, k2_copied, i, n)
                wait(pool, feat_ps, i, 9 * (n - 1) + 8)
                products(fk2, k2[:, :, :], False)

            prepare(0, 0)
            with pool.Fori(0, N) as i:
                for n in range(2):
                    prepare(i, n + 1)

        @block.scalar
        def _(act):
            prime(nc.scalar, exps, psi_b, kt_copied, k2_copied, feat_copied, ot_copied)
            act.wait_ge(params_loaded, 16)
            nc.scalar.activation(bn[:, 0:1], par("var"), ACT.Ln, bias=par("eps")).then_inc(setup_s, 1)
            act.wait_ge(setup_s, 1)
            nc.scalar.activation(bn[:, 0:1], bn[:, 0:1], ACT.Exp, scale=-0.5).then_inc(setup_s, 1)
            act.wait_ge(setup_v, 7)

            def keys_turned(i, n):
                wait(act, kt_ps, i, n)
                nc.scalar.activation(kt_sb[D:P, :], X[D:P, :], ACT.Copy).then_inc(kt_copied.sem, 1)

            def keys_mapped(i, n):
                wait(act, k2_ps, i, n)
                wait(act, mono, i, 3 * (n - 1) + 2)
                nc.scalar.activation(k2[:, :, :].rearrange("p t d -> p (t d)"), X[:, 0:TB * D], ACT.Copy).then_inc(k2_copied.sem, 1)

            def features(i, n, a):
                k = n % 2
                for c in range(3):
                    wait(act, feat_ps, i, 9 * n + 3 * a + c)
                    dst, rows = (fqt, widths) if a == 0 else (fkt, widths) if a == 1 else (fk2t, quads)
                    nc.scalar.activation(dst[k][0:rows[c], c, :], X[0:rows[c], :], ACT.Copy).then_inc(feat_copied.sem, 1)

            def keys_weighted(i, g):
                wait(act, logits, i, (g - 2) * NT + NT - 1)
                wait(act, feat_copied, i, 9 * (g // HEADS) + 8)
                for c in range(3):
                    r = widths[c]
                    last = nc.scalar.activation(psi[g % 2][0:r, c, :], fkt[g // HEADS % 2][0:r, c, :], ACT.Copy,
                                                scale=coef_b[0:r, c, g % HEADS:g % HEADS + 1])
                last.then_inc(psi_b.sem, 1)

            keys_turned(0, 0)
            keys_mapped(0, 0)
            for a in range(3):
                features(0, 0, a)
            keys_weighted(0, 0)
            with act.Fori(0, N) as i:
                for g in range(R + 2):
                    n, o = g // HEADS, g % HEADS
                    if g < R:
                        keys_weighted(i, g + 1)
                        wait(act, turned, i, (g - 2) * NT + NT - 1)
                        for t in range(NT):
                            wait(act, maxes, i, g * NT + t)
                            nc.scalar.activation(prob[g % 2][:, t, :], L[t][:, :], ACT.Exp, bias=nmax[:, g % 2, t:t + 1],
                                                 accum_out=rsum[n][:, t, o:o + 1]).then_inc(exps.sem, 1)
                        if o == 2:
                            keys_turned(i, n + 1)
                        if o == 3:
                            keys_mapped(i, n + 1)
                        if o in (4, 5, 6):
                            features(i, n + 1, o - 4)
                    if g in (HEADS + 1, R + 1):
                        n = g // HEADS - 1
                        wait(act, ot_ps, i, n)
                        nc.scalar.activation(ot[:, :], X[0:D, :], ACT.Copy).then_inc(ot_copied.sem, 1)

        @block.vector
        def _(dve):
            prime(nc.vector, maxes, turned_sb, psi_all, normed, rsum_inv, resid_added)
            setup = [0]

            def then(ins):
                setup[0] += 1
                ins.then_inc(setup_v, 1)
                dve.wait_ge(setup_v, setup[0])

            dve.wait_ge(params_loaded, 16)
            dve.wait_ge(setup_s, 2)
            then(nc.vector.tensor_tensor(bn[:, 1:2], bn[:, 0:1], par("gamma"), ALU.mult))
            then(nc.vector.tensor_tensor(bn[:, 2:3], bn[:, 1:2], par("mean"), ALU.mult))
            then(nc.vector.tensor_tensor(bn[:, 3:4], par("beta"), bn[:, 2:3], ALU.subtract))
            then(nc.vector.tensor_scalar(cw[:, 1, :], par("convT"), bn[:, 3:4], None, ALU.mult))
            then(nc.vector.tensor_scalar(cw[:, 0, :], par("convT"), bn[:, 1:2], par("scales"), ALU.mult, ALU.mult))
            dve.wait_ge(setup_pe, 1)
            nc.vector.tensor_copy(coef_b[:, :, :].rearrange("p c o -> p (c o)"), X[:, 0:24])
            then(nc.vector.tensor_copy(coef_c[:, :, :].rearrange("p c o -> p (c o)"), X[:, 24:48]))
            then(nc.vector.scalar_tensor_tensor(coef_b[:, 2, :], par("conv_b"), par("last"), coef_b[:, 2, :], ALU.mult, ALU.add))

            def keys_mixed(i, g):
                wait(dve, psi_b, i, g)
                for c in range(3):
                    r = quads[c]
                    last = nc.vector.scalar_tensor_tensor(psi[g % 2][0:r, c, :], fk2t[g // HEADS % 2][0:r, c, :],
                                                          coef_c[0:r, c, g % HEADS:g % HEADS + 1], psi[g % 2][0:r, c, :],
                                                          ALU.mult, ALU.add)
                last.then_inc(psi_all.sem, 1)

            keys_mixed(0, 0)
            with dve.Fori(0, N) as i:
                for g in range(R + 2):
                    for half in range(2):
                        if g < R:
                            for t in (2 * half, 2 * half + 1):
                                wait(dve, logits, i, g * NT + t)
                                wait(dve, exps, i, (g - 2) * NT + t)
                                nc.vector.tensor_reduce(nmax[:, g % 2, t:t + 1], L[t][:, :], AX, ALU.max, negate=True
                                                        ).then_inc(maxes.sem, 1)
                        if 1 <= g <= R:
                            if half == 0:
                                wait(dve, values, i, g - 3)
                            for t in (2 * half, 2 * half + 1):
                                wait(dve, turned, i, (g - 1) * NT + t)
                                nc.vector.tensor_copy(probt[(g - 1) % 2][:, t, :], PT[t % 2][:, :]).then_inc(turned_sb.sem, 1)
                        if half == 0 and g < R:
                            keys_mixed(i, g + 1)
                    if g in (HEADS + 1, R + 1):
                        n = g // HEADS - 1
                        wait(dve, exps, i, n * HEADS * NT + HEADS * NT - 1)
                        nc.vector.reciprocal(rsum[n][:, :, :], rsum[n][:, :, :]).then_inc(rsum_inv.sem, 1)
                        wait(dve, rsum_inv, i, n)
                        wait(dve, values, i, n * HEADS + HEADS - 1)
                        nc.vector.tensor_tensor(
                            on[:, :, 0:D].rearrange("p t (h d) -> p t h d", h=HEADS),
                            O[:, 0:NT * D].rearrange("p (t h d) -> p t h d", t=NT, h=HEADS),
                            rsum[n][:, :, :].rearrange("p t (h o) -> p t h o", o=1).to_broadcast((P, NT, HEADS, HD)), ALU.mult
                        ).then_inc(normed.sem, 1)
                        wait(dve, proj_ps, i, n)
                        dve.wait_ge(res_in[n], i * 16 + 16)
                        dve.wait_ge(stored, i * 32 + 16 * n)
                        nc.vector.scalar_tensor_tensor(hout[:, :], X[0:D, :], par("bproj", 0, D), resid[n][:, :], ALU.add, ALU.add
                                                       ).then_inc(resid_added.sem, 1)

        @block.tensor
        def _(pe):
            prime(nc.tensor, logits, turned, values, kt_ps, k2_ps, feat_ps, ot_ps, proj_ps)
            pe.wait_ge(params_loaded, 16)
            pe.wait_ge(setup_v, 5)
            for c in range(3):
                nc.tensor.matmul(X[:, c * HEADS:(c + 1) * HEADS], par.cols("sel_b", c * P, (c + 1) * P), cw[:, 0, :],
                                 start=True, stop=(c < 2))
            nc.tensor.matmul(X[:, 2 * HEADS:3 * HEADS], par("sel_1"), cw[:, 1, :], start=False, stop=True)
            for c in range(3):
                last = nc.tensor.matmul(X[:, (3 + c) * HEADS:(4 + c) * HEADS], par.cols("sel_c", c * P, (c + 1) * P), cw[:, 0, :],
                                        start=True, stop=True)
            last.then_inc(setup_pe, 1)
            pe.wait_ge(setup_v, 7)

            def keys_turned(i, n):
                k = n % 2
                pe.wait_ge(tok_in[k], i * 16 + 16 * (n // 2 + 1))
                for t in range(TB):
                    last = nc.tensor.transpose(X[:, t * P:(t + 1) * P], tok[k][:, t, 0:2 * D], par("ident"))
                last.then_inc(kt_ps.sem, 1)

            def keys_mapped(i, n):
                k = n % 2
                wait(pe, kt_copied, i, n)
                pe.wait_ge(blk_in[k], i * 16 + 16 * (n // 2 + 1))
                for t in range(TB):
                    last = nc.tensor.matmul(X[:, t * D:(t + 1) * D], kt_sb[D:P, t * P:(t + 1) * P], blk[k][D:P, :], start=True, stop=True)
                last.then_inc(k2_ps.sem, 1)

            def features(i, n, a):
                src, rows = ((fq, widths), (fk, widths), (fk2, quads))[a]
                wait(pe, mono, i, 3 * n + a)
                if a == 0:
                    wait(pe, k2_copied, i, n)
                for c in range(3):
                    if a or c:
                        wait(pe, feat_copied, i, 9 * n + 3 * a + c - 1)
                    for t in range(TB):
                        last = nc.tensor.transpose(X[0:rows[c], t * P:(t + 1) * P], src[:, t, c * P:c * P + rows[c]], par("ident"))
                    last.then_inc(feat_ps.sem, 1)

            def turn(i, g, mt):
                wait(pe, turned_sb, i, g * NT + mt - 2)
                for t in range(NT):
                    last = nc.tensor.transpose(PT[mt % 2][:, t * P:(t + 1) * P], prob[g % 2][:, t, mt * P:(mt + 1) * P], par("ident"))
                last.then_inc(turned.sem, 1)

            pe.wait_ge(ones_set, 1)
            keys_turned(0, 0)
            keys_mapped(0, 0)
            for a in range(3):
                features(0, 0, a)
            with pe.Fori(0, N) as i:
                for g in range(R + 2):
                    n, o = g // HEADS, g % HEADS
                    for half in range(2):
                        if g < R:
                            if half == 0:
                                wait(pe, psi_all, i, g)
                            for t in (2 * half, 2 * half + 1):
                                wait(pe, exps, i, (g - 1) * NT + t)
                                for c in range(3):
                                    last = nc.tensor.matmul(L[t][:, :], fqt[n][0:widths[c], c, t * P:(t + 1) * P],
                                                            psi[g % 2][0:widths[c], c, :], start=(c == 0), stop=(c == 2))
                                last.then_inc(logits.sem, 1)
                        if 1 <= g <= R:
                            if half == 0:
                                wait(pe, exps, i, (g - 1) * NT + NT - 1)
                            for mt in (2 * half, 2 * half + 1):
                                turn(i, g - 1, mt)
                    if g >= 2:
                        v = g - 2
                        wait(pe, turned_sb, i, v * NT + NT - 1)
                        if v % HEADS == 0:
                            wait(pe, normed, i, v // HEADS - 1)
                        for t in range(NT):
                            for mt in range(NT):
                                last = nc.tensor.matmul(O[:, t * D + (v % HEADS) * HD:t * D + (v % HEADS + 1) * HD],
                                                        probt[v % 2][:, mt, t * P:(t + 1) * P],
                                                        tok[v // HEADS][:, mt, 2 * D + (v % HEADS) * HD:2 * D + (v % HEADS + 1) * HD],
                                                        start=(mt == 0), stop=(mt == NT - 1))
                        last.then_inc(values.sem, 1)
                    if g in (HEADS + 1, R + 1):
                        m = g // HEADS - 1
                        wait(pe, normed, i, m)
                        wait(pe, feat_copied, i, 9 * (m + 1) + 8)
                        for t in range(NT):
                            last = nc.tensor.transpose(X[:, t * P:(t + 1) * P], on[:, t, :], par("ident"))
                        last.then_inc(ot_ps.sem, 1)
                        wait(pe, ot_copied, i, m)
                        nc.tensor.matmul(X[:, :], par("wproj"), ot[:, :], start=True, stop=True).then_inc(proj_ps.sem, 1)
                    if g < R:
                        if o == 2:
                            wait(pe, resid_added, i, n - 1)
                            keys_turned(i, n + 1)
                        if o == 3:
                            keys_mapped(i, n + 1)
                        if o in (4, 5, 6):
                            features(i, n + 1, o - 4)



def top2(nc, steps, wait_own, score, ge, gt, mask, tri):
    a = score[:, :, :].rearrange("p n (e o) -> p n e o", o=1).to_broadcast((P, 2 * TB, NE, NE))
    b = score[:, :, :].rearrange("p n (o e) -> p n o e", o=1).to_broadcast((P, 2 * TB, NE, NE))

    def table(t):
        return t.rearrange("p (o e f) -> p o e f", o=1, e=NE).to_broadcast((P, 2 * TB, NE, NE))

    nc.vector.tensor_tensor(ge[:, :, :, :], b, a, ALU.is_ge)
    nc.vector.tensor_tensor(gt[:, :, :, :], b, a, ALU.is_gt).then_inc(steps.mark("compare"), 1)
    wait_own("compare")
    nc.vector.tensor_tensor(ge[:, :, :, :], ge[:, :, :, :], table(tri), ALU.mult).then_inc(steps.mark("lower"), 1)
    wait_own("lower")
    nc.vector.tensor_tensor(ge[:, :, :, :], ge[:, :, :, :], gt[:, :, :, :], ALU.max).then_inc(steps.mark("above"), 1)
    wait_own("above")
    nc.vector.tensor_reduce(mask[:, :, :], ge[:, :, :, :], AX, ALU.add).then_inc(steps.mark("rank"), 1)
    wait_own("rank")
    nc.vector.tensor_scalar(mask[:, :, :], mask[:, :, :], 2.0, None, ALU.is_lt).then_inc(steps.mark("mask"), 1)


def gelu_stage(nc, dram):
    YS = [(q, t) for q in range(2) for t in range(TB)]
    VS = (["norm", "score", "compare", "lower", "above", "rank", "mask"]
          + [x for q, t in YS for x in (f"masked{q}{t}", f"summed{q}{t}")] + ["out"])
    SSN = ["square", "log", "rstd", "maskT"] + [f"gelu{q}{e}" for q in range(2) for e in range(NE)]
    TS = ["center", "var", "score", "maskT"] + [x for q in range(2) for x in
                                               [f"up{q}{e}" for e in range(NE)] + [f"down{q}{t}" for t in range(TB)]] + ["out"]
    with ExitStack() as ctx:
        def sb(name, shape, dt=F32):
            return [ctx.enter_context(nc.sbuf_tensor(f"gelu_{name}{s}", shape, dt)) for s in STREAMS]

        def sem(name):
            return nc.alloc_semaphore(f"gelu_{name}")

        params, par, params_loaded = load_params(nc, ctx, "gelu", dram)
        h, sq, xn = sb("h", [P, T]), sb("sq", [P, T]), sb("xn", [P, T])
        score, mask = sb("score", [P, 2 * TB, NE]), sb("mask", [P, 2 * TB, NE])
        ge, gt = sb("ge", [P, 2 * TB, NE, NE]), sb("gt", [P, 2 * TB, NE, NE])
        maskt = sb("maskt", [NE, 2, T])
        hid = sb("hid", [P, NE, T])
        ym = sb("ym", [P, 2, NE, D])
        z = sb("z", [P, 2, TB, D])
        ho = sb("ho", [P, T])
        ps = [[ctx.enter_context(nc.psum_tensor(f"gelu_ps{s}{k}", [P, T], F32)) for k in range(4)] for s in STREAMS]
        h_in, stored = ([sem(f"{n}{s}") for s in STREAMS] for n in ("h_in", "stored"))
        V = [Steps(sem(f"vector_steps{s}"), VS) for s in STREAMS]
        S = [Steps(sem(f"scalar_steps{s}"), SSN) for s in STREAMS]
        TE = [Steps(sem(f"tensor_steps{s}"), TS) for s in STREAMS]
        block = ctx.enter_context(nc.Block())
        N = PAIRS // 2

        @block.sync
        def _(sp):
            sp.dma_start(params[:, :], dram["params_gelu"]).then_inc(params_loaded, 16)
            with sp.Fori(0, N) as i:
                for s in STREAMS:
                    wait_before(sp, V[s], i, "out")
                    sp.dma_start(h[s][:, :], dram["h1"][bass.ds(i * 2 + s, 1), :, :].rearrange("a p t -> (a p) t")).then_inc(h_in[s], 16)
                for s in STREAMS:
                    wait_now(sp, V[s], i, "out")
                    sp.dma_start(dram["h2"][bass.ds(i * 2 + s, 1), :, :].rearrange("a p t -> (a p) t"), ho[s][:, :]).then_inc(stored[s], 16)
            for s in STREAMS:
                sp.wait_ge(stored[s], 16 * N)

        @block.vector
        def _(dve):
            for s in STREAMS:
                nc.vector.sem_inc(V[s].sem, len(VS))
            dve.wait_ge(params_loaded, 16)
            with dve.Fori(0, N) as i:
                for s in STREAMS:
                    wait_now(dve, S[s], i, "rstd")
                    nc.vector.tensor_tensor(xn[s][:, :], ps[s][0][:, :], sq[s][:, :], ALU.mult).then_inc(V[s].mark("norm"), 1)
                for s in STREAMS:
                    wait_now(dve, TE[s], i, "score")
                    nc.vector.tensor_tensor(score[s][:, :, :], ps[s][1][:, 0:2 * TB * NE].rearrange("p (n e) -> p n e", e=NE),
                                            par("bg").rearrange("p (o e) -> p o e", o=1).to_broadcast((P, 2 * TB, NE)), ALU.add
                                            ).then_inc(V[s].mark("score"), 1)
                for s in STREAMS:
                    wait_now(dve, V[s], i, "score")
                    top2(nc, V[s], lambda name, s=s: wait_now(dve, V[s], i, name), score[s], ge[s], gt[s], mask[s],
                         par("tri"))
                for q, t in YS:
                    for s in STREAMS:
                        wait_now(dve, TE[s], i, f"down{q}{t}")
                        k = q * TB + t
                        if k >= 2:
                            wait_now(dve, V[s], i, "summed%d%d" % YS[k - 2])
                        else:
                            wait_now(dve, V[s], i, "mask")
                        m = mask[s][:, 2 * t + q, :].rearrange("p (e o) -> p e o", o=1).to_broadcast((P, NE, D))
                        nc.vector.tensor_tensor(ym[s][:, t % 2], ps[s][2 + t % 2][:, :].rearrange("p (e d) -> p e d", e=NE), m, ALU.mult
                                                ).then_inc(V[s].mark(f"masked{q}{t}"), 1)
                    for s in STREAMS:
                        wait_now(dve, V[s], i, f"masked{q}{t}")
                        nc.vector.tensor_reduce(z[s][:, q, t, :], ym[s][:, t % 2].rearrange("p e d -> p d e"), AX, ALU.add
                                                ).then_inc(V[s].mark(f"summed{q}{t}"), 1)
                for s in STREAMS:
                    wait_now(dve, TE[s], i, "out")
                    dve.wait_ge(stored[s], i * 16)
                    nc.vector.tensor_tensor(ho[s][:, :], ps[s][0][:, :], h[s][:, :], ALU.add).then_inc(V[s].mark("out"), 1)

        @block.scalar
        def _(act):
            for s in STREAMS:
                nc.scalar.sem_inc(S[s].sem, len(SSN))
            act.wait_ge(params_loaded, 16)
            with act.Fori(0, N) as i:
                for s in STREAMS:
                    wait_now(act, TE[s], i, "center")
                    nc.scalar.activation(sq[s][:, :], ps[s][0][:, :], ACT.Square).then_inc(S[s].mark("square"), 1)
                for s in STREAMS:
                    wait_now(act, TE[s], i, "var")
                    nc.scalar.activation(sq[s][:, :], ps[s][1][:, :], ACT.Ln, bias=par("eps")).then_inc(S[s].mark("log"), 1)
                for s in STREAMS:
                    wait_now(act, S[s], i, "log")
                    nc.scalar.activation(sq[s][:, :], sq[s][:, :], ACT.Exp, scale=-0.5).then_inc(S[s].mark("rstd"), 1)
                for s in STREAMS:
                    wait_now(act, TE[s], i, "maskT")
                    nc.scalar.activation(maskt[s][:, 0, :], ps[s][2][0:NE, :], ACT.Copy)
                    nc.scalar.activation(maskt[s][:, 1, :], ps[s][3][0:NE, :], ACT.Copy).then_inc(S[s].mark("maskT"), 1)
                for q in range(2):
                    for e in range(NE):
                        for s in STREAMS:
                            wait_now(act, TE[s], i, f"up{q}{e}")
                            nc.scalar.activation(hid[s][:, e, :], ps[s][e % 2][:, :], ACT.Gelu, bias=par.cols("b1", e, e + 1)
                                                 ).then_inc(S[s].mark(f"gelu{q}{e}"), 1)

        @block.tensor
        def _(pe):
            for s in STREAMS:
                nc.tensor.sem_inc(TE[s].sem, len(TS))
            pe.wait_ge(params_loaded, 16)
            with pe.Fori(0, N) as i:
                for s in STREAMS:
                    wait_load(pe, h_in[s], i)
                    nc.tensor.matmul(ps[s][0][:, :], par("cen2"), h[s][:, :], start=True, stop=True).then_inc(TE[s].mark("center"), 1)
                for s in STREAMS:
                    wait_now(pe, S[s], i, "square")
                    nc.tensor.matmul(ps[s][1][:, :], par("avg2"), sq[s][:, :], start=True, stop=True).then_inc(TE[s].mark("var"), 1)
                for s in STREAMS:
                    wait_now(pe, V[s], i, "norm")
                    for t in range(TB):
                        last = nc.tensor.matmul(ps[s][1][:, t * 2 * NE:(t + 1) * 2 * NE], xn[s][:, t * P:(t + 1) * P], par("wg"),
                                                start=True, stop=True)
                    last.then_inc(TE[s].mark("score"), 1)
                for s in STREAMS:
                    wait_now(pe, V[s], i, "mask")
                    for q in range(2):
                        for t in range(TB):
                            last = nc.tensor.transpose(ps[s][2 + q][0:NE, t * P:(t + 1) * P], mask[s][:, 2 * t + q, :], par("ident"))
                    last.then_inc(TE[s].mark("maskT"), 1)
                for q in range(2):
                    for e in range(NE):
                        for s in STREAMS:
                            if e >= 2:
                                wait_now(pe, S[s], i, f"gelu{q}{e - 2}")
                            elif q == 1:
                                wait_now(pe, S[s], i, f"gelu0{NE - 2 + e}")
                            nc.tensor.matmul(ps[s][e % 2][:, :], par.cols("w1", e * FH, (e + 1) * FH, D * q, D * (q + 1)),
                                             xn[s][D * q:D * (q + 1), :], start=True, stop=True).then_inc(TE[s].mark(f"up{q}{e}"), 1)
                    for t in range(TB):
                        for s in STREAMS:
                            if t == 0:
                                wait_now(pe, S[s], i, f"gelu{q}{NE - 1}")
                            if t >= 2:
                                wait_now(pe, V[s], i, f"masked{q}{t - 2}")
                            elif q == 1:
                                wait_now(pe, V[s], i, f"masked0{t + 2}")
                            for e in range(NE):
                                last = nc.tensor.matmul(ps[s][2 + t % 2][:, e * D:(e + 1) * D], hid[s][:, e, t * P:(t + 1) * P],
                                                        par.cols("w2", e * D, (e + 1) * D), start=True, stop=True)
                            last.then_inc(TE[s].mark(f"down{q}{t}"), 1)
                for s in STREAMS:
                    wait_now(pe, V[s], i, f"summed1{TB - 1}")
                    for q in range(2):
                        for t in range(TB):
                            nc.tensor.matmul(ps[s][0][D * q:D * (q + 1), t * P:(t + 1) * P], z[s][:, q, t, :], par("ident"), start=True, stop=False)
                            last = nc.tensor.matmul(ps[s][0][D * q:D * (q + 1), t * P:(t + 1) * P], par("b2"), maskt[s][:, q, t * P:(t + 1) * P],
                                                    start=False, stop=True)
                    last.then_inc(TE[s].mark("out"), 1)



def ssm_stage(nc, dram):
    VS = ["norm"] + [f"{x}{q}" for q in range(2) for x in ("cos_part", "sin_part", "rotated", "states")] + ["relu", "out"]
    SSN = ["square", "log", "rstd"]
    TS = ["center", "var", "bu0", "bu1", "y"]
    GS = [f"{x}{q}" for q in range(2) for x in ("back_cos", "back_sin")]
    with ExitStack() as ctx:
        def one(name, shape, dt=F32):
            return ctx.enter_context(nc.sbuf_tensor(f"ssm_{name}", shape, dt))

        def sb(name, shape):
            return [one(f"{name}{s}", shape) for s in STREAMS]

        def sem(name):
            return nc.alloc_semaphore(f"ssm_{name}")

        params, par, params_loaded = load_params(nc, ctx, "ssm", dram)
        cos, sin, decay = one("cos", [P, T]), one("sin", [P, T]), one("decay", [P, T])
        w = one("small", [P, 24])
        bmat, bt = one("bmat", [P, 4, D]), one("bt", [P, 2, P])
        c1, c2 = one("c1", [P, D]), one("c2", [P, D])
        h, sq, xn = sb("h", [P, T]), sb("sq", [P, T]), sb("xn", [P, T])
        za, zb = sb("za", [P, T]), sb("zb", [P, T])
        y = sb("y", [P, 2, T])
        u1, u2 = sb("u1", [P, 2, T]), sb("u2", [P, 2, T])
        ho = sb("ho", [P, T])
        ps = [[ctx.enter_context(nc.psum_tensor(f"ssm_ps{s}{k}", [P, T], F32)) for k in range(4)] for s in STREAMS]
        h_in, stored = ([sem(f"{n}{s}") for s in STREAMS] for n in ("h_in", "stored"))
        V = [Steps(sem(f"vector_steps{s}"), VS) for s in STREAMS]
        S = [Steps(sem(f"scalar_steps{s}"), SSN) for s in STREAMS]
        TE = [Steps(sem(f"tensor_steps{s}"), TS) for s in STREAMS]
        G = [Steps(sem(f"gpsimd_steps{s}"), GS) for s in STREAMS]
        setup_v, setup_s, setup_pe = sem("setup_v"), sem("setup_s"), sem("setup_pe")
        block = ctx.enter_context(nc.Block())
        N = PAIRS // 2

        def c(k):
            return w[:, k:k + 1]

        STEP, RE, R, TH, TC, TS_, CO, SI, LRE, LIM, GRE, GIM, T1, T2, T3, T4 = range(16)
        marks = {}

        @block.sync
        def _(sp):
            sp.dma_start(params[:, :], dram["params_ssm"]).then_inc(params_loaded, 16)
            with sp.Fori(0, N) as i:
                for s in STREAMS:
                    wait_before(sp, V[s], i, "out")
                    sp.dma_start(h[s][:, :], dram["h2"][bass.ds(i * 2 + s, 1), :, :].rearrange("a p t -> (a p) t")).then_inc(h_in[s], 16)
                for s in STREAMS:
                    wait_now(sp, V[s], i, "out")
                    sp.dma_start(dram["h3"][bass.ds(i * 2 + s, 1), :, :].rearrange("a p t -> (a p) t"), ho[s][:, :]).then_inc(stored[s], 16)
            for s in STREAMS:
                sp.wait_ge(stored[s], 16 * N)

        @block.vector
        def _(dve):
            count = [0]

            def then(ins):
                count[0] += 1
                ins.then_inc(setup_v, 1)
                dve.wait_ge(setup_v, count[0])

            def tt(out, a, b, op):
                then(nc.vector.tensor_tensor(out, a, b, op))

            def ts(out, a, x, y, op0, op1):
                then(nc.vector.tensor_scalar(out, a, x, y, op0, op1))

            for s in STREAMS:
                nc.vector.sem_inc(V[s].sem, len(VS))
            dve.wait_ge(params_loaded, 16)
            ts(c(T1), par("lre"), -1.0, None, ALU.mult, ALU.bypass)
            tt(c(RE), par("lre"), c(T1), ALU.min)
            dve.wait_ge(setup_s, 1)
            tt(c(TH), par("lim"), c(STEP), ALU.mult)
            tt(c(T2), c(RE), c(STEP), ALU.mult)
            for at, quarter in ((TS_, 0.0), (TC, float(np.pi / 2))):
                ts(c(T3), c(TH), quarter, float(1 / (2 * np.pi)), ALU.add, ALU.mult)
                ts(c(T3), c(T3), float(1.5 * 2 ** 23), float(-1.5 * 2 ** 23), ALU.add, ALU.add)
                ts(c(T4), c(T3), -6.28125, quarter, ALU.mult, ALU.add)
                tt(c(at), c(TH), c(T4), ALU.add)
                ts(c(T4), c(T3), float(-(2 * np.pi - 6.28125)), None, ALU.mult, ALU.bypass)
                tt(c(at), c(at), c(T4), ALU.add)
                ts(c(at), c(at), 3.1415925, -3.1415925, ALU.min, ALU.max)
            marks["angles"] = count[0]
            dve.wait_ge(setup_s, 4)
            tt(c(LRE), c(R), c(CO), ALU.mult)
            ts(c(LRE), c(LRE), -1.0, None, ALU.add, ALU.bypass)
            tt(c(LIM), c(R), c(SI), ALU.mult)
            tt(c(T1), c(RE), c(RE), ALU.mult)
            tt(c(T2), par("lim"), par("lim"), ALU.mult)
            tt(c(T1), c(T1), c(T2), ALU.add)
            then(nc.vector.reciprocal(c(T1), c(T1)))
            tt(c(T2), c(LRE), c(RE), ALU.mult)
            tt(c(T3), c(LIM), par("lim"), ALU.mult)
            tt(c(GRE), c(T2), c(T3), ALU.add)
            tt(c(GRE), c(GRE), c(T1), ALU.mult)
            tt(c(T2), c(LIM), c(RE), ALU.mult)
            tt(c(T3), c(LRE), par("lim"), ALU.mult)
            tt(c(GIM), c(T2), c(T3), ALU.subtract)
            tt(c(GIM), c(GIM), c(T1), ALU.mult)
            tt(c(T2), c(GIM), par("sgn"), ALU.mult)
            ts(bmat[:, 0, :], par("b_mine"), c(GRE), None, ALU.mult, ALU.bypass)
            ts(bmat[:, 1, :], par("b_other"), c(T2), None, ALU.mult, ALU.bypass)
            tt(bmat[:, 2, :], bmat[:, 0, :], bmat[:, 1, :], ALU.add)
            then(nc.vector.tensor_copy(bmat[:, 3, :], bmat[:, 2, :]))
            marks["bmat"] = count[0]
            dve.wait_ge(setup_pe, 1)
            then(nc.vector.tensor_copy(bt[:, 0, :], ps[0][0][:, 0:P]))
            nc.vector.tensor_copy(bt[:, 1, 0:D], ps[0][0][:, D:P])
            ts(bt[:, 1, D:P], ps[0][0][:, 0:D], -1.0, None, ALU.mult, ALU.bypass)
            ts(c1[:, :], par("c1"), par("neg1"), None, ALU.mult, ALU.bypass)
            ts(c2[:, :], par("c2"), par("neg2"), None, ALU.mult, ALU.bypass)
            then(nc.vector.memset(cos[:, 0:1], 1.0))
            then(nc.vector.memset(sin[:, 0:1], 0.0))
            length = 1
            while length < T:
                lo, hi = slice(0, length), slice(length, 2 * length)
                ts(cos[:, hi], sin[:, lo], c(SI), -1.0, ALU.mult, ALU.mult)
                then(nc.vector.scalar_tensor_tensor(cos[:, hi], cos[:, lo], c(CO), cos[:, hi], ALU.mult, ALU.add))
                ts(sin[:, hi], cos[:, lo], c(SI), None, ALU.mult, ALU.bypass)
                then(nc.vector.scalar_tensor_tensor(sin[:, hi], sin[:, lo], c(CO), sin[:, hi], ALU.mult, ALU.add))
                tt(c(T1), c(CO), c(CO), ALU.mult)
                tt(c(T2), c(SI), c(SI), ALU.mult)
                tt(c(T3), c(CO), c(SI), ALU.mult)
                tt(c(CO), c(T1), c(T2), ALU.subtract)
                ts(c(SI), c(T3), 2.0, None, ALU.mult, ALU.bypass)
                length *= 2
            then(nc.vector.memset(decay[:, :], 1.0))
            ts(decay[:, :], decay[:, :], c(R), None, ALU.mult, ALU.bypass)
            marks["total"] = count[0]
            with dve.Fori(0, N) as i:
                for s in STREAMS:
                    wait_now(dve, S[s], i, "rstd")
                    nc.vector.tensor_tensor(xn[s][:, :], ps[s][0][:, :], sq[s][:, :], ALU.mult).then_inc(V[s].mark("norm"), 1)
                for q in range(2):
                    for s in STREAMS:
                        wait_now(dve, TE[s], i, f"bu{q}")
                        wait_now(dve, V[s], i, "states0") if q else wait_before(dve, V[s], i, "states1")
                        nc.vector.tensor_tensor(za[s][:, :], ps[s][2 * q][:, :], cos[:, :], ALU.mult).then_inc(V[s].mark(f"cos_part{q}"), 1)
                        nc.vector.tensor_tensor(zb[s][:, :], ps[s][2 * q + 1][:, :], sin[:, :], ALU.mult).then_inc(V[s].mark(f"sin_part{q}"), 1)
                    for s in STREAMS:
                        wait_now(dve, V[s], i, f"sin_part{q}")
                        nc.vector.tensor_tensor(zb[s][:, :], za[s][:, :], zb[s][:, :], ALU.add).then_inc(V[s].mark(f"rotated{q}"), 1)
                    for s in STREAMS:
                        wait_now(dve, V[s], i, f"rotated{q}")
                        wait_before(dve, G[s], i, f"back_sin{q}")
                        nc.vector.tensor_tensor_scan(y[s][:, q, :], decay[:, :], zb[s][:, :], 0.0, ALU.mult, ALU.add
                                                     ).then_inc(V[s].mark(f"states{q}"), 1)
                for s in STREAMS:
                    wait_now(dve, TE[s], i, "y")
                    dve.wait_ge(stored[s], i * 16)
                    nc.vector.scalar_tensor_tensor(ho[s][:, :], ps[s][0][:, :], 0.0, xn[s][:, :], ALU.max, ALU.add).then_inc(V[s].mark("relu"), 1)
                for s in STREAMS:
                    wait_now(dve, V[s], i, "relu")
                    nc.vector.tensor_tensor(ho[s][:, :], ho[s][:, :], h[s][:, :], ALU.add).then_inc(V[s].mark("out"), 1)

        @block.gpsimd
        def _(pool):
            for s in STREAMS:
                nc.gpsimd.sem_inc(G[s].sem, len(GS))
            pool.wait_ge(setup_v, marks["total"])
            with pool.Fori(0, N) as i:
                for q in range(2):
                    for s in STREAMS:
                        wait_now(pool, V[s], i, f"states{q}")
                        wait_before(pool, TE[s], i, "y")
                        nc.gpsimd.tensor_tensor(u1[s][:, q, :], y[s][:, q, :], cos[:, :], ALU.mult).then_inc(G[s].mark(f"back_cos{q}"), 1)
                        nc.gpsimd.tensor_tensor(u2[s][:, q, :], y[s][:, q, :], sin[:, :], ALU.mult).then_inc(G[s].mark(f"back_sin{q}"), 1)

        @block.scalar
        def _(act):
            for s in STREAMS:
                nc.scalar.sem_inc(S[s].sem, len(SSN))
            act.wait_ge(params_loaded, 16)
            nc.scalar.activation(c(STEP), par("lstep"), ACT.Exp).then_inc(setup_s, 1)
            act.wait_ge(setup_v, marks["angles"])
            nc.scalar.activation(c(R), c(T2), ACT.Exp).then_inc(setup_s, 1)
            nc.scalar.activation(c(SI), c(TS_), ACT.Sin).then_inc(setup_s, 1)
            nc.scalar.activation(c(CO), c(TC), ACT.Sin).then_inc(setup_s, 1)
            with act.Fori(0, N) as i:
                for s in STREAMS:
                    wait_now(act, TE[s], i, "center")
                    nc.scalar.activation(sq[s][:, :], ps[s][0][:, :], ACT.Square).then_inc(S[s].mark("square"), 1)
                for s in STREAMS:
                    wait_now(act, TE[s], i, "var")
                    nc.scalar.activation(sq[s][:, :], ps[s][1][:, :], ACT.Ln, bias=par("eps")).then_inc(S[s].mark("log"), 1)
                for s in STREAMS:
                    wait_now(act, S[s], i, "log")
                    nc.scalar.activation(sq[s][:, :], sq[s][:, :], ACT.Exp, scale=-0.5).then_inc(S[s].mark("rstd"), 1)

        @block.tensor
        def _(pe):
            for s in STREAMS:
                nc.tensor.sem_inc(TE[s].sem, len(TS))
            pe.wait_ge(params_loaded, 16)
            pe.wait_ge(setup_v, marks["bmat"])
            nc.tensor.transpose(ps[0][0][:, 0:P], bmat[:, 2:4, :].rearrange("p a d -> p (a d)"), par("ident")).then_inc(setup_pe, 1)
            pe.wait_ge(setup_v, marks["total"])
            with pe.Fori(0, N) as i:
                for s in STREAMS:
                    wait_load(pe, h_in[s], i)
                    nc.tensor.matmul(ps[s][0][:, :], par("cen2"), h[s][:, :], start=True, stop=True).then_inc(TE[s].mark("center"), 1)
                for s in STREAMS:
                    wait_now(pe, S[s], i, "square")
                    nc.tensor.matmul(ps[s][1][:, :], par("avg2"), sq[s][:, :], start=True, stop=True).then_inc(TE[s].mark("var"), 1)
                for q in range(2):
                    for s in STREAMS:
                        wait_now(pe, V[s], i, "norm")
                        for k in range(2):
                            last = nc.tensor.matmul(ps[s][2 * q + k][:, :], bt[D * q:D * (q + 1), k, :], xn[s][D * q:D * (q + 1), :], start=True, stop=True)
                        last.then_inc(TE[s].mark(f"bu{q}"), 1)
                for s in STREAMS:
                    wait_now(pe, G[s], i, "back_sin1")
                    for q in range(2):
                        nc.tensor.matmul(ps[s][0][D * q:D * (q + 1), :], c1[:, :], u1[s][:, q, :], start=True, stop=False)
                        last = nc.tensor.matmul(ps[s][0][D * q:D * (q + 1), :], c2[:, :], u2[s][:, q, :], start=False, stop=True)
                    last.then_inc(TE[s].mark("y"), 1)



def causal_stage(nc, dram):
    NPAIR, NSEQ = 2, 4
    R = NSEQ * NH2
    NT = TB
    PREP, POST = 10, 2
    USES = NPAIR * PREP + NSEQ * POST
    starts = (2, 12)
    plan = [[] for _ in range(R + 2)]
    for n in range(NPAIR):
        at = starts[n]
        plan[at].append(("ms", n + 1, 0, 0))
        for q in range(2):
            for half in range(2):
                plan[at + 1 + 2 * q + half] += [("proj", n + 1, q, 2 * half), ("proj", n + 1, q, 2 * half + 1)]
        plan[at + 5].append(("v", n + 1, 0, 0))
    for m in range(NSEQ):
        plan[min(4 * m + 6, R + 1)] += [("turn", m, 0, 0), ("out", m, 0, 0)]
    uses, u = [], 0
    for step in plan:
        uses.append([(u + k, *what) for k, what in enumerate(step)])
        u += len(step)
    assert u == USES
    first = [(k - PREP, *what) for k, what in enumerate(
        [("ms", 0, 0, 0)] + [("proj", 0, q, w) for q in range(2) for w in range(4)] + [("v", 0, 0, 0)])]

    with ExitStack() as ctx:
        def one(name, shape, dt=F32):
            return ctx.enter_context(nc.sbuf_tensor(f"causal_{name}", shape, dt))

        def sb(name, shape):
            return [one(f"{name}{k}", shape) for k in range(2)]

        def sem(name):
            return nc.alloc_semaphore(f"causal_{name}")

        def bank(name):
            return ctx.enter_context(nc.psum_tensor(f"causal_{name}", [P, T], F32))

        params, par, params_loaded = load_params(nc, ctx, "causal", dram)
        h = sb("h", [P, T])
        sq, rs = one("sq", [P, T]), one("rs", [P, T])
        xn = sb("xn", [P, T])
        qt, kt = sb("qt", [P, 2, T]), sb("kt", [P, 2, T])
        rot = sb("rot", [P, T])
        vt = sb("vt", [P, NT, 2, NKV2, HD2])
        prob, probt = sb("prob", [P, NT, T]), sb("probt", [P, NT, T])
        nmax = one("nmax", [P, 2, NT])
        rsum = sb("rsum", [P, NT, NH2])
        on = one("on", [P, NT, 2 * D])
        ot = one("ot", [D, T])
        ho = sb("ho", [P, T])
        lb = [bank(f"logits{k}") for k in range(3)]
        tb_ = [bank(f"turned{k}") for k in range(3)]
        X, values_bank = bank("spare"), bank("values")
        L_TILES, T_TILES, NU = ((3,), (0, 2), (1,)), ((0,), (1, 3), (2,)), 3
        L = [lb[1][:, 3 * P:4 * P], lb[2][:, 0:2 * P], lb[1][:, 0:3 * P], lb[0][:, :]]
        PT = [tb_[0][:, :], tb_[1][:, 0:3 * P], tb_[2][:, 0:2 * P], tb_[1][:, 3 * P:4 * P]]
        O = values_bank[:, 0:2 * P]

        h_in, stored, extra = [sem(f"h_in{k}") for k in range(2)], [sem(f"stored{k}") for k in range(2)], sem("extra_copied")
        cleared, weighted = sem("on_cleared"), sem("weights_normed")

        def count(name, per_round):
            return Count(sem(name), per_round)

        logits, maxes, exps = count("logits", R * NU), count("maxes", R * NU), count("exps", R * NU)
        turned, turned_sb = count("turned", R * NU), count("turned_sb", R * NU)
        values = count("values", R)
        used, read = count("spare_written", USES), count("spare_read", USES)
        squared, logged, rstd, normed_h = (count(n, NPAIR) for n in ("squared", "logged", "rstd", "h_normed"))
        roped = count("roped", NPAIR * 4)
        inverted, weighed = (count(n, NSEQ) for n in ("sums_inverted", "values_normed"))
        block = ctx.enter_context(nc.Block())
        N = PAIRS // NPAIR

        def wait(eng, c, i, j):
            eng.wait_ge(c.sem, c.value(i, j))

        def prime(eng, *counts):
            for c in counts:
                eng.sem_inc(c.sem, c.per_round)

        def last_use(kind, n, q=0, w=0):
            for step in [first] + uses:
                for u, *what in step:
                    if what == [kind, n, q, w]:
                        return u

        @block.sync
        def _(sp):
            sp.dma_start(params[:, :], dram["params_causal"]).then_inc(params_loaded, 16)
            sp.dma_start(dram["x3"][PAIRS], dram["x3"][0]).then_inc(extra, 16)
            sp.dma_start(h[0][:, :], dram["x3"][0]).then_inc(h_in[0], 16)
            sp.wait_ge(extra, 16)
            with sp.Fori(0, N) as i:
                for n in range(NPAIR):
                    wait(sp, read, i, last_use("out", 1) if n else last_use("out", 3) - USES)
                    sp.dma_start(h[(n + 1) % 2][:, :], dram["x3"][bass.ds(i * 2 + n + 1, 1), :, :].rearrange("a p t -> (a p) t")
                                 ).then_inc(h_in[(n + 1) % 2], 16)
                    wait(sp, read, i, last_use("out", 2 * n + 1))
                    sp.dma_start(dram["h4"][bass.ds(i * 2 + n, 1), :, :].rearrange("a p t -> (a p) t"), ho[n][:, :]).then_inc(stored[n], 16)
            for n in range(NPAIR):
                sp.wait_ge(stored[n], 16 * N)

        def landed(eng, i, n):
            eng.wait_ge(h_in[n % 2], i * 16 + 16 * (n // 2 + 1))

        @block.gpsimd
        def _(pool):
            prime(nc.gpsimd, roped)
            nc.gpsimd.memset(on[:, :, D:2 * D], 0.0).then_inc(cleared, 1)

            def add_turned(i, n, q, w):
                dst = (qt, kt)[w // 2][n % 2][:, q, :]
                wait(pool, read, i, last_use("proj", n, q, w))
                nc.gpsimd.tensor_tensor(dst, dst, rot[w // 2][:, :], ALU.add).then_inc(roped.sem, 1)

            for q in range(2):
                for w in (1, 3):
                    add_turned(0, 0, q, w)
            with pool.Fori(0, N) as i:
                for step in uses:
                    for _, kind, n, q, w in step:
                        if kind == "proj" and w % 2:
                            add_turned(i, n, q, w)

        @block.scalar
        def _(act):
            prime(nc.scalar, exps, squared, logged, rstd)
            act.wait_ge(params_loaded, 16)

            def norm(i, n):
                landed(act, i, n)
                wait(act, used, i, last_use("ms", n - 1) if n else -PREP - 1)
                nc.scalar.activation(sq[:, :], h[n % 2][:, :], ACT.Square).then_inc(squared.sem, 1)

            def root(i, n):
                wait(act, read, i, last_use("ms", n))
                nc.scalar.activation(rs[:, :], rs[:, :], ACT.Ln).then_inc(logged.sem, 1)
                wait(act, logged, i, n)
                nc.scalar.activation(rs[:, :], rs[:, :], ACT.Exp, scale=-0.5).then_inc(rstd.sem, 1)

            norm(0, 0)
            root(0, 0)
            with act.Fori(0, N) as i:
                for g in range(R):
                    s = g // NH2
                    for k, n in enumerate((1, 2)):
                        if g == starts[k]:
                            norm(i, n)
                    wait(act, turned, i, (g - 2) * NU + NU - 1)
                    for u, tiles in enumerate(L_TILES):
                        wait(act, maxes, i, g * NU + u)
                        for t in tiles:
                            last = nc.scalar.activation(prob[g % 2][:, t, 0:(t + 1) * P], L[t], ACT.Exp, bias=nmax[:, g % 2, t:t + 1],
                                                        accum_out=rsum[s % 2][:, t, g % NH2:g % NH2 + 1])
                        last.then_inc(exps.sem, 1)
                    for k, n in enumerate((1, 2)):
                        if g == starts[k]:
                            root(i, n)

        @block.vector
        def _(dve):
            prime(nc.vector, maxes, turned_sb, normed_h, inverted, weighed)
            nc.vector.sem_inc(read.sem, USES - PREP)
            dve.wait_ge(params_loaded, 16)
            for k, w in enumerate(("wq", "wqr", "wk", "wkr", "wv")):
                last = nc.vector.tensor_scalar(par(w), par(w), par("ln"), None, ALU.mult)
            last.then_inc(weighted, 1)

            def spare(i, u, kind, n, q, w):
                x = X
                if kind == "ms":
                    wait(dve, used, i, u)
                    wait(dve, normed_h, i, n - 1)
                    nc.vector.tensor_scalar(rs[:, :], x[:, :], par("eps"), None, ALU.add).then_inc(read.sem, 1)
                    wait(dve, rstd, i, n)
                    wait(dve, used, i, last_use("v", n - 1) if n else -PREP - 1)
                    nc.vector.tensor_tensor(xn[n % 2][:, :], h[n % 2][:, :], rs[:, :], ALU.mult).then_inc(normed_h.sem, 1)
                elif kind == "proj":
                    wait(dve, used, i, u)
                    if w % 2 == 0:
                        wait(dve, logits, i, (n - 1) * 2 * NH2 * NU - 1)
                    else:
                        wait(dve, roped, i, n * 4 + q * 2 + w // 2 - 2)
                    dst = (qt, kt)[w // 2][n % 2][:, q, :] if w % 2 == 0 else rot[w // 2][:, :]
                    nc.vector.scalar_tensor_tensor(dst, x[:, :], HD2 ** -0.5 if w < 2 else 1.0, par("sin" if w % 2 else "cos"),
                                                   ALU.mult, ALU.mult).then_inc(read.sem, 1)
                elif kind == "v":
                    wait(dve, used, i, u)
                    wait(dve, values, i, (n - 1) * 8 - 1)
                    nc.vector.tensor_copy(vt[n % 2][:].rearrange("p t q k d -> p (t q k d)"), x[:, 0:NT * D]).then_inc(read.sem, 1)
                elif kind == "turn":
                    wait(dve, used, i, u)
                    nc.vector.tensor_copy(ot[:, :], x[0:D, :]).then_inc(read.sem, 1)
                else:
                    wait(dve, used, i, u)
                    rows = slice(D * (n % 2), D * (n % 2) + D)
                    if n % 2 == 0:
                        dve.wait_ge(stored[n // 2], i * 16)
                    nc.vector.tensor_tensor(ho[n // 2][rows, :], x[rows, :], h[n // 2][rows, :], ALU.add).then_inc(read.sem, 1)

            def values_normed(i, m):
                wait(dve, exps, i, m * NH2 * NU + NH2 * NU - 1)
                nc.vector.reciprocal(rsum[m % 2][:, :, :], rsum[m % 2][:, :, :]).then_inc(inverted.sem, 1)
                wait(dve, inverted, i, m)
                wait(dve, values, i, m * NH2 + NH2 - 1)
                nc.vector.tensor_tensor(on[:, :, 0:D].rearrange("p t (h d) -> p t h d", h=NH2),
                                        O.rearrange("p (t h d) -> p t h d", t=NT, h=NH2),
                                        rsum[m % 2][:, :, :].rearrange("p t (h o) -> p t h o", o=1).to_broadcast((P, NT, NH2, HD2)),
                                        ALU.mult).then_inc(weighed.sem, 1)

            for u, kind, n, q, w in first:
                spare(0, u, kind, n, q, w)
            with dve.Fori(0, N) as i:
                for g in range(R + 2):
                    for u in range(NU):
                        if g < R:
                            wait(dve, logits, i, g * NU + u)
                            wait(dve, exps, i, (g - 2) * NU + u)
                            for t in L_TILES[u]:
                                last = nc.vector.tensor_reduce(nmax[:, g % 2, t:t + 1], L[t], AX, ALU.max, negate=True)
                            last.then_inc(maxes.sem, 1)
                        if 1 <= g <= R:
                            if u == 0:
                                wait(dve, values, i, g - 3)
                            wait(dve, turned, i, (g - 1) * NU + u)
                            for t in T_TILES[u]:
                                last = nc.vector.tensor_copy(probt[(g - 1) % 2][:, t, t * P:T], PT[t])
                            last.then_inc(turned_sb.sem, 1)
                    if (g >= 5 and g % 4 == 1 and g < R) or g == R + 1:
                        values_normed(i, (g - 5) // 4 if g < R else NSEQ - 1)
                    for u, kind, n, q, w in uses[g]:
                        spare(i, u, kind, n, q, w)

        @block.tensor
        def _(pe):
            prime(nc.tensor, logits, turned, values)
            nc.tensor.sem_inc(used.sem, USES - PREP)
            pe.wait_ge(params_loaded, 16)
            pe.wait_ge(weighted, 1)
            pe.wait_ge(cleared, 1)

            def spare(i, u, kind, n, q, w):
                x = X
                wait(pe, read, i, u - 1)
                if kind == "ms":
                    wait(pe, squared, i, n)
                    last = nc.tensor.matmul(x[:, :], par("avg2"), sq[:, :], start=True, stop=True)
                elif kind == "proj":
                    wait(pe, normed_h, i, n)
                    last = nc.tensor.matmul(x[:, :], par(("wq", "wqr", "wk", "wkr")[w], D * q, D * (q + 1)), xn[n % 2][D * q:D * (q + 1), :],
                                            start=True, stop=True)
                elif kind == "v":
                    for t in range(NT):
                        last = nc.tensor.matmul(x[:, t * D:(t + 1) * D], xn[n % 2][:, t * P:(t + 1) * P], par("wv"), start=True, stop=True)
                elif kind == "turn":
                    wait(pe, weighed, i, n)
                    for t in range(NT):
                        last = nc.tensor.transpose(x[:, t * P:(t + 1) * P], on[:, t, :], par("ident"))
                else:
                    last = nc.tensor.matmul(x[:, :], par("wo"), ot[:, :], start=True, stop=True)
                last.then_inc(used.sem, 1)

            for u, kind, n, q, w in first:
                spare(0, u, kind, n, q, w)
            with pe.Fori(0, N) as i:
                for g in range(R + 2):
                    s = g // NH2
                    for u in range(NU):
                        if g < R:
                            if u == 0:
                                wait(pe, roped, i, s * 2 + 1)
                            wait(pe, exps, i, (g - 1) * NU + u)
                            for t in L_TILES[u]:
                                rows = slice(32 * (g % NH2), 32 * (g % NH2) + 32)
                                nc.tensor.matmul(L[t], qt[s // 2][rows, s % 2, t * P:(t + 1) * P], kt[s // 2][rows, s % 2, 0:(t + 1) * P],
                                                 start=True, stop=False)
                                last = nc.tensor.matmul(L[t][:, t * P:(t + 1) * P], par("ident"), par("mask"), start=False, stop=True)
                            last.then_inc(logits.sem, 1)
                        if 1 <= g <= R:
                            if u == 0:
                                wait(pe, exps, i, (g - 1) * NU + NU - 1)
                            wait(pe, turned_sb, i, (g - 2) * NU + u)
                            for mt in T_TILES[u]:
                                for t in range(mt, NT):
                                    last = nc.tensor.transpose(PT[mt][:, (t - mt) * P:(t - mt + 1) * P], prob[(g - 1) % 2][:, t, mt * P:(mt + 1) * P],
                                                               par("ident"))
                            last.then_inc(turned.sem, 1)
                    if g >= 2:
                        v = g - 2
                        wait(pe, turned_sb, i, v * NU + NU - 1)
                        if v % NH2 == 0:
                            wait(pe, weighed, i, v // NH2 - 1)
                        hh, sv = v % NH2, v // NH2
                        for t in range(NT):
                            for mt in range(t + 1):
                                last = nc.tensor.matmul(O[:, t * D + hh * HD2:t * D + (hh + 1) * HD2], probt[v % 2][:, mt, t * P:(t + 1) * P],
                                                        vt[sv // 2][:, mt, sv % 2, hh // 2, :], start=(mt == 0), stop=(mt == t))
                        last.then_inc(values.sem, 1)
                    for u, kind, n, q, w in uses[g]:
                        spare(i, u, kind, n, q, w)



def norm_stage(nc, dram):
    VS, SSN, TS = ["norm"], ["square", "log", "rstd"], ["center", "var"]
    with ExitStack() as ctx:
        def sb(name, shape):
            return [ctx.enter_context(nc.sbuf_tensor(f"norm_{name}{s}", shape, F32)) for s in STREAMS]

        def sem(name):
            return nc.alloc_semaphore(f"norm_{name}")

        params, par, params_loaded = load_params(nc, ctx, "norm", dram)
        h, sq, xn = sb("h", [P, T]), sb("sq", [P, T]), sb("xn", [P, T])
        ps = [[ctx.enter_context(nc.psum_tensor(f"norm_ps{s}{k}", [P, T], F32)) for k in range(2)] for s in STREAMS]
        h_in, stored = ([sem(f"{n}{s}") for s in STREAMS] for n in ("h_in", "stored"))
        V = [Steps(sem(f"vector_steps{s}"), VS) for s in STREAMS]
        S = [Steps(sem(f"scalar_steps{s}"), SSN) for s in STREAMS]
        TE = [Steps(sem(f"tensor_steps{s}"), TS) for s in STREAMS]
        block = ctx.enter_context(nc.Block())
        N = PAIRS // 2

        @block.sync
        def _(sp):
            sp.dma_start(params[:, :], dram["params_norm"]).then_inc(params_loaded, 16)
            with sp.Fori(0, N) as i:
                for s in STREAMS:
                    wait_before(sp, TE[s], i, "center")
                    sp.dma_start(h[s][:, :], dram["h3"][bass.ds(i * 2 + s, 1), :, :].rearrange("a p t -> (a p) t")).then_inc(h_in[s], 16)
                for s in STREAMS:
                    wait_now(sp, V[s], i, "norm")
                    sp.dma_start(dram["x3"][bass.ds(i * 2 + s, 1), :, :].rearrange("a p t -> (a p) t"), xn[s][:, :]).then_inc(stored[s], 16)
            for s in STREAMS:
                sp.wait_ge(stored[s], 16 * N)

        @block.vector
        def _(dve):
            for s in STREAMS:
                nc.vector.sem_inc(V[s].sem, len(VS))
            with dve.Fori(0, N) as i:
                for s in STREAMS:
                    wait_now(dve, S[s], i, "rstd")
                    dve.wait_ge(stored[s], i * 16)
                    nc.vector.tensor_tensor(xn[s][:, :], ps[s][0][:, :], sq[s][:, :], ALU.mult).then_inc(V[s].mark("norm"), 1)

        @block.scalar
        def _(act):
            for s in STREAMS:
                nc.scalar.sem_inc(S[s].sem, len(SSN))
            act.wait_ge(params_loaded, 16)
            with act.Fori(0, N) as i:
                for s in STREAMS:
                    wait_now(act, TE[s], i, "center")
                    nc.scalar.activation(sq[s][:, :], ps[s][0][:, :], ACT.Square).then_inc(S[s].mark("square"), 1)
                for s in STREAMS:
                    wait_now(act, TE[s], i, "var")
                    nc.scalar.activation(sq[s][:, :], ps[s][1][:, :], ACT.Ln, bias=par("eps")).then_inc(S[s].mark("log"), 1)
                for s in STREAMS:
                    wait_now(act, S[s], i, "log")
                    nc.scalar.activation(sq[s][:, :], sq[s][:, :], ACT.Exp, scale=-0.5).then_inc(S[s].mark("rstd"), 1)

        @block.tensor
        def _(pe):
            for s in STREAMS:
                nc.tensor.sem_inc(TE[s].sem, len(TS))
            pe.wait_ge(params_loaded, 16)
            with pe.Fori(0, N) as i:
                for s in STREAMS:
                    wait_load(pe, h_in[s], i)
                    wait_before(pe, V[s], i, "norm")
                    nc.tensor.matmul(ps[s][0][:, :], par("cen2"), h[s][:, :], start=True, stop=True).then_inc(TE[s].mark("center"), 1)
                for s in STREAMS:
                    wait_now(pe, S[s], i, "square")
                    nc.tensor.matmul(ps[s][1][:, :], par("avg2"), sq[s][:, :], start=True, stop=True).then_inc(TE[s].mark("var"), 1)



def swiglu_stage(nc, dram):
    NT = NE + NE // 2
    QT = [(q, t) for q in range(2) for t in range(TB)]
    VS = (["norm", "max", "shift", "sum", "invert", "probs", "compare", "lower", "above", "rank", "mask", "picked",
           "total", "guarded", "inverse", "weights", "both"]
          + [x for q in range(2) for x in [f"hidden{q}_{k}" for k in range(NT)]
             + [f"{a}{q}{t}" for t in range(TB) for a in ("weighed", "summed")]] + ["out"])
    SSN = ["square", "log", "rstd", "exp"] + [f"silu{q}_{k}" for q in range(2) for k in range(NT)]
    TS = ["ms", "score"] + [x for q in range(2) for x in
                            [f"up{q}_{k}" for k in range(NT)] + [f"down{q}{t}" for t in range(TB)]] + ["turn"]
    with ExitStack() as ctx:
        def sb(name, shape, dt=F32):
            return [ctx.enter_context(nc.sbuf_tensor(f"swiglu_{name}{s}", shape, dt)) for s in STREAMS]

        def sem(name):
            return nc.alloc_semaphore(f"swiglu_{name}")

        params, par, params_loaded = load_params(nc, ctx, "swiglu", dram)
        h, x = sb("h", [P, T]), sb("x", [P, T])
        sq, xn = sb("sq", [P, T]), sb("xn", [P, T])
        N8 = 2 * TB
        score, prob, mask = sb("score", [P, N8, NE]), sb("prob", [P, N8, NE]), sb("mask", [P, N8, NE])
        pick, small = sb("pick", [P, N8, NE]), sb("small", [P, 3, N8])
        ge, gt = sb("ge", [P, N8, NE, NE]), sb("gt", [P, N8, NE, NE])
        gate, hid = sb("gate", [P, T]), sb("hid", [P, NT, T])
        ym, z, o = sb("ym", [P, 2, NE, D]), sb("z", [P, TB, 2, D]), sb("o", [P, TB, 2, D])
        ps = [[ctx.enter_context(nc.psum_tensor(f"swiglu_ps{s}{k}", [P, T], F32)) for k in range(4)] for s in STREAMS]
        in_h, in_x, stored = ([sem(f"{n}{s}") for s in STREAMS] for n in ("h_in", "x_in", "stored"))
        scaled = sem("weights_scaled")
        V = [Steps(sem(f"vector_steps{s}"), VS) for s in STREAMS]
        S = [Steps(sem(f"scalar_steps{s}"), SSN) for s in STREAMS]
        TE = [Steps(sem(f"tensor_steps{s}"), TS) for s in STREAMS]
        block = ctx.enter_context(nc.Block())
        N = PAIRS // 2

        @block.sync
        def _(sp):
            sp.dma_start(params[:, :], dram["params_swiglu"]).then_inc(params_loaded, 16)
            with sp.Fori(0, N) as i:
                for s in STREAMS:
                    wait_before(sp, TE[s], i, "turn")
                    sp.dma_start(x[s][:, :], dram["h4"][bass.ds(i * 2 + s, 1), :, :].rearrange("a p t -> (a p) t")).then_inc(in_x[s], 16)
                    sp.dma_start(h[s][:, :], dram["h3"][bass.ds(i * 2 + s, 1), :, :].rearrange("a p t -> (a p) t")).then_inc(in_h[s], 16)
                for s in STREAMS:
                    wait_now(sp, V[s], i, "out")
                    for q in range(2):
                        sp.dma_start(dram["out"][bass.ds(i * 4 + 2 * s + q, 1), :, :].rearrange("a (t p) d -> (a p) t d", p=P), o[s][:, :, q, :]
                                     ).then_inc(stored[s], 16)
            for s in STREAMS:
                sp.wait_ge(stored[s], 32 * N)

        @block.vector
        def _(dve):
            for s in STREAMS:
                nc.vector.sem_inc(V[s].sem, len(VS))
            dve.wait_ge(params_loaded, 16)
            for name in ("router", "w1", "w3"):
                last = nc.vector.tensor_scalar(par(name), par(name), par("ln"), None, ALU.mult)
            last.then_inc(scaled, 1)
            with dve.Fori(0, N) as i:
                def each(name, op, *waits):
                    for s in STREAMS:
                        for steps, what in waits:
                            wait_now(dve, steps[s], i, what)
                        op(s).then_inc(V[s].mark(name), 1)

                def over(a):
                    return a.rearrange("p (n o) -> p n o", o=1).to_broadcast((P, N8, NE))

                tt, red = nc.vector.tensor_tensor, nc.vector.tensor_reduce
                each("norm", lambda s: tt(xn[s][:, :], x[s][:, :], sq[s][:, :], ALU.mult), (S, "rstd"))

                def logits(s):
                    return ps[s][1][:, 0:N8 * NE].rearrange("p (n e) -> p n e", e=NE)

                each("max", lambda s: red(small[s][:, 0, :], logits(s), AX, ALU.max), (TE, "score"))
                each("shift", lambda s: tt(score[s][:, :, :], logits(s), over(small[s][:, 0, :]), ALU.subtract), (V, "max"))
                each("sum", lambda s: red(small[s][:, 1, :], prob[s][:, :, :], AX, ALU.add), (S, "exp"))
                each("invert", lambda s: nc.vector.reciprocal(small[s][:, 1, :], small[s][:, 1, :]), (V, "sum"))
                each("probs", lambda s: tt(score[s][:, :, :], prob[s][:, :, :], over(small[s][:, 1, :]), ALU.mult), (V, "invert"))
                for s in STREAMS:
                    wait_now(dve, V[s], i, "probs")
                    top2(nc, V[s], lambda name, s=s: wait_now(dve, V[s], i, name), score[s], ge[s], gt[s], mask[s], par("tri"))
                each("picked", lambda s: tt(pick[s][:, :, :], score[s][:, :, :], mask[s][:, :, :], ALU.mult), (V, "mask"))
                each("total", lambda s: red(small[s][:, 2, :], pick[s][:, :, :], AX, ALU.add), (V, "picked"))
                each("guarded", lambda s: nc.vector.tensor_scalar(small[s][:, 2, :], small[s][:, 2, :], 1e-9, None, ALU.add), (V, "total"))
                each("inverse", lambda s: nc.vector.reciprocal(small[s][:, 2, :], small[s][:, 2, :]), (V, "guarded"))
                each("weights", lambda s: tt(mask[s][:, :, :], pick[s][:, :, :], over(small[s][:, 2, :]), ALU.mult), (V, "inverse"))
                for s in STREAMS:
                    wait_load(dve, in_h[s], i)
                each("both", lambda s: tt(h[s][:, :], h[s][:, :], x[s][:, :], ALU.add))
                for q in range(2):
                    for k in range(NT):
                        each(f"hidden{q}_{k}", lambda s: tt(hid[s][:, k, :], ps[s][1][:, :], gate[s][:, :], ALU.mult),
                             (S, f"silu{q}_{k}"), *([(TE, f"down0{TB - 1}")] if (q, k) == (1, 0) else []))
                    for t in range(TB):
                        before = QT[q * TB + t - 2] if q * TB + t >= 2 else None
                        each(f"weighed{q}{t}", lambda s: tt(
                            ym[s][:, t % 2], ps[s][2 + t % 2][:, :].rearrange("p (e d) -> p e d", e=NE),
                            mask[s][:, 2 * t + q, :].rearrange("p (e o) -> p e o", o=1).to_broadcast((P, NE, D)), ALU.mult),
                            (TE, f"down{q}{t}"), (V, "summed%d%d" % before if before else "weights"))
                        each(f"summed{q}{t}", lambda s: red(z[s][:, t, q, :], ym[s][:, t % 2].rearrange("p e d -> p d e"), AX, ALU.add),
                             (V, f"weighed{q}{t}"))
                for s in STREAMS:
                    wait_now(dve, TE[s], i, "turn")
                    wait_now(dve, V[s], i, f"summed1{TB - 1}")
                    dve.wait_ge(stored[s], i * 32)
                    tt(o[s][:].rearrange("p t q d -> p (t q d)"), ps[s][0][:, :], z[s][:].rearrange("p t q d -> p (t q d)"), ALU.add
                       ).then_inc(V[s].mark("out"), 1)

        @block.scalar
        def _(act):
            for s in STREAMS:
                nc.scalar.sem_inc(S[s].sem, len(SSN))
            act.wait_ge(params_loaded, 16)
            with act.Fori(0, N) as i:
                for s in STREAMS:
                    wait_load(act, in_x[s], i)
                    nc.scalar.activation(sq[s][:, :], x[s][:, :], ACT.Square).then_inc(S[s].mark("square"), 1)
                for s in STREAMS:
                    wait_now(act, TE[s], i, "ms")
                    nc.scalar.activation(sq[s][:, :], ps[s][0][:, :], ACT.Ln, bias=par("eps")).then_inc(S[s].mark("log"), 1)
                for s in STREAMS:
                    wait_now(act, S[s], i, "log")
                    nc.scalar.activation(sq[s][:, :], sq[s][:, :], ACT.Exp, scale=-0.5).then_inc(S[s].mark("rstd"), 1)
                for s in STREAMS:
                    wait_now(act, V[s], i, "shift")
                    nc.scalar.activation(prob[s][:, :, :], score[s][:, :, :], ACT.Exp).then_inc(S[s].mark("exp"), 1)
                for q in range(2):
                    for k in range(NT):
                        for s in STREAMS:
                            wait_now(act, TE[s], i, f"up{q}_{k}")
                            nc.scalar.activation(gate[s][:, :], ps[s][0][:, :], ACT.Silu).then_inc(S[s].mark(f"silu{q}_{k}"), 1)

        @block.tensor
        def _(pe):
            for s in STREAMS:
                nc.tensor.sem_inc(TE[s].sem, len(TS))
            pe.wait_ge(params_loaded, 16)
            pe.wait_ge(scaled, 1)
            with pe.Fori(0, N) as i:
                for s in STREAMS:
                    wait_now(pe, S[s], i, "square")
                    wait_before(pe, V[s], i, "out")
                    nc.tensor.matmul(ps[s][0][:, :], par("avg2"), sq[s][:, :], start=True, stop=True).then_inc(TE[s].mark("ms"), 1)
                for s in STREAMS:
                    wait_now(pe, V[s], i, "norm")
                    for t in range(TB):
                        last = nc.tensor.matmul(ps[s][1][:, t * 2 * NE:(t + 1) * 2 * NE], xn[s][:, t * P:(t + 1) * P], par("router"),
                                                start=True, stop=True)
                    last.then_inc(TE[s].mark("score"), 1)
                for q in range(2):
                    rows = slice(D * q, D * (q + 1))
                    for k in range(NT):
                        for s in STREAMS:
                            wait_now(pe, V[s], i, f"hidden{q}_{k - 1}" if k else "shift" if q == 0 else f"hidden0_{NT - 1}")
                            for w, bank in (("w1", 0), ("w3", 1)):
                                last = nc.tensor.matmul(ps[s][bank][:, :], par.cols(w, k * P, (k + 1) * P, rows.start, rows.stop),
                                                        xn[s][rows, :], start=True, stop=True)
                            last.then_inc(TE[s].mark(f"up{q}_{k}"), 1)
                    for t in range(TB):
                        for s in STREAMS:
                            if t == 0:
                                wait_now(pe, V[s], i, f"hidden{q}_{NT - 1}")
                            elif t >= 2:
                                wait_now(pe, V[s], i, f"weighed{q}{t - 2}")
                            for j in range(NE // 2):
                                cols = slice(t * P, (t + 1) * P)
                                nc.tensor.matmul(ps[s][2 + t % 2][:, 2 * j * D:2 * (j + 1) * D], hid[s][:, NE + j, cols],
                                                 par.cols("w2r", 2 * j * D, 2 * (j + 1) * D), start=True, stop=False)
                                for e in (2 * j, 2 * j + 1):
                                    last = nc.tensor.matmul(ps[s][2 + t % 2][:, e * D:(e + 1) * D], hid[s][:, e, cols],
                                                            par.cols("w2", e * D, (e + 1) * D), start=False, stop=e % 2 == 1)
                            last.then_inc(TE[s].mark(f"down{q}{t}"), 1)
                for s in STREAMS:
                    wait_now(pe, V[s], i, f"hidden1_{NT - 1}")
                    for t in range(TB):
                        last = nc.tensor.transpose(ps[s][0][:, t * P:(t + 1) * P], h[s][:, t * P:(t + 1) * P], par("ident"))
                    last.then_inc(TE[s].mark("turn"), 1)


def build(nc, dram, run=None):
    scratch = {"match": (B, len(MATCH), T), "h0": (PAIRS, P, T), "h1": (PAIRS, P, T), "h2": (PAIRS, P, T),
               "h3": (PAIRS, P, T), "x3": (PAIRS + 1, P, T), "h4": (PAIRS, P, T), "tokens": (B + 1, P, TB, 3 * D), "gram": (B, P, P),
               "blocks": (B + 1, D, D)}
    for name, shape in scratch.items():
        if name not in dram:
            dram[name] = nc.dram_tensor(name, shape, F32, kind="Internal").ap()
    dram["index"] = nc.dram_tensor("index_rows", (P, PAIRS * NSCALE * TB * 2), I32, kind="Internal").ap()
    for stage in (hash_stage, token_stage, qkv_stage, qr_stage, attention_stage, gelu_stage, ssm_stage, norm_stage,
                  causal_stage, swiglu_stage):
        if run is None or stage.__name__ in run:
            with nc.cleanup_on_exit():
                stage(nc, dram)



def pad_rows(a, rows=P):
    out = np.zeros((rows, a.shape[1]), np.float32)
    out[:a.shape[0]] = a
    return out


def col(a):
    return a.reshape(-1, 1)


def two(a):
    return np.concatenate([a, a], axis=0)


def apart(a):
    zero = np.zeros_like(a)
    return np.concatenate([np.concatenate([a, zero], axis=1), np.concatenate([zero, a], axis=1)])


def rows_of(a, n=P):
    return np.broadcast_to(a.reshape(1, -1), (n, a.size))


def cols_of(a):
    return a.transpose(1, 0, 2).reshape(a.shape[1], -1)


def feature_rows():
    quad_b, quad_c, const = np.zeros((24, 3 * P)), np.zeros((24, 3 * P)), np.zeros((24, P))
    for h in range(HEADS):
        for m, (i, j) in enumerate(mono_pairs()):
            quad_b[HEADS + h, h * MONO + m] = 1 if i == j else 2
            quad_c[2 * HEADS + h, h * MONO + m] = 1 if i == j else 2
        quad_b[h, NQUAD + h * HD:NQUAD + (h + 1) * HD] = 1
    const[:, NFEAT - 1 - 2 * P] = 1
    return quad_b.astype(np.float32), quad_c.astype(np.float32), const.astype(np.float32)


def rope_tables():
    inv_freq = 1.0 / 10000.0 ** (np.arange(0, HD2, 2, dtype=np.float32) / HD2)
    freqs = np.outer(np.arange(T, dtype=np.float32), inv_freq)
    emb = np.concatenate([freqs, freqs], axis=-1).T
    sign = np.where(np.arange(HD2) < HD2 // 2, -1, 1)[:, None]
    cos, sin = np.zeros((P, T), np.float32), np.zeros((P, T), np.float32)
    for h in range(NH2):
        cos[32 * h:32 * h + HD2] = np.cos(emb)
        sin[32 * h:32 * h + HD2] = np.sin(emb) * sign
    return cos, sin


def heads_apart(w, rep, turned):
    out = np.zeros((D, P), np.float32)
    for h in range(NH2):
        rows = w[(h // rep) * HD2:(h // rep + 1) * HD2]
        if turned:
            rows = np.concatenate([rows[HD2 // 2:], rows[:HD2 // 2]], axis=0)
        out[:, 32 * h:32 * h + HD2] = rows.T
    return out


def hidden_tiles(w):
    out = np.zeros((D, 12, P), np.float32)
    for e in range(NE):
        out[:, e] = w[e, :P].T
        out[:, NE + e // 2, 64 * (e % 2):64 * (e % 2) + REST] = w[e, P:].T
    return out.reshape(D, 12 * P)


def lay_out(a):
    t = {k[7:]: v for k, v in a.items() if k.startswith("L0_tok_")}
    n = {k[8:]: v for k, v in a.items() if k.startswith("L0_attn_")}
    g = {k[7:]: v for k, v in a.items() if k.startswith("L0_ffn_")}
    s = {k[8:]: v for k, v in a.items() if k.startswith("L1_attn_")}
    m = {k[7:]: v for k, v in a.items() if k.startswith("L1_ffn_")}
    eye = np.eye(P, dtype=np.float32)
    halves = np.kron(np.eye(2), np.ones((D, D))).astype(np.float32)
    quad_b, quad_c, const = feature_rows()
    cos, sin = rope_tables()
    start = np.broadcast_to((np.arange(T) % CHUNK == 0).astype(np.float32), (2 * SS, T))
    tri = np.broadcast_to((np.arange(NE)[:, None] > np.arange(NE)[None]).astype(np.float32).reshape(1, -1), (P, NE * NE))
    rest = np.zeros((P, NE, D), np.float32)
    for e in range(NE):
        rest[64 * (e % 2):64 * (e % 2) + REST, e] = m["w2"][e, :, P:].T
    eps5 = np.full((P, 1), 1e-5, np.float32)
    half = np.where(np.arange(P)[:, None] < D, 1, -1).astype(np.float32)
    parts = {
        "token": dict(
            embT=np.concatenate([t["emb_byte"].T, t["emb_byte"].T], axis=1), wq=t["Wq"], bq=rows_of(t["bq"]),
            win_e=t["Win"][:D], w1a=two(t["Win"][D:2 * D]), w1b=two(t["Win"][D:2 * D]), wmf=t["Win"][2 * D:],
            b_in=col(t["b_in"]), wg=t["Wg"], wi=t["Wi"], bg=two(col(t["bg"])), bi=two(col(t["bi"])),
            woT=np.concatenate([t["Wo"].T, t["Wo"].T], axis=1), bo=col(t["bo"]), ln_g=col(t["ln_g"]),
            ln_b=col(t["ln_b"]), mlp_w=cols_of(t["mlp_w"]), mlp_b=t["mlp_b"].T, wout=t["Wout"],
            bout=two(col(t["bout"])), conv_w=two(t["conv_w"].reshape(D, 4)), conv_b=two(col(t["conv_b"])),
            cen=eye - np.float32(1 / H), avg=np.full((P, P), 1 / H, np.float32), ident=eye,
            iota=two(col(np.arange(VOCAB, dtype=np.float32))), first=start, rest=1 - start, eps=eps5),
        "qkv": dict(cen2=eye - halves / D, avg2=halves / D, wqkv=two(n["w_qkv"].T), bqkv=rows_of(n["b_qkv"]),
                    eps=eps5),
        "qr": dict(eye=rows_of(np.tile(np.eye(HD, dtype=np.float32), (4, 1)))),
        "attn": dict(
            ident=eye, convT=n["conv_w"].T, gamma=col(n["bn_gamma"]), beta=col(n["bn_beta"]),
            mean=col(n["bn_mean"]), var=col(n["bn_var"]),
            scales=col(np.concatenate([np.broadcast_to(n[k].reshape(1), (HEADS,)) for k in
                                       ("scale", "riem_scale", "grassman_scale")])),
            conv_b=rows_of(n["conv_b"]), sel_b=quad_b, sel_c=quad_c, sel_1=const,
            last=col(np.arange(P) == NFEAT - 1 - 2 * P).astype(np.float32),
            wproj=np.concatenate([n["w_proj"].T, n["w_proj"].T], axis=1), bproj=two(col(n["b_proj"])),
            eps=eps5[:24]),
        "gelu": dict(cen2=eye - halves / D, avg2=halves / D, ident=eye, wg=apart(g["Wg"]), bg=rows_of(g["bg"]),
                     w1=two(cols_of(g["W1"])), b1=g["b1"].T, w2=cols_of(g["W2"]), b2=g["b2"], tri=tri, eps=eps5),
        "ssm": dict(
            cen2=eye - halves / D, avg2=halves / D, lre=two(col(s["Lambda_re"])), lim=two(col(s["Lambda_im"])),
            lstep=two(col(s["log_step"])), b_mine=np.concatenate([s["B_re"], s["B_im"]]),
            b_other=np.concatenate([s["B_im"], s["B_re"]]), sgn=-half,
            c1=np.concatenate([s["C_re"].T, s["C_im"].T]), c2=np.concatenate([s["C_im"].T, s["C_re"].T]),
            neg1=half, neg2=-np.ones((P, 1), np.float32), ident=eye, eps=eps5),
        "norm": dict(cen2=eye - halves / D, avg2=halves / D, eps=eps5),
        "causal": dict(
            avg2=halves / D, ident=eye, ln=two(col(m["ln1_w"])), wq=two(heads_apart(m["wq"], 1, False)),
            wqr=two(heads_apart(m["wq"], 1, True)), wk=two(heads_apart(m["wk"], 2, False)),
            wkr=two(heads_apart(m["wk"], 2, True)), wv=apart(m["wv"].T),
            wo=np.concatenate([m["wo"].T, m["wo"].T], axis=1), cos=cos, sin=sin,
            mask=np.where(np.arange(P)[:, None] >= np.arange(P)[None], 0, -1e30).astype(np.float32),
            eps=np.full((P, 1), 1e-6, np.float32)),
        "swiglu": dict(avg2=halves / D, ident=eye, ln=two(col(m["ln2_w"])), router=apart(m["router_w"].T),
                       w1=two(hidden_tiles(m["w1"])), w3=two(hidden_tiles(m["w3"])),
                       w2=cols_of(m["w2"][:, :, :P].transpose(0, 2, 1)), w2r=rest.reshape(P, NE * D),
                       tri=tri, eps=np.full((P, 1), 1e-6, np.float32)),
    }
    out = {}
    for stage in STAGES:
        where, width = spec(stage)
        whole = np.zeros((P, width), np.float32)
        assert set(where) == set(parts[stage]), (stage, set(where) ^ set(parts[stage]))
        for name, (rows, at, cols) in where.items():
            part = parts[stage][name]
            assert part.shape == (rows, cols), (name, part.shape, rows, cols)
            whole[:rows, at:at + cols] = part
        out[f"params_{stage}"] = whole
    out["x"] = a["x"]
    out["hash_tables"] = t["hash_tables"].reshape(NSCALE * HASH_MOD, D)
    return out


def kernel(**inputs):
    import concourse.bacc as bacc
    from concourse.bass_utils import run_bass_kernel_spmd

    arrays = {k: np.ascontiguousarray(v) for k, v in lay_out({k: np.asarray(v) for k, v in inputs.items()}).items()}
    nc = bacc.Bacc("TRN2", target_bir_lowering=False, num_devices=1)
    dram = {k: nc.dram_tensor(k, v.shape, mybir.dt.from_np(v.dtype), kind="ExternalInput").ap() for k, v in arrays.items()}
    dram["out"] = nc.dram_tensor("out", (B, T, D), F32, kind="ExternalOutput").ap()
    build(nc, dram)
    result = run_bass_kernel_spmd(nc, [arrays], core_ids=[0])
    return result.results[0]["out"]
```

```python
from contextlib import ExitStack

import numpy as np

import concourse.bass as bass
from concourse import mybir

F32 = mybir.dt.float32
F32R = mybir.dt.float32r
I32 = mybir.dt.int32
U32 = mybir.dt.uint32
ALU = mybir.AluOpType
ACT = mybir.ActivationFunctionType
AX = mybir.AxisListType.X

P = 128
B = 32
T = 512
D = 64
TB = T // P
PAIRS = B // 2
STREAMS = (0, 1)
VOCAB = 64
NSCALE = 4
HASH_MOD = 1024
MATCH = (1, 2, 4, 8)
H = 128
SS = 32
CHUNK = 32
NMLP = 3
HEADS = 8
HD = D // HEADS
MONO = HD * (HD + 1) // 2
NQUAD = HEADS * MONO
NFEAT = NQUAD + D + 1
NE = 8
FH = 128
NH2, NKV2, HD2 = 4, 2, 16
HID = int(8 / 3 * D)
REST = HID - P



class Steps:

    def __init__(self, sem, names):
        self.sem, self.names, self.at = sem, names, 0

    def mark(self, name):
        assert self.names[self.at % len(self.names)] == name, (name, self.names[self.at % len(self.names)])
        self.at += 1
        return self.sem

    def now(self, i, name):
        return (i + 1) * len(self.names) + self.names.index(name) + 1

    def before(self, i, name):
        return i * len(self.names) + self.names.index(name) + 1


def wait_now(eng, steps, i, name):
    eng.wait_ge(steps.sem, steps.now(i, name))


def wait_before(eng, steps, i, name):
    eng.wait_ge(steps.sem, steps.before(i, name))


def wait_load(eng, sem, i, count=1):
    eng.wait_ge(sem, i * (16 * count) + 16 * count)



def mono_pairs():
    return [(i, i + r) for r in range(HD) for i in range(HD - r)]


def spec(stage):
    s = {
        "token": [("embT", D, P), ("wq", D, D), ("bq", P, D), ("win_e", D, H), ("w1a", P, H), ("w1b", P, H),
                  ("wmf", P, H), ("b_in", H, 1), ("wg", H, SS), ("wi", H, SS), ("bg", 2 * SS, 1),
                  ("bi", 2 * SS, 1), ("woT", H, 2 * SS), ("bo", H, 1), ("ln_g", H, 1), ("ln_b", H, 1),
                  ("mlp_w", H, NMLP * H), ("mlp_b", H, NMLP), ("wout", H, D), ("bout", P, 1),
                  ("conv_w", P, 4), ("conv_b", P, 1), ("cen", P, P), ("avg", P, P), ("ident", P, P),
                  ("iota", P, 1), ("first", 2 * SS, T), ("rest", 2 * SS, T), ("eps", P, 1)],
        "qkv": [("cen2", P, P), ("avg2", P, P), ("wqkv", P, 3 * D), ("bqkv", P, 3 * D), ("eps", P, 1)],
        "qr": [("eye", P, 4 * HD * HD)],
        "attn": [("ident", P, P), ("convT", 3 * HEADS, HEADS), ("gamma", 3 * HEADS, 1), ("beta", 3 * HEADS, 1),
                 ("mean", 3 * HEADS, 1), ("var", 3 * HEADS, 1), ("scales", 3 * HEADS, 1),
                 ("conv_b", P, HEADS), ("sel_b", 3 * HEADS, 3 * P), ("sel_c", 3 * HEADS, 3 * P),
                 ("sel_1", 3 * HEADS, P), ("last", P, 1), ("wproj", P, P), ("bproj", P, 1),
                 ("eps", 3 * HEADS, 1)],
        "gelu": [("cen2", P, P), ("avg2", P, P), ("ident", P, P), ("wg", P, 2 * NE), ("bg", P, NE),
                 ("w1", P, NE * FH), ("b1", FH, NE), ("w2", FH, NE * P), ("b2", P, D), ("tri", P, NE * NE),
                 ("eps", P, 1)],
        "ssm": [("cen2", P, P), ("avg2", P, P), ("lre", P, 1), ("lim", P, 1), ("lstep", P, 1), ("b_mine", P, D),
                ("b_other", P, D), ("sgn", P, 1), ("c1", P, D), ("c2", P, D), ("neg1", P, 1), ("neg2", P, 1),
                ("ident", P, P), ("eps", P, 1)],
        "norm": [("cen2", P, P), ("avg2", P, P), ("eps", P, 1)],
        "causal": [("avg2", P, P), ("ident", P, P), ("ln", P, 1), ("wq", P, P), ("wqr", P, P), ("wk", P, P),
                   ("wkr", P, P), ("wv", P, P), ("heads", P, NH2), ("wo", P, P), ("cos", P, T), ("sin", P, T),
                   ("mask", P, P), ("eps", P, 1)],
        "swiglu": [("avg2", P, P), ("ident", P, P), ("ln", P, 1), ("router", P, 2 * NE), ("w1", P, 12 * P),
                   ("w3", P, 12 * P), ("w2", P, NE * P), ("w2r", P, NE * D), ("tri", P, NE * NE), ("eps", P, 1)],
    }[stage]
    at, out = 0, {}
    for name, rows, cols in s:
        out[name] = (rows, at, cols)
        at += cols
    return out, at


class Params:

    def __init__(self, tile, stage):
        self.tile, (self.parts, _) = tile, spec(stage)

    def __call__(self, name, r0=0, r1=None):
        rows, at, cols = self.parts[name]
        return self.tile[r0:rows if r1 is None else r1, at:at + cols]

    def cols(self, name, c0, c1, r0=0, r1=None):
        rows, at, _ = self.parts[name]
        return self.tile[r0:rows if r1 is None else r1, at + c0:at + c1]


STAGES = ("token", "qkv", "qr", "attn", "gelu", "ssm", "norm", "causal", "swiglu")


def load_params(nc, ctx, stage, dram):
    tile = ctx.enter_context(nc.sbuf_tensor(f"sb_params_{stage}", [P, spec(stage)[1]], F32))
    return tile, Params(tile, stage), nc.alloc_semaphore(f"params_{stage}_loaded")



def hash_stage(nc, dram):
    pad = 16
    with ExitStack() as ctx:
        def sb(name, shape, dt=F32):
            return ctx.enter_context(nc.sbuf_tensor(f"hash_{name}", shape, dt))

        chars_i = sb("chars_i", [B, T], I32)
        ident = sb("hash_ident", [P, P])
        win = [sb(f"window{s}", [B, pad + T]) for s in range(NSCALE + 1)]
        match = sb("match", [B, len(MATCH), T])
        index_i = sb("index_i", [P, NSCALE * TB * B], I32)
        index = sb("index", [P, PAIRS, NSCALE, TB, 2], I32)
        turned = ctx.enter_context(nc.psum_tensor("turned", [P, NSCALE, TB, B], F32))
        loaded, padded, windows, matched, transposed, indexed, stored = (
            ctx.enter_context(nc.semaphore(n)) for n in
            ("chars_loaded", "windows_padded", "windows_made", "match_made", "hashes_turned", "index_made",
             "hashes_stored"))
        block = ctx.enter_context(nc.Block())

        @block.sync
        def _(sp):
            sp.dma_start(chars_i[:, :], dram["x"]).then_inc(loaded, 16)
            parts, _ = spec("token")
            at = parts["ident"][1]
            sp.dma_start(ident[:, :], dram["params_token"][:, at:at + P]).then_inc(loaded, 16)
            sp.wait_ge(matched, 2)
            sp.dma_start(dram["match"], match[:, :, :]).then_inc(stored, 16)
            sp.wait_ge(indexed, 2)
            sp.dma_start(dram["index"], index[:, :, :, :, :].rearrange("p a b c d -> p (a b c d)")).then_inc(stored, 16)
            sp.wait_ge(stored, 32)

        @block.gpsimd
        def _(pool):
            for s in range(NSCALE + 1):
                last = nc.gpsimd.memset(win[s][:, 0:pad], 0.0)
            last.then_inc(padded, 1)

        @block.vector
        def _(dve):
            step = [0]

            def done(ins):
                step[0] += 1
                ins.then_inc(windows, 1)
                dve.wait_ge(windows, step[0])

            def ago(s, k):
                return win[s][:, pad - k:pad - k + T]

            dve.wait_ge(loaded, 32)
            dve.wait_ge(padded, 1)
            done(nc.vector.tensor_copy(ago(0, 0), chars_i[:, :]))
            done(nc.vector.scalar_tensor_tensor(ago(1, 0), ago(0, 1), 257.0, ago(0, 0), ALU.mult, ALU.add))
            done(nc.vector.scalar_tensor_tensor(ago(2, 0), ago(0, 2), 513.0, ago(1, 0), ALU.mult, ALU.add))
            done(nc.vector.scalar_tensor_tensor(ago(2, 0), ago(0, 3), 769.0, ago(2, 0), ALU.mult, ALU.add))
            done(nc.vector.tensor_tensor(ago(3, 0), ago(2, 0), ago(2, 4), ALU.add))
            done(nc.vector.tensor_tensor(ago(4, 0), ago(3, 0), ago(3, 8), ALU.add))
            for m, k in enumerate(MATCH):
                last = nc.vector.tensor_tensor(match[:, m, :], ago(0, 0), ago(0, k), ALU.is_equal)
            last.then_inc(matched, 1)
            dve.wait_ge(matched, 1)
            for m, k in enumerate(MATCH):
                last = nc.vector.memset(match[:, m, 0:k], 0.0)
            last.then_inc(matched, 1)
            dve.wait_ge(transposed, 1)
            nc.vector.tensor_copy(index_i[:, :], turned[:, :, :, :].rearrange("p a b c -> p (a b c)")).then_inc(indexed, 1)
            dve.wait_ge(indexed, 1)
            for s in range(NSCALE):
                src = index_i[:, s * TB * B:(s + 1) * TB * B].rearrange("p (t a q) -> p a t q", t=TB, q=2)
                last = nc.vector.tensor_scalar(index[:, :, s, :, :], src, HASH_MOD - 1, s * HASH_MOD,
                                               ALU.bitwise_and, ALU.bitwise_or)
            last.then_inc(indexed, 1)

        @block.tensor
        def _(pe):
            pe.wait_ge(loaded, 32)
            pe.wait_ge(windows, 6)
            for s in range(NSCALE):
                for t in range(TB):
                    last = nc.tensor.transpose(turned[:, s, t, :], win[s + 1][:, pad + t * P:pad + (t + 1) * P],
                                               ident[0:B, 0:B])
            last.then_inc(transposed, 1)


def token_stage(nc, dram):
    VS = ["onehot", "prod", "score", "smax", "sub", "sum", "rec", "weight", "wprod", "hsum",
          "conv0", "conv1", "conv2", "conv3", "gate", "d0", "d1", "clamped", "cum", "keep", "drive", "ratio",
          "fed", "states", "norm", "res0", "res1", "res2"]
    SSN = ["exp", "hashT", "silu_hash", "h1", "tanh", "centered", "square", "log", "rstd", "affine",
           "act0", "act1", "act2", "out"]
    TS = ["q", "hashT", "feat", "gates", "center", "var", "mlp0", "mlp1", "mlp2", "out"]
    with ExitStack() as ctx:
        def sb(name, shape, dt=F32):
            return [ctx.enter_context(nc.sbuf_tensor(f"token_{name}{s}", shape, dt)) for s in STREAMS]

        def one(name, shape, dt=F32):
            return ctx.enter_context(nc.sbuf_tensor(f"token_{name}", shape, dt))

        def sem(name):
            return nc.alloc_semaphore(f"token_{name}")

        params, par, params_loaded = load_params(nc, ctx, "token", dram)
        tq = one("tq", [P, D])
        w1b = one("w1b_sb", [P, H])
        wo_c = one("wo_c", [P, 2, H])
        bo_c = one("bo_c", [P, 1])
        half_bg = one("half_bg", [2 * SS, 1])
        mark, carrier = sb("mark", [P, 1]), sb("carrier", [P, 1])
        index = sb("idx", [P, NSCALE * TB * 2], U32)
        xb = sb("xb", [P, T], I32)
        mf = sb("mf", [P, 2, T])
        feat = sb("feat", [P, 2, T])
        emb = sb("emb", [P, TB, 2, NSCALE, D])
        prod = sb("prod", [P, 2, TB, NSCALE, D])
        sc = sb("sc", [P, 2, TB, NSCALE])
        wt = sb("wt", [P, 2, TB, NSCALE])
        mx = sb("mx", [P, 2 * TB])
        hsum = sb("hsum", [P, TB, 2, D])
        hpad = sb("hpad", [P, 3 + T])
        conv = sb("conv", [P, T])
        h = sb("h", [P, 2, T])
        sq = sb("sq", [P, 2, T])
        xc = sb("xc", [P, 2, T])
        gate, clamped, d0, d1, cum, keep, fed = (
            sb(n, [2 * SS, T]) for n in ("gate", "clamped", "d0", "d1", "cum", "keep", "fed"))
        states = sb("states", [P, T])
        ho = sb("ho", [P, T])
        ps = [[ctx.enter_context(nc.psum_tensor(f"token_ps{s}{k}", [P, T], F32)) for k in range(4)] for s in STREAMS]
        marked = [sem(f"round_open{s}") for s in STREAMS]
        x_in, idx_in, mf_in, gathered, stored = (
            [sem(f"{n}{s}") for s in STREAMS] for n in ("chars_in", "index_in", "match_in", "rows_gathered", "h_stored"))
        V = [Steps(sem(f"vector_steps{s}"), VS) for s in STREAMS]
        S = [Steps(sem(f"scalar_steps{s}"), SSN) for s in STREAMS]
        TE = [Steps(sem(f"tensor_steps{s}"), TS) for s in STREAMS]
        setup_pe, setup_v, pads = sem("setup_products"), sem("setup_weights"), sem("pads_cleared")
        block = ctx.enter_context(nc.Block())
        N = PAIRS // 2

        @block.sync
        def _(sp):
            sp.dma_start(params[:, :], dram["params_token"]).then_inc(params_loaded, 16)
            sp.wait_ge(pads, 1)
            with sp.Fori(0, N) as i:
                for s in STREAMS:
                    seq = i * 4 + 2 * s
                    wait_before(sp, V[s], i, "onehot")
                    sp.dma_start(xb[s][0:D, :], dram["x"][bass.ds(seq + 1, 1), :].to_broadcast((D, T))).then_inc(x_in[s], 16)
                    sp.dma_start(xb[s][D:P, :], dram["x"][bass.ds(seq, 1), :].to_broadcast((D, T))).then_inc(x_in[s], 16)
                    wait_before(sp, TE[s], i, "feat")
                    sp.dma_start(mf[s][0:4, :, :], dram["match"][bass.ds(seq, 2), :, :].rearrange("q k t -> k q t")).then_inc(mf_in[s], 16)
                for s in STREAMS:
                    wait_now(sp, S[s], i, "out")
                    sp.dma_start(dram["h0"][bass.ds(i * 2 + s, 1), :, :].rearrange("a p t -> (a p) t"), ho[s][:, :]).then_inc(stored[s], 16)
            for s in STREAMS:
                sp.wait_ge(stored[s], 16 * N)

        @block.gpsimd
        def _(pool):
            for s in STREAMS:
                nc.gpsimd.memset(mark[s][:, :], 0.0)
                nc.gpsimd.memset(mf[s][:, :, :], 0.0)
                nc.gpsimd.memset(states[s][:, :], 0.0)
                nc.gpsimd.memset(hpad[s][:, 0:3], 0.0)
            nc.gpsimd.memset(wo_c[:, :, :], 0.0).then_inc(pads, 1)
            pool.wait_ge(pads, 1)
            with pool.Fori(0, N) as i:
                for s in STREAMS:
                    pool.wait_ge(gathered[s], i * (16 * NSCALE * TB * 2))
                    pool.dma_start(index[s][:, :], dram["index"][:, bass.ds((i * 2 + s) * (NSCALE * TB * 2), NSCALE * TB * 2)]
                                   ).then_inc(idx_in[s], 16)
                for s in STREAMS:
                    pool.wait_ge(marked[s], i)
                    wait_before(pool, V[s], i, "wprod")
                    wait_load(pool, idx_in[s], i)
                    nc.gpsimd.tensor_tensor(carrier[s][:, :], mark[s][:, :], mark[s][:, :], ALU.mult).then_inc(marked[s], 1)
                    for c in range(NSCALE):
                        for t in range(TB):
                            for q in range(2):
                                k = (c * TB + t) * 2 + q
                                nc.gpsimd.indirect_dma_start(
                                    out=emb[s][:, t, q, c, :], out_offset=None, in_=dram["hash_tables"],
                                    in_offset=bass.IndirectOffsetOnAxis(ap=index[s][:, k:k + 1], axis=0),
                                ).then_inc(gathered[s], 16)

        @block.vector
        def _(dve):
            for s in STREAMS:
                nc.vector.sem_inc(V[s].sem, len(VS))
            dve.wait_ge(params_loaded, 16)
            dve.wait_ge(setup_pe, 1)
            nc.vector.tensor_tensor(tq[:, :], ps[0][0][:, 0:D], par("bq"), ALU.add)
            nc.vector.tensor_copy(par("w1a", D, P), ps[0][1][D:P, 0:H])
            nc.vector.tensor_copy(par("w1b", 0, D), ps[0][1][0:D, 0:H])
            dve.wait_ge(pads, 1)
            for q in range(2):
                nc.vector.tensor_copy(wo_c[SS * q:SS * (q + 1), q, :], ps[0][2][SS * q:SS * (q + 1), 0:H])
            nc.vector.tensor_copy(bo_c[:, :], ps[0][3][:, 0:1])
            nc.vector.tensor_scalar(half_bg[:, :], par("bg"), 0.5, None, ALU.mult).then_inc(setup_v, 1)
            with dve.Fori(0, N) as i:
                def hash_scores(s):
                    wait_load(dve, x_in[s], i, 2)
                    wait_before(dve, TE[s], i, "feat")
                    nc.vector.tensor_scalar(feat[s][D:P, 0, :], xb[s][D:P, :], par("iota", D, P), None, ALU.is_equal)
                    nc.vector.tensor_scalar(feat[s][0:D, 1, :], xb[s][0:D, :], par("iota", 0, D), None, ALU.is_equal
                                            ).then_inc(V[s].mark("onehot"), 1)

                def scores(s):
                    wait_load(dve, gathered[s], i, NSCALE * TB * 2)
                    wait_now(dve, TE[s], i, "q")
                    for q in range(2):
                        query = ps[s][q][:, 0:TB * D].rearrange("p (t o d) -> p t o d", t=TB, o=1).to_broadcast((P, TB, NSCALE, D))
                        last = nc.vector.tensor_tensor(prod[s][:, q], emb[s][:, :, q], query, ALU.mult)
                    last.then_inc(V[s].mark("prod"), 1)

                for s in STREAMS:
                    hash_scores(s)
                for s in STREAMS:
                    scores(s)
                for s in STREAMS:
                    wait_now(dve, V[s], i, "prod")
                    nc.vector.tensor_reduce(sc[s][:].rearrange("p q t c -> p (q t c)"), prod[s][:].rearrange("p q t c d -> p (q t c) d"), AX, ALU.add
                                            ).then_inc(V[s].mark("score"), 1)
                for s in STREAMS:
                    wait_now(dve, V[s], i, "score")
                    nc.vector.tensor_reduce(mx[s][:, :], sc[s][:].rearrange("p q t c -> p (q t) c"), AX, ALU.max
                                            ).then_inc(V[s].mark("smax"), 1)

                def across(tile):
                    return tile[:, :].rearrange("p (n o) -> p n o", o=1).to_broadcast((P, 2 * TB, NSCALE))

                def by_token(tile):
                    return tile[:].rearrange("p q t c -> p (q t) c")

                for s in STREAMS:
                    wait_now(dve, V[s], i, "smax")
                    nc.vector.tensor_tensor(by_token(sc[s]), by_token(sc[s]), across(mx[s]), ALU.subtract
                                            ).then_inc(V[s].mark("sub"), 1)
                for s in STREAMS:
                    wait_now(dve, S[s], i, "exp")
                    nc.vector.tensor_reduce(mx[s][:, :], by_token(wt[s]), AX, ALU.add).then_inc(V[s].mark("sum"), 1)
                for s in STREAMS:
                    wait_now(dve, V[s], i, "sum")
                    nc.vector.reciprocal(mx[s][:, :], mx[s][:, :]).then_inc(V[s].mark("rec"), 1)
                for s in STREAMS:
                    wait_now(dve, V[s], i, "rec")
                    nc.vector.tensor_tensor(by_token(wt[s]), by_token(wt[s]), across(mx[s]), ALU.mult
                                            ).then_inc(V[s].mark("weight"), 1)
                for s in STREAMS:
                    wait_now(dve, V[s], i, "weight")
                    for q in range(2):
                        w = wt[s][:, q].rearrange("p t (c o) -> p t c o", o=1).to_broadcast((P, TB, NSCALE, D))
                        last = nc.vector.tensor_tensor(prod[s][:, q], emb[s][:, :, q], w, ALU.mult)
                    last.then_inc(V[s].mark("wprod"), 1)
                for s in STREAMS:
                    wait_now(dve, V[s], i, "wprod")
                    wait_before(dve, TE[s], i, "hashT")
                    for q in range(2):
                        last = nc.vector.tensor_reduce(hsum[s][:, :, q, :], prod[s][:, q].rearrange("p t c d -> p t d c"), AX, ALU.add)
                    last.then_inc(V[s].mark("hsum"), 1)
                for k in range(4):
                    for s in STREAMS:
                        if k == 0:
                            wait_now(dve, S[s], i, "hashT")
                            nc.vector.tensor_scalar(conv[s][:, :], hpad[s][:, 0:T], par.cols("conv_w", 0, 1), par("conv_b"),
                                                    ALU.mult, ALU.add).then_inc(V[s].mark("conv0"), 1)
                        else:
                            wait_now(dve, V[s], i, f"conv{k - 1}")
                            nc.vector.scalar_tensor_tensor(conv[s][:, :], hpad[s][:, k:k + T], par.cols("conv_w", k, k + 1),
                                                           conv[s][:, :], ALU.mult, ALU.add).then_inc(V[s].mark(f"conv{k}"), 1)
                for s in STREAMS:
                    wait_now(dve, S[s], i, "tanh")
                    nc.vector.tensor_scalar(gate[s][:, :], keep[s][:, :], 0.5, 0.5, ALU.mult, ALU.add).then_inc(V[s].mark("gate"), 1)
                for s in STREAMS:
                    wait_now(dve, V[s], i, "gate")
                    nc.vector.scalar_tensor_tensor(d0[s][:, :], gate[s][:, :], 1e-6, par("rest"), ALU.max, ALU.mult).then_inc(V[s].mark("d0"), 1)
                    nc.vector.scalar_tensor_tensor(d1[s][:, :], gate[s][:, :], 1e-6, par("first"), ALU.max, ALU.mult).then_inc(V[s].mark("d1"), 1)
                    nc.vector.tensor_scalar(clamped[s][:, :], gate[s][:, :], 1e-6, None, ALU.max).then_inc(V[s].mark("clamped"), 1)
                for s in STREAMS:
                    wait_now(dve, V[s], i, "d1")
                    nc.vector.tensor_tensor_scan(cum[s][:, :], d0[s][:, :], d1[s][:, :], 0.0, ALU.mult, ALU.add).then_inc(V[s].mark("cum"), 1)
                    nc.vector.tensor_scalar(keep[s][:, :], keep[s][:, :], -0.5, 0.5, ALU.mult, ALU.add).then_inc(V[s].mark("keep"), 1)
                for s in STREAMS:
                    wait_now(dve, V[s], i, "keep")
                    nc.vector.scalar_tensor_tensor(fed[s][:, :], ps[s][3][0:2 * SS, :], par("bi"), keep[s][:, :], ALU.add, ALU.mult
                                                   ).then_inc(V[s].mark("drive"), 1)
                    nc.vector.tensor_scalar(cum[s][:, :], cum[s][:, :], 1e8, 1.0, ALU.mult, ALU.min).then_inc(V[s].mark("ratio"), 1)
                for s in STREAMS:
                    wait_now(dve, V[s], i, "ratio")
                    nc.vector.tensor_tensor(fed[s][:, :], fed[s][:, :], cum[s][:, :], ALU.mult).then_inc(V[s].mark("fed"), 1)
                for s in STREAMS:
                    wait_now(dve, V[s], i, "fed")
                    nc.vector.tensor_tensor_scan(states[s][0:2 * SS, :], clamped[s][:, :], fed[s][:, :], 0.0, ALU.mult, ALU.add
                                                 ).then_inc(V[s].mark("states"), 1)
                for s in STREAMS:
                    wait_now(dve, S[s], i, "rstd")
                    nc.vector.tensor_tensor(xc[s][:], xc[s][:], sq[s][:], ALU.mult).then_inc(V[s].mark("norm"), 1)
                for l in range(NMLP):
                    for s in STREAMS:
                        wait_now(dve, S[s], i, f"act{l}")
                        nc.vector.tensor_tensor(h[s][:], h[s][:], sq[s][:], ALU.add).then_inc(V[s].mark(f"res{l}"), 1)

        @block.scalar
        def _(act):
            for s in STREAMS:
                nc.scalar.sem_inc(S[s].sem, len(SSN))
            act.wait_ge(setup_v, 1)
            act.wait_ge(pads, 1)
            with act.Fori(0, N) as i:
                for s in STREAMS:
                    wait_now(act, V[s], i, "sub")
                    nc.scalar.activation(wt[s][:], sc[s][:], ACT.Exp, scale=D ** -0.5).then_inc(S[s].mark("exp"), 1)
                for s in STREAMS:
                    wait_now(act, TE[s], i, "hashT")
                    nc.scalar.activation(hpad[s][:, 3:3 + T], ps[s][2][:, :], ACT.Copy).then_inc(S[s].mark("hashT"), 1)
                for s in STREAMS:
                    wait_now(act, V[s], i, "conv3")
                    nc.scalar.activation(feat[s][0:D, 0, :], conv[s][0:D, :], ACT.Silu)
                    nc.scalar.activation(feat[s][D:P, 1, :], conv[s][D:P, :], ACT.Silu).then_inc(S[s].mark("silu_hash"), 1)
                for s in STREAMS:
                    wait_now(act, TE[s], i, "feat")
                    wait_before(act, TE[s], i, "out")
                    for q in range(2):
                        last = nc.scalar.activation(h[s][:, q, :], ps[s][q][:, :], ACT.Silu, bias=par("b_in"))
                    last.then_inc(S[s].mark("h1"), 1)
                for s in STREAMS:
                    wait_now(act, TE[s], i, "gates")
                    nc.scalar.activation(keep[s][:, :], ps[s][2][0:2 * SS, :], ACT.Tanh, bias=half_bg[:, :], scale=0.5
                                         ).then_inc(S[s].mark("tanh"), 1)
                for s in STREAMS:
                    wait_now(act, TE[s], i, "center")
                    for q in range(2):
                        last = nc.scalar.activation(xc[s][:, q, :], ps[s][q][:, :], ACT.Identity, bias=bo_c[:, :])
                    last.then_inc(S[s].mark("centered"), 1)
                    for q in range(2):
                        last = nc.scalar.activation(sq[s][:, q, :], ps[s][q][:, :], ACT.Square, bias=bo_c[:, :])
                    last.then_inc(S[s].mark("square"), 1)
                for s in STREAMS:
                    wait_now(act, TE[s], i, "var")
                    for q in range(2):
                        last = nc.scalar.activation(sq[s][:, q, :], ps[s][2 + q][:, :], ACT.Ln, bias=par("eps"))
                    last.then_inc(S[s].mark("log"), 1)
                for s in STREAMS:
                    wait_now(act, S[s], i, "log")
                    nc.scalar.activation(sq[s][:], sq[s][:], ACT.Exp, scale=-0.5).then_inc(S[s].mark("rstd"), 1)
                for s in STREAMS:
                    wait_now(act, V[s], i, "norm")
                    for q in range(2):
                        last = nc.scalar.activation(h[s][:, q, :], xc[s][:, q, :], ACT.Identity, bias=par("ln_b"), scale=par("ln_g"))
                    last.then_inc(S[s].mark("affine"), 1)
                for l in range(NMLP):
                    for s in STREAMS:
                        wait_now(act, TE[s], i, f"mlp{l}")
                        wait_now(act, V[s], i, "norm" if l == 0 else f"res{l - 1}")
                        for q in range(2):
                            last = nc.scalar.activation(sq[s][:, q, :], ps[s][q][:, :], ACT.Silu, bias=par.cols("mlp_b", l, l + 1))
                        last.then_inc(S[s].mark(f"act{l}"), 1)
                for s in STREAMS:
                    wait_now(act, TE[s], i, "out")
                    act.wait_ge(stored[s], i * 16)
                    nc.scalar.activation(ho[s][:, :], ps[s][2][:, :], ACT.Identity, bias=par("bout")).then_inc(S[s].mark("out"), 1)

        @block.tensor
        def _(pe):
            for s in STREAMS:
                nc.tensor.sem_inc(TE[s].sem, len(TS))
            pe.wait_ge(params_loaded, 16)
            nc.tensor.matmul(ps[0][0][:, 0:D], par("embT"), par("wq"), start=True, stop=True)
            nc.tensor.matmul(ps[0][1][:, 0:H], par("embT"), par("win_e"), start=True, stop=True)
            nc.tensor.matmul(ps[0][2][0:2 * SS, 0:H], par("woT"), par("cen"), start=True, stop=True)
            nc.tensor.matmul(ps[0][3][:, 0:1], par("cen"), par("bo"), start=True, stop=True).then_inc(setup_pe, 1)
            pe.wait_ge(setup_v, 1)
            with pe.Fori(0, N) as i:
                for s in STREAMS:
                    wait_now(pe, V[s], i, "onehot")
                    wait_before(pe, S[s], i, "act2")
                    for t in range(TB):
                        nc.tensor.matmul(ps[s][0][:, t * D:(t + 1) * D], feat[s][D:P, 0, t * P:(t + 1) * P], tq[D:P, :], start=True, stop=True)
                        last = nc.tensor.matmul(ps[s][1][:, t * D:(t + 1) * D], feat[s][0:D, 1, t * P:(t + 1) * P], tq[0:D, :], start=True, stop=True)
                    last.then_inc(TE[s].mark("q"), 1)
                for s in STREAMS:
                    wait_now(pe, V[s], i, "hsum")
                    wait_before(pe, S[s], i, "out")
                    for t in range(TB):
                        last = nc.tensor.transpose(ps[s][2][:, t * P:(t + 1) * P], hsum[s][:, t].rearrange("p q d -> p (q d)"), par("ident"))
                    last.then_inc(TE[s].mark("hashT"), 1)
                for s in STREAMS:
                    wait_now(pe, S[s], i, "silu_hash")
                    wait_load(pe, mf_in[s], i)
                    for q, w in enumerate(("w1a", "w1b")):
                        nc.tensor.matmul(ps[s][q][:, :], par(w), feat[s][:, q, :], start=True, stop=False)
                        last = nc.tensor.matmul(ps[s][q][:, :], par("wmf"), mf[s][:, q, :], start=False, stop=True)
                    last.then_inc(TE[s].mark("feat"), 1)
                for s in STREAMS:
                    wait_now(pe, S[s], i, "h1")
                    for q in range(2):
                        nc.tensor.matmul(ps[s][2][SS * q:SS * (q + 1), :], par("wg"), h[s][:, q, :], start=True, stop=True)
                        last = nc.tensor.matmul(ps[s][3][SS * q:SS * (q + 1), :], par("wi"), h[s][:, q, :], start=True, stop=True)
                    last.then_inc(TE[s].mark("gates"), 1)
                for s in STREAMS:
                    wait_now(pe, V[s], i, "states")
                    for q in range(2):
                        nc.tensor.matmul(ps[s][q][:, :], par("cen"), h[s][:, q, :], start=True, stop=False)
                        last = nc.tensor.matmul(ps[s][q][:, :], wo_c[:, q, :], states[s][:, :], start=False, stop=True)
                    last.then_inc(TE[s].mark("center"), 1)
                for s in STREAMS:
                    wait_now(pe, S[s], i, "square")
                    for q in range(2):
                        last = nc.tensor.matmul(ps[s][2 + q][:, :], par("avg"), sq[s][:, q, :], start=True, stop=True)
                    last.then_inc(TE[s].mark("var"), 1)
                for l in range(NMLP):
                    for s in STREAMS:
                        if l == 0:
                            wait_now(pe, S[s], i, "affine")
                        else:
                            wait_now(pe, V[s], i, f"res{l - 1}")
                        for q in range(2):
                            last = nc.tensor.matmul(ps[s][q][:, :], par.cols("mlp_w", l * H, (l + 1) * H), h[s][:, q, :], start=True, stop=True)
                        last.then_inc(TE[s].mark(f"mlp{l}"), 1)
                for s in STREAMS:
                    wait_now(pe, V[s], i, "res2")
                    for q in range(2):
                        last = nc.tensor.matmul(ps[s][2][D * q:D * (q + 1), :], par("wout"), h[s][:, q, :], start=True, stop=True)
                    last.then_inc(TE[s].mark("out"), 1)



def qkv_stage(nc, dram):
    VS = ["norm", "bias0", "bias1", "bias2", "bias3"]
    SSN = ["square", "log", "rstd", "gram"]
    TS = ["center", "var", "qkv0", "qkv1", "qkv2", "qkv3", "gram"]
    with ExitStack() as ctx:
        def sb(name, shape, dt=F32):
            return [ctx.enter_context(nc.sbuf_tensor(f"qkv_{name}{s}", shape, dt)) for s in STREAMS]

        def sem(name):
            return nc.alloc_semaphore(f"qkv_{name}")

        params, par, params_loaded = load_params(nc, ctx, "qkv", dram)
        h, sq, xn = sb("h", [P, T]), sb("sq", [P, T]), sb("xn", [P, T])
        qkv = sb("qkv", [P, 2, TB, 3 * D])
        gram = sb("gram", [P, 2, P])
        ps = [[ctx.enter_context(nc.psum_tensor(f"qkv_ps{s}{k}", [P, T], F32)) for k in range(4)] for s in STREAMS]
        h_in, tok_out, gram_out = ([sem(f"{n}{s}") for s in STREAMS] for n in ("h_in", "tokens_stored", "gram_stored"))
        V = [Steps(sem(f"vector_steps{s}"), VS) for s in STREAMS]
        S = [Steps(sem(f"scalar_steps{s}"), SSN) for s in STREAMS]
        TE = [Steps(sem(f"tensor_steps{s}"), TS) for s in STREAMS]
        block = ctx.enter_context(nc.Block())
        N = PAIRS // 2

        @block.sync
        def _(sp):
            sp.dma_start(params[:, :], dram["params_qkv"]).then_inc(params_loaded, 16)
            with sp.Fori(0, N) as i:
                for s in STREAMS:
                    wait_before(sp, TE[s], i, "center")
                    sp.dma_start(h[s][:, :], dram["h0"][bass.ds(i * 2 + s, 1), :, :].rearrange("a p t -> (a p) t")).then_inc(h_in[s], 16)
                for s in STREAMS:
                    wait_now(sp, V[s], i, "bias3")
                    sp.dma_start(dram["tokens"][bass.ds(i * 4 + 2 * s, 2), :, :, :].rearrange("q p t c -> p q (t c)"),
                                 qkv[s][:].rearrange("p q t c -> p q (t c)")).then_inc(tok_out[s], 16)
                    wait_now(sp, S[s], i, "gram")
                    sp.dma_start(dram["gram"][bass.ds(i * 4 + 2 * s, 2), :, :].rearrange("q p c -> p q c"), gram[s][:]).then_inc(gram_out[s], 16)
            for s in STREAMS:
                sp.wait_ge(tok_out[s], 16 * N)
                sp.wait_ge(gram_out[s], 16 * N)

        @block.vector
        def _(dve):
            for s in STREAMS:
                nc.vector.sem_inc(V[s].sem, len(VS))
            dve.wait_ge(params_loaded, 16)
            with dve.Fori(0, N) as i:
                for s in STREAMS:
                    wait_now(dve, S[s], i, "rstd")
                    wait_before(dve, TE[s], i, "qkv3")
                    nc.vector.tensor_tensor(xn[s][:, :], ps[s][0][:, :], sq[s][:, :], ALU.mult).then_inc(V[s].mark("norm"), 1)
                bias = par("bqkv").rearrange("p (o c) -> p o c", o=1).to_broadcast((P, 2, 3 * D))
                for k in range(4):
                    for s in STREAMS:
                        if k == 0:
                            dve.wait_ge(tok_out[s], i * 16)
                        wait_now(dve, TE[s], i, f"qkv{k}")
                        nc.vector.tensor_tensor(qkv[s][:, k // 2, 2 * (k % 2):2 * (k % 2) + 2, :],
                                                ps[s][k][:, 0:6 * D].rearrange("p (t c) -> p t c", t=2), bias, ALU.add
                                                ).then_inc(V[s].mark(f"bias{k}"), 1)

        @block.scalar
        def _(act):
            for s in STREAMS:
                nc.scalar.sem_inc(S[s].sem, len(SSN))
            act.wait_ge(params_loaded, 16)
            with act.Fori(0, N) as i:
                for s in STREAMS:
                    wait_now(act, TE[s], i, "center")
                    nc.scalar.activation(sq[s][:, :], ps[s][0][:, :], ACT.Square).then_inc(S[s].mark("square"), 1)
                for s in STREAMS:
                    wait_now(act, TE[s], i, "var")
                    nc.scalar.activation(sq[s][:, :], ps[s][1][:, :], ACT.Ln, bias=par("eps")).then_inc(S[s].mark("log"), 1)
                for s in STREAMS:
                    wait_now(act, S[s], i, "log")
                    nc.scalar.activation(sq[s][:, :], sq[s][:, :], ACT.Exp, scale=-0.5).then_inc(S[s].mark("rstd"), 1)
                for s in STREAMS:
                    wait_now(act, TE[s], i, "gram")
                    act.wait_ge(gram_out[s], i * 16)
                    for q in range(2):
                        last = nc.scalar.activation(gram[s][:, q, :], ps[s][q][:, 384:384 + P], ACT.Copy)
                    last.then_inc(S[s].mark("gram"), 1)

        @block.tensor
        def _(pe):
            for s in STREAMS:
                nc.tensor.sem_inc(TE[s].sem, len(TS))
            pe.wait_ge(params_loaded, 16)
            with pe.Fori(0, N) as i:
                for s in STREAMS:
                    wait_load(pe, h_in[s], i)
                    wait_before(pe, S[s], i, "gram")
                    wait_before(pe, V[s], i, "bias1")
                    nc.tensor.matmul(ps[s][0][:, :], par("cen2"), h[s][:, :], start=True, stop=True).then_inc(TE[s].mark("center"), 1)
                for s in STREAMS:
                    wait_now(pe, S[s], i, "square")
                    nc.tensor.matmul(ps[s][1][:, :], par("avg2"), sq[s][:, :], start=True, stop=True).then_inc(TE[s].mark("var"), 1)
                for s in STREAMS:
                    wait_now(pe, V[s], i, "norm")
                    wait_before(pe, V[s], i, "bias3")
                    for k in range(4):
                        q = k // 2
                        for t in range(2):
                            tt = 2 * (k % 2) + t
                            last = nc.tensor.matmul(ps[s][k][:, t * 3 * D:(t + 1) * 3 * D], xn[s][D * q:D * (q + 1), tt * P:(tt + 1) * P],
                                                    par("wqkv", D * q, D * (q + 1)), start=True, stop=True)
                        last.then_inc(TE[s].mark(f"qkv{k}"), 1)
                for s in STREAMS:
                    wait_now(pe, V[s], i, "bias3")
                    for q in range(2):
                        for t in range(TB):
                            last = nc.tensor.matmul(ps[s][q][:, 384:384 + P], qkv[s][:, q, t, 0:P], qkv[s][:, q, t, 0:P],
                                                    start=(t == 0), stop=(t == TB - 1))
                    last.then_inc(TE[s].mark("gram"), 1)


def qr_stage(nc, dram):
    G = 4
    with ExitStack() as ctx:
        def sb(name, shape):
            return ctx.enter_context(nc.sbuf_tensor(f"qr_{name}", shape, F32))

        def sem(name):
            return nc.alloc_semaphore(f"qr_{name}")

        aug = sb("aug", [P, G, HD, 2 * HD])
        top = sb("top", [P, G, HD, HD])
        eye = sb("eye", [P, G * HD * HD])
        prod = sb("prod", [P, HD, HD, HD])
        outer = sb("outer", [P, G, HD, 2 * HD])
        factor = sb("factor", [P, G, HD])
        rec = sb("rec", [P, G])
        diag = sb("diag", [P, G, HD])
        root = sb("root", [P, G, HD])
        li = sb("li", [P, G, HD, HD])
        w = sb("w", [P, G, HD, HD])
        sign = sb("sign", [P, G, HD])
        both = sb("both", [P, 2, HD])
        lq = sb("lq", [P, 2, HD, HD])
        blocks = sb("blocks", [P, 2, HD, HD])
        zero = sb("zero", [P, B * D * D // P])
        loaded, cleared, zeroed, steps, rooted, pivots, made, stored = (
            sem(n) for n in ("loaded", "zero_made", "blocks_zeroed", "vector_steps", "roots", "pivots", "blocks_made", "stored"))
        block = ctx.enter_context(nc.Block())
        LOADS = 2 * G * 4 + 1

        @block.sync
        def _(sp):
            sp.dma_start(eye[:, :], dram["params_qr"]).then_inc(loaded, 16)
            for a in range(4):
                for g in range(G):
                    r = (g // 2) * D + (2 * a + g % 2) * HD
                    sp.dma_start(aug[32 * a:32 * a + 32, g, :, 0:HD], dram["gram"][:, r:r + HD, r:r + HD]).then_inc(loaded, 16)
                    sp.dma_start(top[32 * a:32 * a + 32, g, :, :], dram["tokens"][0:B, 0:HD, 0, r:r + HD]).then_inc(loaded, 16)
            sp.wait_ge(cleared, 1)
            sp.dma_start(dram["blocks"][0:B].rearrange("b r c -> (b r c)").rearrange("(p n) -> p n", p=P), zero[:, :]).then_inc(zeroed, 16)
            sp.wait_ge(made, 1)
            sp.wait_ge(zeroed, 16)
            for a in range(4):
                for k in range(2):
                    r = (2 * a + k) * HD
                    sp.dma_start(dram["blocks"][0:B, r:r + HD, r:r + HD], blocks[32 * a:32 * a + 32, k, :, :]).then_inc(stored, 16)
            sp.wait_ge(stored, 16 * 8)

        @block.gpsimd
        def _(pool):
            nc.gpsimd.memset(zero[:, :], 0.0).then_inc(cleared, 1)

        @block.scalar
        def _(act):
            act.wait_ge(pivots, 1)
            nc.scalar.activation(root[:, :, :], diag[:, :, :], ACT.Sqrt).then_inc(rooted, 1)

        @block.vector
        def _(dve):
            count = [0]

            def then(ins):
                count[0] += 1
                ins.then_inc(steps, 1)
                dve.wait_ge(steps, count[0])

            dve.wait_ge(loaded, 16 * LOADS)
            then(nc.vector.tensor_copy(aug[:, :, :, HD:2 * HD], eye[:, :].rearrange("p (g r c) -> p g r c", g=G, r=HD)))
            for j in range(HD):
                then(nc.vector.tensor_copy(diag[:, :, j], aug[:, :, j, j]))
                if j == HD - 1:
                    break
                n = HD - 1 - j
                then(nc.vector.reciprocal(rec[:, :], aug[:, :, j, j]))
                then(nc.vector.tensor_tensor(factor[:, :, 0:n], aug[:, :, j + 1:HD, j],
                                             rec[:, :].rearrange("p (g o) -> p g o", o=1).to_broadcast((P, G, n)), ALU.mult))
                then(nc.vector.tensor_tensor(
                    outer[:, :, 0:n, :], factor[:, :, 0:n].rearrange("p g (n o) -> p g n o", o=1).to_broadcast((P, G, n, 2 * HD)),
                    aug[:, :, j:j + 1, :].to_broadcast((P, G, n, 2 * HD)), ALU.mult))
                then(nc.vector.tensor_tensor(aug[:, :, j + 1:HD, :], aug[:, :, j + 1:HD, :], outer[:, :, 0:n, :], ALU.subtract))
            nc.vector.sem_inc(pivots, 1)
            dve.wait_ge(rooted, 1)
            then(nc.vector.reciprocal(root[:, :, :], root[:, :, :]))
            then(nc.vector.tensor_tensor(li[:, :, :, :], aug[:, :, :, HD:2 * HD],
                                         root[:, :, :].rearrange("p g (r o) -> p g r o", o=1).to_broadcast((P, G, HD, HD)), ALU.mult))
            for g in range(G):
                then(nc.vector.tensor_tensor(
                    prod[:, :, :, :], top[:, g, :, :].rearrange("p n (o j) -> p n o j", o=1).to_broadcast((P, HD, HD, HD)),
                    li[:, g:g + 1, :, :].to_broadcast((P, HD, HD, HD)), ALU.mult))
                then(nc.vector.tensor_reduce(w[:, g, :, :], prod[:, :, :, :], AX, ALU.add))
            for d in range(HD):
                then(nc.vector.tensor_scalar(sign[:, :, d], w[:, :, d, d], 0.0, None, ALU.is_ge))
                then(nc.vector.tensor_scalar(sign[:, :, d], sign[:, :, d], -2.0, 1.0, ALU.mult, ALU.add))
                if d == HD - 1:
                    break
                n = HD - 1 - d
                then(nc.vector.tensor_tensor(rec[:, :], w[:, :, d, d], sign[:, :, d], ALU.subtract))
                then(nc.vector.reciprocal(rec[:, :], rec[:, :]))
                then(nc.vector.tensor_tensor(factor[:, :, 0:n], w[:, :, d + 1:HD, d],
                                             rec[:, :].rearrange("p (g o) -> p g o", o=1).to_broadcast((P, G, n)), ALU.mult))
                then(nc.vector.tensor_tensor(
                    outer[:, :, 0:n, 0:n], factor[:, :, 0:n].rearrange("p g (n o) -> p g n o", o=1).to_broadcast((P, G, n, n)),
                    w[:, :, d:d + 1, d + 1:HD].to_broadcast((P, G, n, n)), ALU.mult))
                then(nc.vector.tensor_tensor(w[:, :, d + 1:HD, d + 1:HD], w[:, :, d + 1:HD, d + 1:HD], outer[:, :, 0:n, 0:n], ALU.subtract))
            then(nc.vector.tensor_tensor(both[:, :, :], sign[:, 0:2, :], sign[:, 2:4, :], ALU.mult))
            then(nc.vector.tensor_tensor(lq[:, :, :, :], li[:, 0:2, :, :],
                                         both[:, :, :].rearrange("p g (r o) -> p g r o", o=1).to_broadcast((P, 2, HD, HD)), ALU.mult))
            for k in range(2):
                then(nc.vector.tensor_tensor(
                    prod[:, :, :, :], li[:, 2 + k, :, :].rearrange("p d (j o) -> p j o d", o=1).to_broadcast((P, HD, HD, HD)),
                    lq[:, k, :, :].rearrange("p d (o i) -> p o i d", o=1).to_broadcast((P, HD, HD, HD)), ALU.mult))
                then(nc.vector.tensor_reduce(blocks[:, k, :, :], prod[:, :, :, :], AX, ALU.add))
            nc.vector.sem_inc(made, 1)


class Count:

    def __init__(self, sem, per_round):
        self.sem, self.per_round = sem, per_round

    def value(self, i, j):
        return i * self.per_round + (self.per_round + j + 1)


def attention_stage(nc, dram):
    R = 2 * HEADS
    VR = 2 * HD
    VW = P + VR
    NT = TB
    widths = [P, P, NFEAT - 2 * P]
    quads = [P, P, NQUAD - 2 * P]
    with ExitStack() as ctx:
        def one(name, shape, dt=F32):
            return ctx.enter_context(nc.sbuf_tensor(f"attn_{name}", shape, dt))

        def sb(name, shape, dt=F32):
            return [one(f"{name}{k}", shape, dt) for k in range(2)]

        def sem(name):
            return nc.alloc_semaphore(f"attn_{name}")

        def bank(name):
            return ctx.enter_context(nc.psum_tensor(f"attn_{name}", [P, T], F32))

        params, par, params_loaded = load_params(nc, ctx, "attn", dram)
        tok = sb("tok", [P, TB, 3 * D])
        blk = sb("blk", [P, 2 * D])
        resid = sb("resid", [D, T])
        kt_sb = one("kt", [P, T])
        k2 = one("k2", [P, TB, D])
        fq, fk, fk2 = one("fq", [P, TB, NFEAT]), one("fk", [P, TB, NFEAT]), one("fk2", [P, TB, NQUAD])
        fq_high, fq_low = sb("fq_high", [P, 3, T], F32R), sb("fq_low", [P, 3, T], F32R)
        fkt, fk2t = sb("fkt", [P, 3, T]), sb("fk2t", [P, 3, T])
        psi = one("psi", [P, 3, T])
        psi_hi, psi_lo = sb("psi_high", [P, 3, T], F32R), sb("psi_low", [P, 3, T], F32R)
        prob = sb("prob", [P, NT, T])
        pt_hi, pt_lo = sb("turned_high", [P, NT, T], F32R), sb("turned_low", [P, NT, T], F32R)
        vp = one("value_parts", [P, NT, HEADS * VW], F32R)
        nmax = one("nmax", [P, 2, NT])
        rsum = sb("rsum", [P, NT, HEADS])
        rsx = one("rsum_inverse", [P, NT, HEADS, VR])
        rinv, on = one("rsum_turned", [P, T]), one("on", [P, T])
        hout = one("hout", [D, T])
        coef_b, coef_c = one("coef_b", [P, 3, HEADS]), one("coef_c", [P, 3, HEADS])
        bn = one("bn", [3 * HEADS, 4])
        cw = one("cw", [3 * HEADS, 2, HEADS])
        L = [bank(f"logits{k}") for k in range(NT)]
        PT = [bank(f"turned{k}") for k in range(2)]
        O, X = bank("values"), bank("features")

        tok_in = [sem(f"tokens_in{k}") for k in range(2)]
        blk_in = [sem(f"blocks_in{k}") for k in range(2)]
        res_in = [sem(f"residual_in{k}") for k in range(2)]
        stored, extra = sem("h_stored"), sem("extra_copied")
        setup_s, setup_v, setup_pe, ones_set = sem("setup_s"), sem("setup_v"), sem("setup_pe"), sem("ones_set")

        def count(name, per_round):
            return Count(sem(name), per_round)

        logits, maxes, exps = count("logits", R * NT), count("maxes", R * NT), count("exps", R * NT)
        turned, turned_high, turned_low = (count(n, R * NT) for n in ("turned", "turned_high_made", "turned_low_made"))
        values = count("values", R)
        psi_b, psi_all, psi_high, psi_low = (count(n, R) for n in ("psi_b", "psi_all", "psi_high_made", "psi_low_made"))
        kt_ps, kt_copied, k2_ps, k2_copied = (count(n, 2) for n in ("kt_ps", "kt_copied", "k2_ps", "k2_copied"))
        mono = count("mono", 6)
        feat_ps, feat_copied = count("feat_ps", 18), count("feat_copied", 18)
        queries_low = count("queries_low", 6)
        v_high, v_low = count("v_high", 2), count("v_low", 2)
        normed, rsum_inv = count("normed", 2), count("rsum_inv", 4)
        rinv_ps, rinv_copied = count("rinv_ps", 2), count("rinv_copied", 2)
        proj_ps, resid_added = count("proj_ps", 2), count("resid_added", 2)
        block = ctx.enter_context(nc.Block())
        N = B // 2
        h0, h1 = dram["h0"].rearrange("a (q d) t -> (a q) d t", q=2), dram["h1"].rearrange("a (q d) t -> (a q) d t", q=2)

        def wait(eng, c, i, j):
            eng.wait_ge(c.sem, c.value(i, j))

        def prime(eng, *counts):
            for c in counts:
                eng.sem_inc(c.sem, c.per_round)

        def placed(part):
            return vp[:, :, :].rearrange("p t (h c) -> p t h c", c=VW)[:, :, :, part * HD:(part + 1) * HD]

        @block.sync
        def _(sp):
            sp.dma_start(params[:, :], dram["params_attn"]).then_inc(params_loaded, 16)
            sp.dma_start(dram["tokens"][B], dram["tokens"][0]).then_inc(extra, 16)
            sp.dma_start(dram["blocks"][B], dram["blocks"][0]).then_inc(extra, 16)
            sp.wait_ge(extra, 32)

            def load(i, n, seq):
                k = n % 2
                wait(sp, values, i, (n - 2) * HEADS + HEADS - 1)
                sp.dma_start(tok[k][:, :, :], dram["tokens"][bass.ds(seq, 1), :, :, :].rearrange("a p t c -> p (a t) c")).then_inc(tok_in[k], 16)
                wait(sp, k2_ps, i, n - 2)
                sp.dma_start(blk[k][D:P, 0:D], dram["blocks"][bass.ds(seq, 1), :, :].rearrange("a r c -> (a r) c")).then_inc(blk_in[k], 16)

            sp.wait_ge(ones_set, 1)
            load(0, 0, 0)
            with sp.Fori(0, N) as i:
                nexts = [sp.snap(i * 2 + 1), sp.snap(i * 2 + 2)]
                for n in range(2):
                    wait(sp, resid_added, i, n - 2)
                    sp.dma_start(resid[n][:, :], h0[bass.ds(i * 2 + n, 1), :, :].rearrange("a p t -> (a p) t")).then_inc(res_in[n], 16)
                    load(i, n + 1, nexts[n])
                    wait(sp, resid_added, i, n)
                    sp.dma_start(h1[bass.ds(i * 2 + n, 1), :, :].rearrange("a p t -> (a p) t"), hout[:, :]).then_inc(stored, 16)
            sp.wait_ge(stored, 16 * B)

        @block.gpsimd
        def _(pool):
            prime(nc.gpsimd, mono, psi_low)
            for k in range(2):
                nc.gpsimd.memset(blk[k][:, :], 0.0)
            nc.gpsimd.memset(vp[:, :, :].bitcast(F32), 0.0)
            nc.gpsimd.memset(psi[:, :, :], 0.0)
            nc.gpsimd.memset(fq[:, :, NFEAT - 1:NFEAT], 1.0)
            nc.gpsimd.memset(fk[:, :, NFEAT - 1:NFEAT], 1.0).then_inc(ones_set, 1)

            def products(dst, src, linear):
                at = 0
                quad = dst[:, :, 0:NQUAD].rearrange("p t (h m) -> p t h m", h=HEADS)
                x = src.rearrange("p t (h d) -> p t h d", h=HEADS)
                for r in range(HD):
                    last = nc.gpsimd.tensor_tensor(quad[:, :, :, at:at + HD - r], x[:, :, :, 0:HD - r], x[:, :, :, r:HD], ALU.mult)
                    at += HD - r
                if linear:
                    last = nc.gpsimd.tensor_copy(dst[:, :, NQUAD:NQUAD + D], src)
                last.then_inc(mono.sem, 1)

            def prepare(i, n):
                k = n % 2

                def queries():
                    pool.wait_ge(tok_in[k], i * 16 + 16 * (n // 2 + 1))
                    wait(pool, feat_ps, i, 9 * (n - 1) + 2)
                    products(fq, tok[k][:, :, 0:D], True)

                def keys():
                    wait(pool, feat_ps, i, 9 * (n - 1) + 5)
                    products(fk, tok[k][:, :, D:2 * D], True)

                def mapped_keys():
                    wait(pool, k2_copied, i, n)
                    wait(pool, feat_ps, i, 9 * (n - 1) + 8)
                    products(fk2, k2[:, :, :], False)

                return queries, keys, mapped_keys

            def keys_low(i, g):
                wait(pool, psi_high, i, g)
                nc.gpsimd.tensor_tensor(psi_lo[g % 2][:, :, :], psi[:, :, :], psi_hi[g % 2][:, :, :].bitcast(F32), ALU.subtract
                                        ).then_inc(psi_low.sem, 1)

            for part in prepare(0, 0):
                part()
            keys_low(0, 0)
            keys_low(0, 1)
            keys_low(0, 2)
            with pool.Fori(0, N) as i:
                for g in range(2, R + 2):
                    keys_low(i, g + 1)
                    if g % HEADS in (2, 3, 4):
                        prepare(i, g // HEADS + 1)[g % HEADS - 2]()

        @block.scalar
        def _(act):
            prime(nc.scalar, exps, turned_high, psi_b, psi_high, kt_copied, k2_copied, feat_copied, v_high, rinv_copied)
            act.wait_ge(params_loaded, 16)
            nc.scalar.activation(bn[:, 0:1], par("var"), ACT.Ln, bias=par("eps")).then_inc(setup_s, 1)
            act.wait_ge(setup_s, 1)
            nc.scalar.activation(bn[:, 0:1], bn[:, 0:1], ACT.Exp, scale=-0.5).then_inc(setup_s, 1)
            act.wait_ge(setup_v, 7)
            act.wait_ge(ones_set, 1)

            def keys_turned(i, n):
                wait(act, kt_ps, i, n)
                nc.scalar.activation(kt_sb[:, :], X[:, :], ACT.Copy).then_inc(kt_copied.sem, 1)

            def keys_mapped(i, n):
                wait(act, k2_ps, i, n)
                wait(act, mono, i, 3 * (n - 1) + 2)
                nc.scalar.activation(k2[:, :, :], X[:, :].rearrange("p (t d) -> p t d", t=TB)[:, :, 0:D], ACT.Copy
                                     ).then_inc(k2_copied.sem, 1)

            def values_high(i, n):
                k = n % 2
                act.wait_ge(tok_in[k], i * 16 + 16 * (n // 2 + 1))
                wait(act, values, i, (n - 1) * HEADS + HEADS - 1)
                nc.scalar.activation(placed(0), tok[k][:, :, 2 * D:3 * D].rearrange("p t (h d) -> p t h d", h=HEADS), ACT.Copy
                                     ).then_inc(v_high.sem, 1)

            def features(i, n, a, c):
                wait(act, feat_ps, i, 9 * n + 3 * a + c)
                dst, rows = (fq_high, widths) if a == 0 else (fkt, widths) if a == 1 else (fk2t, quads)
                nc.scalar.activation(dst[n % 2][0:rows[c], c, :], X[0:rows[c], :], ACT.Copy).then_inc(feat_copied.sem, 1)

            def keys_weighted(i, g):
                wait(act, psi_low, i, g - 1)
                wait(act, feat_copied, i, 9 * (g // HEADS) + 8)
                for c in range(3):
                    r = widths[c]
                    last = nc.scalar.activation(psi[0:r, c, :], fkt[g // HEADS % 2][0:r, c, :], ACT.Copy,
                                                scale=coef_b[0:r, c, g % HEADS:g % HEADS + 1])
                last.then_inc(psi_b.sem, 1)

            def keys_high(i, g):
                wait(act, psi_all, i, g)
                wait(act, logits, i, (g - 2) * NT + NT - 1)
                nc.scalar.activation(psi_hi[g % 2][:, :, :], psi[:, :, :], ACT.Copy).then_inc(psi_high.sem, 1)

            keys_turned(0, 0)
            keys_mapped(0, 0)
            values_high(0, 0)
            for a in range(3):
                for c in range(3):
                    features(0, 0, a, c)
            keys_weighted(0, 0)
            keys_high(0, 0)
            def step(i, g):
                n, o = g // HEADS, g % HEADS
                keys_weighted(i, g + 1)
                wait(act, turned, i, (g - 2) * NT + NT - 1)
                for t in range(NT):
                    if g >= 1:
                        if t == 0:
                            wait(act, values, i, g - 3)
                        wait(act, turned, i, (g - 1) * NT + t)
                        nc.scalar.activation(pt_hi[(g - 1) % 2][:, t, :], PT[t % 2][:, :], ACT.Copy).then_inc(turned_high.sem, 1)
                    if t == 1:
                        keys_high(i, g + 1)
                    wait(act, maxes, i, g * NT + t)
                    nc.scalar.activation(prob[g % 2][:, t, :], L[t][:, :], ACT.Exp, bias=nmax[:, g % 2, t:t + 1],
                                         accum_out=rsum[n % 2][:, t, o:o + 1]).then_inc(exps.sem, 1)
                    if o in (4, 5, 6) and t < 3:
                        features(i, n + 1, o - 4, t)
                    if o == 2 and t == 1:
                        keys_turned(i, n + 1)
                    if o == 3 and t == 1:
                        keys_mapped(i, n + 1)
                if g in (HEADS, R):
                    m = g // HEADS - 1
                    wait(act, normed, i, m - 1)
                    wait(act, rinv_ps, i, m)
                    nc.scalar.activation(rinv[:, :], X[:, :], ACT.Copy).then_inc(rinv_copied.sem, 1)
                if g in (HEADS + 1, R + 1):
                    values_high(i, g // HEADS)

            step(0, 0)
            step(0, 1)
            with act.Fori(0, N) as i:
                for g in range(2, R + 2):
                    step(i, g)

        @block.vector
        def _(dve):
            prime(nc.vector, maxes, turned_low, psi_all, queries_low, v_low, normed, rsum_inv, resid_added)
            setup = [0]

            def then(ins):
                setup[0] += 1
                ins.then_inc(setup_v, 1)
                dve.wait_ge(setup_v, setup[0])

            dve.wait_ge(params_loaded, 16)
            dve.wait_ge(setup_s, 2)
            then(nc.vector.tensor_tensor(bn[:, 1:2], bn[:, 0:1], par("gamma"), ALU.mult))
            then(nc.vector.tensor_tensor(bn[:, 2:3], bn[:, 1:2], par("mean"), ALU.mult))
            then(nc.vector.tensor_tensor(bn[:, 3:4], par("beta"), bn[:, 2:3], ALU.subtract))
            then(nc.vector.tensor_scalar(cw[:, 1, :], par("convT"), bn[:, 3:4], None, ALU.mult))
            then(nc.vector.tensor_scalar(cw[:, 0, :], par("convT"), bn[:, 1:2], par("scales"), ALU.mult, ALU.mult))
            dve.wait_ge(setup_pe, 1)
            nc.vector.tensor_copy(coef_b[:, :, :].rearrange("p c o -> p (c o)"), X[:, 0:24])
            then(nc.vector.tensor_copy(coef_c[:, :, :].rearrange("p c o -> p (c o)"), X[:, 24:48]))
            then(nc.vector.scalar_tensor_tensor(coef_b[:, 2, :], par("conv_b"), par("last"), coef_b[:, 2, :], ALU.mult, ALU.add))

            def keys_mixed(i, g):
                wait(dve, psi_b, i, g)
                for c in range(3):
                    r = quads[c]
                    last = nc.vector.scalar_tensor_tensor(psi[0:r, c, :], fk2t[g // HEADS % 2][0:r, c, :],
                                                          coef_c[0:r, c, g % HEADS:g % HEADS + 1], psi[0:r, c, :], ALU.mult, ALU.add)
                last.then_inc(psi_all.sem, 1)

            def low_queries(i, n, c):
                r = widths[c]
                wait(dve, feat_copied, i, 9 * n + c)
                nc.vector.tensor_tensor(fq_low[n % 2][0:r, c, :], X[0:r, :], fq_high[n % 2][0:r, c, :].bitcast(F32), ALU.subtract
                                        ).then_inc(queries_low.sem, 1)

            def low_values(i, n):
                k = n % 2
                wait(dve, v_high, i, n)
                nc.vector.tensor_tensor(placed(1), tok[k][:, :, 2 * D:3 * D].rearrange("p t (h d) -> p t h d", h=HEADS),
                                        placed(0).bitcast(F32), ALU.subtract).then_inc(v_low.sem, 1)

            low_values(0, 0)
            for c in range(3):
                low_queries(0, 0, c)
            keys_mixed(0, 0)
            def step(i, g):
                for t in range(NT):
                    wait(dve, logits, i, g * NT + t)
                    wait(dve, exps, i, (g - 2) * NT + t)
                    nc.vector.tensor_reduce(nmax[:, g % 2, t:t + 1], L[t][:, :], AX, ALU.max, negate=True
                                            ).then_inc(maxes.sem, 1)
                    if t == 0:
                        keys_mixed(i, g + 1)
                    if g >= 1:
                        wait(dve, turned_high, i, (g - 1) * NT + t)
                        nc.vector.tensor_tensor(pt_lo[(g - 1) % 2][:, t, :], PT[t % 2][:, :], pt_hi[(g - 1) % 2][:, t, :].bitcast(F32),
                                                ALU.subtract).then_inc(turned_low.sem, 1)
                    if g % HEADS == 4 and t < 3:
                        low_queries(i, g // HEADS + 1, t)
                if g in (HEADS, R):
                    m = g // HEADS - 1
                    wait(dve, exps, i, m * HEADS * NT + HEADS * NT - 1)
                    nc.vector.reciprocal(rsum[m][:, :, :], rsum[m][:, :, :]).then_inc(rsum_inv.sem, 1)
                    wait(dve, rsum_inv, i, 2 * m)
                    wait(dve, rinv_ps, i, m - 1)
                    nc.vector.tensor_copy(rsx[:, :, :, :], rsum[m][:, :, :].rearrange("p t (h o) -> p t h o", o=1
                                                                                    ).to_broadcast((P, NT, HEADS, VR))).then_inc(rsum_inv.sem, 1)
                if g in (HEADS + 1, R + 1):
                    m = g // HEADS - 1
                    wait(dve, proj_ps, i, m - 1)
                    wait(dve, values, i, m * HEADS + HEADS - 1)
                    wait(dve, rinv_copied, i, m)
                    nc.vector.tensor_tensor(on[:, :], O[:, :], rinv[:, :], ALU.mult).then_inc(normed.sem, 1)
                    low_values(i, m + 1)
                if g in (HEADS + 1, R + 1):
                    m = g // HEADS - 1
                    wait(dve, proj_ps, i, m)
                    dve.wait_ge(res_in[m], i * 16 + 16)
                    dve.wait_ge(stored, i * 32 + 16 * m)
                    nc.vector.scalar_tensor_tensor(hout[:, :], X[0:D, :], par("bproj", 0, D), resid[m][:, :], ALU.add, ALU.add
                                                   ).then_inc(resid_added.sem, 1)

            step(0, 0)
            step(0, 1)
            with dve.Fori(0, N) as i:
                for g in range(2, R + 2):
                    step(i, g)

        @block.tensor
        def _(pe):
            prime(nc.tensor, logits, turned, values, kt_ps, k2_ps, feat_ps, rinv_ps, proj_ps)
            pe.wait_ge(params_loaded, 16)
            pe.wait_ge(setup_v, 5)
            for c in range(3):
                nc.tensor.matmul(X[:, c * HEADS:(c + 1) * HEADS], par.cols("sel_b", c * P, (c + 1) * P), cw[:, 0, :],
                                 start=True, stop=(c < 2))
            nc.tensor.matmul(X[:, 2 * HEADS:3 * HEADS], par("sel_1"), cw[:, 1, :], start=False, stop=True)
            for c in range(3):
                last = nc.tensor.matmul(X[:, (3 + c) * HEADS:(4 + c) * HEADS], par.cols("sel_c", c * P, (c + 1) * P), cw[:, 0, :],
                                        start=True, stop=True)
            last.then_inc(setup_pe, 1)
            pe.wait_ge(setup_v, 7)

            def keys_turned(i, n):
                k = n % 2
                pe.wait_ge(tok_in[k], i * 16 + 16 * (n // 2 + 1))
                for t in range(TB):
                    last = nc.tensor.transpose(X[:, t * P:(t + 1) * P], tok[k][:, t, 0:2 * D], par("ident"))
                last.then_inc(kt_ps.sem, 1)

            def keys_mapped(i, n):
                k = n % 2
                wait(pe, kt_copied, i, n)
                pe.wait_ge(blk_in[k], i * 16 + 16 * (n // 2 + 1))
                for t in range(TB):
                    last = nc.tensor.matmul(X[:, t * P:(t + 1) * P], kt_sb[:, t * P:(t + 1) * P], blk[k][:, :], start=True, stop=True)
                last.then_inc(k2_ps.sem, 1)

            def features(i, n, a, c):
                src, rows = ((fq, widths), (fk, widths), (fk2, quads))[a]
                wait(pe, mono, i, 3 * n + a)
                if a == 0 and c == 0:
                    wait(pe, k2_copied, i, n)
                elif a == 0 or a == 1 and c == 0:
                    wait(pe, queries_low, i, 3 * n + (c - 1 if c else 2))
                else:
                    wait(pe, feat_copied, i, 9 * n + 3 * a + c - 1)
                for t in range(TB):
                    last = nc.tensor.transpose(X[0:rows[c], t * P:(t + 1) * P], src[:, t, c * P:c * P + rows[c]], par("ident"))
                last.then_inc(feat_ps.sem, 1)

            def turn(i, g, mt):
                wait(pe, turned_low, i, g * NT + mt - 2)
                for t in range(NT):
                    last = nc.tensor.transpose(PT[mt % 2][:, t * P:(t + 1) * P], prob[g % 2][:, t, mt * P:(mt + 1) * P], par("ident"))
                last.then_inc(turned.sem, 1)

            pe.wait_ge(ones_set, 1)
            keys_turned(0, 0)
            keys_mapped(0, 0)
            for a in range(3):
                for c in range(3):
                    features(0, 0, a, c)
            def step(i, g):
                n, o = g // HEADS, g % HEADS
                for t in range(NT):
                    if t == 0:
                        wait(pe, psi_low, i, g)
                        if o == 0:
                            wait(pe, queries_low, i, 3 * n + 2)
                    wait(pe, exps, i, (g - 1) * NT + t)
                    tt = slice(t * P, (t + 1) * P)
                    for c in range(3):
                        w = widths[c]
                        for a, b in ((fq_high, psi_hi), (fq_high, psi_lo), (fq_low, psi_hi)):
                            last = nc.tensor.matmul(L[t][:, :], a[n % 2][0:w, c, tt], b[g % 2][0:w, c, :],
                                                    start=c == 0 and b is psi_hi and a is fq_high, stop=c == 2 and a is fq_low)
                    last.then_inc(logits.sem, 1)
                    if g >= 1:
                        if t == 0:
                            wait(pe, exps, i, (g - 1) * NT + NT - 1)
                        turn(i, g - 1, t)
                    if o == 2 and t == 1:
                        wait(pe, resid_added, i, n - 1)
                        keys_turned(i, n + 1)
                    if o == 3 and t == 1:
                        keys_mapped(i, n + 1)
                    if o in (4, 5, 6) and t < 3:
                        features(i, n + 1, o - 4, t)
                if g >= 2:
                    v = g - 2
                    wait(pe, turned_low, i, v * NT + NT - 1)
                    if v % HEADS == 0:
                        wait(pe, v_low, i, v // HEADS)
                        wait(pe, normed, i, v // HEADS - 1)
                    h = v % HEADS
                    for mt in range(NT):
                        for part in (pt_hi, pt_lo):
                            last = nc.tensor.matmul(O[:, :], vp[:, mt, h * P:(h + 1) * P], part[v % 2][:, mt, :],
                                                    start=h == 0 and mt == 0 and part is pt_hi,
                                                    stop=h == HEADS - 1 and mt == NT - 1 and part is pt_lo)
                    last.then_inc(values.sem, 1)
                if g in (HEADS, R):
                    m = g // HEADS - 1
                    wait(pe, rsum_inv, i, 2 * m + 1)
                    wait(pe, feat_copied, i, 9 * (m + 1) + 8)
                    for t in range(NT):
                        last = nc.tensor.transpose(X[:, t * P:(t + 1) * P], rsx[:, t, :, :].rearrange("p h r -> p (h r)"), par("ident"))
                    last.then_inc(rinv_ps.sem, 1)
                if g in (HEADS + 1, R + 1):
                    m = g // HEADS - 1
                    wait(pe, normed, i, m)
                    nc.tensor.matmul(X[:, :], par("wproj"), on[:, :], start=True, stop=True).then_inc(proj_ps.sem, 1)

            step(0, 0)
            step(0, 1)
            with pe.Fori(0, N) as i:
                for g in range(2, R + 2):
                    step(i, g)



def top2(nc, steps, wait_own, score, ge, gt, mask, tri):
    a = score[:, :, :].rearrange("p n (e o) -> p n e o", o=1).to_broadcast((P, 2 * TB, NE, NE))
    b = score[:, :, :].rearrange("p n (o e) -> p n o e", o=1).to_broadcast((P, 2 * TB, NE, NE))

    def table(t):
        return t.rearrange("p (o e f) -> p o e f", o=1, e=NE).to_broadcast((P, 2 * TB, NE, NE))

    nc.vector.tensor_tensor(ge[:, :, :, :], b, a, ALU.is_ge)
    nc.vector.tensor_tensor(gt[:, :, :, :], b, a, ALU.is_gt).then_inc(steps.mark("compare"), 1)
    wait_own("compare")
    nc.vector.tensor_tensor(ge[:, :, :, :], ge[:, :, :, :], table(tri), ALU.mult).then_inc(steps.mark("lower"), 1)
    wait_own("lower")
    nc.vector.tensor_tensor(ge[:, :, :, :], ge[:, :, :, :], gt[:, :, :, :], ALU.max).then_inc(steps.mark("above"), 1)
    wait_own("above")
    nc.vector.tensor_reduce(mask[:, :, :], ge[:, :, :, :], AX, ALU.add).then_inc(steps.mark("rank"), 1)
    wait_own("rank")
    nc.vector.tensor_scalar(mask[:, :, :], mask[:, :, :], 2.0, None, ALU.is_lt).then_inc(steps.mark("mask"), 1)


def gelu_stage(nc, dram):
    YS = [(q, t) for q in range(2) for t in range(TB)]
    VS = (["norm", "low0", "low1", "score", "compare", "lower", "above", "rank", "mask"]
          + [x for q, t in YS for x in (f"masked{q}{t}", f"summed{q}{t}")] + ["out"])
    SSN = ["square", "log", "rstd", "high0", "high1"] + [f"gelu{q}{e}" for q in range(2) for e in range(NE)] + ["maskT"]
    UP, DOWN = ([[f"{n}{q}{k}" for k in range(count)] for q in range(2)] for n, count in (("up", NE), ("down", TB)))
    TS = ["center", "var"] + UP[0] + ["score"] + DOWN[0] + UP[1] + ["maskT"] + DOWN[1] + ["out"]
    with ExitStack() as ctx:
        def sb(name, shape, dt=F32):
            return [ctx.enter_context(nc.sbuf_tensor(f"gelu_{name}{s}", shape, dt)) for s in STREAMS]

        def sem(name):
            return nc.alloc_semaphore(f"gelu_{name}")

        params, par, params_loaded = load_params(nc, ctx, "gelu", dram)
        h, sq, xn = sb("h", [P, T]), sb("sq", [P, T]), sb("xn", [P, T])
        score, mask = sb("score", [P, 2 * TB, NE]), sb("mask", [P, 2 * TB, NE])
        ge, gt = sb("ge", [P, 2 * TB, NE, NE]), sb("gt", [P, 2 * TB, NE, NE])
        xs = sb("xs", [P, 2, T], F32R)
        wh, wl = (ctx.enter_context(nc.sbuf_tensor(f"gelu_w1_{part}", [P, NE * FH], F32R)) for part in ("high", "low"))
        split = sem("weights_split")
        maskt = sb("maskt", [P, 2, T])
        zeroed = sem("zeros_set")
        hid = sb("hid", [P, NE, T])
        ym = sb("ym", [P, 2, NE, D])
        z = sb("z", [P, 2, TB, D])
        ho = sb("ho", [P, T])
        ps = [[ctx.enter_context(nc.psum_tensor(f"gelu_ps{s}{k}", [P, T], F32)) for k in range(4)] for s in STREAMS]
        h_in, stored = ([sem(f"{n}{s}") for s in STREAMS] for n in ("h_in", "stored"))
        V = [Steps(sem(f"vector_steps{s}"), VS) for s in STREAMS]
        S = [Steps(sem(f"scalar_steps{s}"), SSN) for s in STREAMS]
        TE = [Steps(sem(f"tensor_steps{s}"), TS) for s in STREAMS]
        block = ctx.enter_context(nc.Block())
        N = PAIRS // 2

        @block.sync
        def _(sp):
            sp.dma_start(params[:, :], dram["params_gelu"]).then_inc(params_loaded, 16)
            with sp.Fori(0, N) as i:
                for s in STREAMS:
                    wait_before(sp, V[s], i, "out")
                    sp.dma_start(h[s][:, :], dram["h1"][bass.ds(i * 2 + s, 1), :, :].rearrange("a p t -> (a p) t")).then_inc(h_in[s], 16)
                for s in STREAMS:
                    wait_now(sp, V[s], i, "out")
                    sp.dma_start(dram["h2"][bass.ds(i * 2 + s, 1), :, :].rearrange("a p t -> (a p) t"), ho[s][:, :]).then_inc(stored[s], 16)
            for s in STREAMS:
                sp.wait_ge(stored[s], 16 * N)

        @block.gpsimd
        def _(pool):
            nc.gpsimd.memset(maskt[0][:, :, :], 0.0)
            nc.gpsimd.memset(maskt[1][:, :, :], 0.0).then_inc(zeroed, 1)

        @block.vector
        def _(dve):
            for s in STREAMS:
                nc.vector.sem_inc(V[s].sem, len(VS))
            dve.wait_ge(params_loaded, 16)
            nc.vector.tensor_copy(wh[:, :], par("w1")).then_inc(split, 1)
            dve.wait_ge(split, 1)
            nc.vector.tensor_tensor(wl[:, :], par("w1"), wh[:, :].bitcast(F32), ALU.subtract).then_inc(split, 1)
            with dve.Fori(0, N) as i:
                for s in STREAMS:
                    wait_now(dve, S[s], i, "rstd")
                    nc.vector.tensor_tensor(xn[s][:, :], ps[s][0][:, :], sq[s][:, :], ALU.mult).then_inc(V[s].mark("norm"), 1)
                for q in range(2):
                    own, other = slice(D * q, D * (q + 1)), slice(D * (1 - q), D * (2 - q))
                    for s in STREAMS:
                        wait_now(dve, S[s], i, f"high{q}")
                        nc.vector.tensor_tensor(xs[s][other, q, :], xn[s][own, :], xs[s][own, q, :].bitcast(F32), ALU.subtract
                                                ).then_inc(V[s].mark(f"low{q}"), 1)
                for s in STREAMS:
                    wait_now(dve, TE[s], i, "score")
                    nc.vector.tensor_tensor(score[s][:, :, :], ps[s][1][:, 0:2 * TB * NE].rearrange("p (n e) -> p n e", e=NE),
                                            par("bg").rearrange("p (o e) -> p o e", o=1).to_broadcast((P, 2 * TB, NE)), ALU.add
                                            ).then_inc(V[s].mark("score"), 1)
                for s in STREAMS:
                    wait_now(dve, V[s], i, "score")
                    top2(nc, V[s], lambda name, s=s: wait_now(dve, V[s], i, name), score[s], ge[s], gt[s], mask[s],
                         par("tri"))
                for q, t in YS:
                    for s in STREAMS:
                        wait_now(dve, TE[s], i, f"down{q}{t}")
                        k = q * TB + t
                        if k >= 2:
                            wait_now(dve, V[s], i, "summed%d%d" % YS[k - 2])
                        else:
                            wait_now(dve, V[s], i, "mask")
                        m = mask[s][:, 2 * t + q, :].rearrange("p (e o) -> p e o", o=1).to_broadcast((P, NE, D))
                        nc.vector.tensor_tensor(ym[s][:, t % 2], ps[s][2 + t % 2][:, :].rearrange("p (e d) -> p e d", e=NE), m, ALU.mult
                                                ).then_inc(V[s].mark(f"masked{q}{t}"), 1)
                    for s in STREAMS:
                        wait_now(dve, V[s], i, f"masked{q}{t}")
                        nc.vector.tensor_reduce(z[s][:, q, t, :], ym[s][:, t % 2].rearrange("p e d -> p d e"), AX, ALU.add
                                                ).then_inc(V[s].mark(f"summed{q}{t}"), 1)
                for s in STREAMS:
                    wait_now(dve, TE[s], i, "out")
                    dve.wait_ge(stored[s], i * 16)
                    nc.vector.tensor_tensor(ho[s][:, :], ps[s][0][:, :], h[s][:, :], ALU.add).then_inc(V[s].mark("out"), 1)

        @block.scalar
        def _(act):
            for s in STREAMS:
                nc.scalar.sem_inc(S[s].sem, len(SSN))
            act.wait_ge(params_loaded, 16)
            act.wait_ge(zeroed, 1)
            with act.Fori(0, N) as i:
                for s in STREAMS:
                    wait_now(act, TE[s], i, "center")
                    nc.scalar.activation(sq[s][:, :], ps[s][0][:, :], ACT.Square).then_inc(S[s].mark("square"), 1)
                for s in STREAMS:
                    wait_now(act, TE[s], i, "var")
                    nc.scalar.activation(sq[s][:, :], ps[s][1][:, :], ACT.Ln, bias=par("eps")).then_inc(S[s].mark("log"), 1)
                for s in STREAMS:
                    wait_now(act, S[s], i, "log")
                    nc.scalar.activation(sq[s][:, :], sq[s][:, :], ACT.Exp, scale=-0.5).then_inc(S[s].mark("rstd"), 1)
                for q in range(2):
                    for s in STREAMS:
                        wait_now(act, V[s], i, "norm")
                        nc.scalar.activation(xs[s][D * q:D * (q + 1), q, :], xn[s][D * q:D * (q + 1), :], ACT.Copy
                                             ).then_inc(S[s].mark(f"high{q}"), 1)
                for q in range(2):
                    for e in range(NE):
                        for s in STREAMS:
                            wait_now(act, TE[s], i, f"up{q}{e}")
                            nc.scalar.activation(hid[s][:, e, :], ps[s][e % 4][:, :], ACT.Gelu, bias=par.cols("b1", e, e + 1)
                                                 ).then_inc(S[s].mark(f"gelu{q}{e}"), 1)
                for s in STREAMS:
                    wait_now(act, TE[s], i, "maskT")
                    for q in range(2):
                        last = nc.scalar.activation(maskt[s][0:NE, q, :], ps[s][q][0:NE, :], ACT.Copy)
                    last.then_inc(S[s].mark("maskT"), 1)

        @block.tensor
        def _(pe):
            for s in STREAMS:
                nc.tensor.sem_inc(TE[s].sem, len(TS))
            pe.wait_ge(params_loaded, 16)
            pe.wait_ge(split, 2)
            with pe.Fori(0, N) as i:
                for s in STREAMS:
                    wait_load(pe, h_in[s], i)
                    nc.tensor.matmul(ps[s][0][:, :], par("cen2"), h[s][:, :], start=True, stop=True).then_inc(TE[s].mark("center"), 1)
                for s in STREAMS:
                    wait_now(pe, S[s], i, "square")
                    nc.tensor.matmul(ps[s][1][:, :], par("avg2"), sq[s][:, :], start=True, stop=True).then_inc(TE[s].mark("var"), 1)
                for q in range(2):
                    for e in range(NE):
                        for s in STREAMS:
                            if e >= 4:
                                wait_now(pe, S[s], i, f"gelu{q}{e - 4}")
                            elif e == 0 and q == 0:
                                wait_now(pe, V[s], i, "low1")
                            elif e >= 2 and q == 1:
                                wait_now(pe, V[s], i, f"masked0{e}")
                            nc.tensor.matmul(ps[s][e % 4][:, :], wh[:, e * FH:(e + 1) * FH], xs[s][:, q, :], start=True, stop=False)
                            nc.tensor.matmul(ps[s][e % 4][:, :], wl[:, e * FH:(e + 1) * FH], xs[s][:, q, :], start=False, stop=True
                                             ).then_inc(TE[s].mark(f"up{q}{e}"), 1)
                    for s in STREAMS:
                        if q == 0:
                            wait_now(pe, S[s], i, f"gelu0{NE - 3}")
                            for t in range(TB):
                                last = nc.tensor.matmul(ps[s][1][:, t * 2 * NE:(t + 1) * 2 * NE], xn[s][:, t * P:(t + 1) * P], par("wg"),
                                                        start=True, stop=True)
                            last.then_inc(TE[s].mark("score"), 1)
                        else:
                            wait_now(pe, S[s], i, f"gelu1{NE - 3}")
                            for r in range(2):
                                for t in range(TB):
                                    last = nc.tensor.transpose(ps[s][r][0:NE, t * P:(t + 1) * P], mask[s][:, 2 * t + r, :], par("ident"))
                            last.then_inc(TE[s].mark("maskT"), 1)
                    for t in range(TB):
                        for s in STREAMS:
                            if t == 0:
                                wait_now(pe, S[s], i, f"gelu{q}{NE - 1}")
                            if t >= 2:
                                wait_now(pe, V[s], i, f"masked{q}{t - 2}")
                            for e in range(NE):
                                last = nc.tensor.matmul(ps[s][2 + t % 2][:, e // 2 * P:(e // 2 + 1) * P], hid[s][:, e, t * P:(t + 1) * P],
                                                        par.cols("w2", e * P, (e + 1) * P), start=e % 2 == 0, stop=e % 2 == 1)
                            last.then_inc(TE[s].mark(f"down{q}{t}"), 1)
                for s in STREAMS:
                    wait_now(pe, V[s], i, f"summed1{TB - 1}")
                    wait_now(pe, S[s], i, "maskT")
                    for q in range(2):
                        for t in range(TB):
                            nc.tensor.matmul(ps[s][0][D * q:D * (q + 1), t * P:(t + 1) * P], z[s][:, q, t, :], par("ident"), start=True, stop=False)
                            last = nc.tensor.matmul(ps[s][0][D * q:D * (q + 1), t * P:(t + 1) * P], par("b2"), maskt[s][:, q, t * P:(t + 1) * P],
                                                    start=False, stop=True)
                    last.then_inc(TE[s].mark("out"), 1)



def ssm_stage(nc, dram):
    VS = ["norm"] + [f"{x}{q}" for q in range(2) for x in ("cos_part", "sin_part", "rotated", "states")] + ["relu", "out"]
    SSN = ["square", "log", "rstd"]
    TS = ["center", "var", "bu0", "bu1", "y"]
    GS = [f"{x}{q}" for q in range(2) for x in ("back_cos", "back_sin")]
    with ExitStack() as ctx:
        def one(name, shape, dt=F32):
            return ctx.enter_context(nc.sbuf_tensor(f"ssm_{name}", shape, dt))

        def sb(name, shape):
            return [one(f"{name}{s}", shape) for s in STREAMS]

        def sem(name):
            return nc.alloc_semaphore(f"ssm_{name}")

        params, par, params_loaded = load_params(nc, ctx, "ssm", dram)
        cos, sin, decay = one("cos", [P, T]), one("sin", [P, T]), one("decay", [P, T])
        w = one("small", [P, 24])
        bmat, bt = one("bmat", [P, 4, D]), one("bt", [P, 2, P])
        c1, c2 = one("c1", [P, D]), one("c2", [P, D])
        h, sq, xn = sb("h", [P, T]), sb("sq", [P, T]), sb("xn", [P, T])
        za, zb = sb("za", [P, T]), sb("zb", [P, T])
        y = sb("y", [P, 2, T])
        u1, u2 = sb("u1", [P, 2, T]), sb("u2", [P, 2, T])
        ho = sb("ho", [P, T])
        ps = [[ctx.enter_context(nc.psum_tensor(f"ssm_ps{s}{k}", [P, T], F32)) for k in range(4)] for s in STREAMS]
        h_in, stored = ([sem(f"{n}{s}") for s in STREAMS] for n in ("h_in", "stored"))
        V = [Steps(sem(f"vector_steps{s}"), VS) for s in STREAMS]
        S = [Steps(sem(f"scalar_steps{s}"), SSN) for s in STREAMS]
        TE = [Steps(sem(f"tensor_steps{s}"), TS) for s in STREAMS]
        G = [Steps(sem(f"gpsimd_steps{s}"), GS) for s in STREAMS]
        setup_v, setup_s, setup_pe = sem("setup_v"), sem("setup_s"), sem("setup_pe")
        block = ctx.enter_context(nc.Block())
        N = PAIRS // 2

        def c(k):
            return w[:, k:k + 1]

        STEP, RE, R, TH, TC, TS_, CO, SI, LRE, LIM, GRE, GIM, T1, T2, T3, T4 = range(16)
        marks = {}

        @block.sync
        def _(sp):
            sp.dma_start(params[:, :], dram["params_ssm"]).then_inc(params_loaded, 16)
            with sp.Fori(0, N) as i:
                for s in STREAMS:
                    wait_before(sp, V[s], i, "out")
                    sp.dma_start(h[s][:, :], dram["h2"][bass.ds(i * 2 + s, 1), :, :].rearrange("a p t -> (a p) t")).then_inc(h_in[s], 16)
                for s in STREAMS:
                    wait_now(sp, V[s], i, "out")
                    sp.dma_start(dram["h3"][bass.ds(i * 2 + s, 1), :, :].rearrange("a p t -> (a p) t"), ho[s][:, :]).then_inc(stored[s], 16)
            for s in STREAMS:
                sp.wait_ge(stored[s], 16 * N)

        @block.vector
        def _(dve):
            count = [0]

            def then(ins):
                count[0] += 1
                ins.then_inc(setup_v, 1)
                dve.wait_ge(setup_v, count[0])

            def tt(out, a, b, op):
                then(nc.vector.tensor_tensor(out, a, b, op))

            def ts(out, a, x, y, op0, op1):
                then(nc.vector.tensor_scalar(out, a, x, y, op0, op1))

            for s in STREAMS:
                nc.vector.sem_inc(V[s].sem, len(VS))
            dve.wait_ge(params_loaded, 16)
            ts(c(T1), par("lre"), -1.0, None, ALU.mult, ALU.bypass)
            tt(c(RE), par("lre"), c(T1), ALU.min)
            dve.wait_ge(setup_s, 1)
            tt(c(TH), par("lim"), c(STEP), ALU.mult)
            tt(c(T2), c(RE), c(STEP), ALU.mult)
            for at, quarter in ((TS_, 0.0), (TC, float(np.pi / 2))):
                ts(c(T3), c(TH), quarter, float(1 / (2 * np.pi)), ALU.add, ALU.mult)
                ts(c(T3), c(T3), float(1.5 * 2 ** 23), float(-1.5 * 2 ** 23), ALU.add, ALU.add)
                ts(c(T4), c(T3), -6.28125, quarter, ALU.mult, ALU.add)
                tt(c(at), c(TH), c(T4), ALU.add)
                ts(c(T4), c(T3), float(-(2 * np.pi - 6.28125)), None, ALU.mult, ALU.bypass)
                tt(c(at), c(at), c(T4), ALU.add)
                ts(c(at), c(at), 3.1415925, -3.1415925, ALU.min, ALU.max)
            marks["angles"] = count[0]
            dve.wait_ge(setup_s, 4)
            tt(c(LRE), c(R), c(CO), ALU.mult)
            ts(c(LRE), c(LRE), -1.0, None, ALU.add, ALU.bypass)
            tt(c(LIM), c(R), c(SI), ALU.mult)
            tt(c(T1), c(RE), c(RE), ALU.mult)
            tt(c(T2), par("lim"), par("lim"), ALU.mult)
            tt(c(T1), c(T1), c(T2), ALU.add)
            then(nc.vector.reciprocal(c(T1), c(T1)))
            tt(c(T2), c(LRE), c(RE), ALU.mult)
            tt(c(T3), c(LIM), par("lim"), ALU.mult)
            tt(c(GRE), c(T2), c(T3), ALU.add)
            tt(c(GRE), c(GRE), c(T1), ALU.mult)
            tt(c(T2), c(LIM), c(RE), ALU.mult)
            tt(c(T3), c(LRE), par("lim"), ALU.mult)
            tt(c(GIM), c(T2), c(T3), ALU.subtract)
            tt(c(GIM), c(GIM), c(T1), ALU.mult)
            tt(c(T2), c(GIM), par("sgn"), ALU.mult)
            ts(bmat[:, 0, :], par("b_mine"), c(GRE), None, ALU.mult, ALU.bypass)
            ts(bmat[:, 1, :], par("b_other"), c(T2), None, ALU.mult, ALU.bypass)
            tt(bmat[:, 2, :], bmat[:, 0, :], bmat[:, 1, :], ALU.add)
            then(nc.vector.tensor_copy(bmat[:, 3, :], bmat[:, 2, :]))
            marks["bmat"] = count[0]
            dve.wait_ge(setup_pe, 1)
            then(nc.vector.tensor_copy(bt[:, 0, :], ps[0][0][:, 0:P]))
            nc.vector.tensor_copy(bt[:, 1, 0:D], ps[0][0][:, D:P])
            ts(bt[:, 1, D:P], ps[0][0][:, 0:D], -1.0, None, ALU.mult, ALU.bypass)
            ts(c1[:, :], par("c1"), par("neg1"), None, ALU.mult, ALU.bypass)
            ts(c2[:, :], par("c2"), par("neg2"), None, ALU.mult, ALU.bypass)
            then(nc.vector.memset(cos[:, 0:1], 1.0))
            then(nc.vector.memset(sin[:, 0:1], 0.0))
            length = 1
            while length < T:
                lo, hi = slice(0, length), slice(length, 2 * length)
                ts(cos[:, hi], sin[:, lo], c(SI), -1.0, ALU.mult, ALU.mult)
                then(nc.vector.scalar_tensor_tensor(cos[:, hi], cos[:, lo], c(CO), cos[:, hi], ALU.mult, ALU.add))
                ts(sin[:, hi], cos[:, lo], c(SI), None, ALU.mult, ALU.bypass)
                then(nc.vector.scalar_tensor_tensor(sin[:, hi], sin[:, lo], c(CO), sin[:, hi], ALU.mult, ALU.add))
                tt(c(T1), c(CO), c(CO), ALU.mult)
                tt(c(T2), c(SI), c(SI), ALU.mult)
                tt(c(T3), c(CO), c(SI), ALU.mult)
                tt(c(CO), c(T1), c(T2), ALU.subtract)
                ts(c(SI), c(T3), 2.0, None, ALU.mult, ALU.bypass)
                length *= 2
            then(nc.vector.memset(decay[:, :], 1.0))
            ts(decay[:, :], decay[:, :], c(R), None, ALU.mult, ALU.bypass)
            marks["total"] = count[0]
            with dve.Fori(0, N) as i:
                for s in STREAMS:
                    wait_now(dve, S[s], i, "rstd")
                    nc.vector.tensor_tensor(xn[s][:, :], ps[s][0][:, :], sq[s][:, :], ALU.mult).then_inc(V[s].mark("norm"), 1)
                for q in range(2):
                    for s in STREAMS:
                        wait_now(dve, TE[s], i, f"bu{q}")
                        wait_now(dve, V[s], i, "states0") if q else wait_before(dve, V[s], i, "states1")
                        nc.vector.tensor_tensor(za[s][:, :], ps[s][2 * q][:, :], cos[:, :], ALU.mult).then_inc(V[s].mark(f"cos_part{q}"), 1)
                        nc.vector.tensor_tensor(zb[s][:, :], ps[s][2 * q + 1][:, :], sin[:, :], ALU.mult).then_inc(V[s].mark(f"sin_part{q}"), 1)
                    for s in STREAMS:
                        wait_now(dve, V[s], i, f"sin_part{q}")
                        nc.vector.tensor_tensor(zb[s][:, :], za[s][:, :], zb[s][:, :], ALU.add).then_inc(V[s].mark(f"rotated{q}"), 1)
                    for s in STREAMS:
                        wait_now(dve, V[s], i, f"rotated{q}")
                        wait_before(dve, G[s], i, f"back_sin{q}")
                        nc.vector.tensor_tensor_scan(y[s][:, q, :], decay[:, :], zb[s][:, :], 0.0, ALU.mult, ALU.add
                                                     ).then_inc(V[s].mark(f"states{q}"), 1)
                for s in STREAMS:
                    wait_now(dve, TE[s], i, "y")
                    dve.wait_ge(stored[s], i * 16)
                    nc.vector.scalar_tensor_tensor(ho[s][:, :], ps[s][0][:, :], 0.0, xn[s][:, :], ALU.max, ALU.add).then_inc(V[s].mark("relu"), 1)
                for s in STREAMS:
                    wait_now(dve, V[s], i, "relu")
                    nc.vector.tensor_tensor(ho[s][:, :], ho[s][:, :], h[s][:, :], ALU.add).then_inc(V[s].mark("out"), 1)

        @block.gpsimd
        def _(pool):
            for s in STREAMS:
                nc.gpsimd.sem_inc(G[s].sem, len(GS))
            pool.wait_ge(setup_v, marks["total"])
            with pool.Fori(0, N) as i:
                for q in range(2):
                    for s in STREAMS:
                        wait_now(pool, V[s], i, f"states{q}")
                        wait_before(pool, TE[s], i, "y")
                        nc.gpsimd.tensor_tensor(u1[s][:, q, :], y[s][:, q, :], cos[:, :], ALU.mult).then_inc(G[s].mark(f"back_cos{q}"), 1)
                        nc.gpsimd.tensor_tensor(u2[s][:, q, :], y[s][:, q, :], sin[:, :], ALU.mult).then_inc(G[s].mark(f"back_sin{q}"), 1)

        @block.scalar
        def _(act):
            for s in STREAMS:
                nc.scalar.sem_inc(S[s].sem, len(SSN))
            act.wait_ge(params_loaded, 16)
            nc.scalar.activation(c(STEP), par("lstep"), ACT.Exp).then_inc(setup_s, 1)
            act.wait_ge(setup_v, marks["angles"])
            nc.scalar.activation(c(R), c(T2), ACT.Exp).then_inc(setup_s, 1)
            nc.scalar.activation(c(SI), c(TS_), ACT.Sin).then_inc(setup_s, 1)
            nc.scalar.activation(c(CO), c(TC), ACT.Sin).then_inc(setup_s, 1)
            with act.Fori(0, N) as i:
                for s in STREAMS:
                    wait_now(act, TE[s], i, "center")
                    nc.scalar.activation(sq[s][:, :], ps[s][0][:, :], ACT.Square).then_inc(S[s].mark("square"), 1)
                for s in STREAMS:
                    wait_now(act, TE[s], i, "var")
                    nc.scalar.activation(sq[s][:, :], ps[s][1][:, :], ACT.Ln, bias=par("eps")).then_inc(S[s].mark("log"), 1)
                for s in STREAMS:
                    wait_now(act, S[s], i, "log")
                    nc.scalar.activation(sq[s][:, :], sq[s][:, :], ACT.Exp, scale=-0.5).then_inc(S[s].mark("rstd"), 1)

        @block.tensor
        def _(pe):
            for s in STREAMS:
                nc.tensor.sem_inc(TE[s].sem, len(TS))
            pe.wait_ge(params_loaded, 16)
            pe.wait_ge(setup_v, marks["bmat"])
            nc.tensor.transpose(ps[0][0][:, 0:P], bmat[:, 2:4, :].rearrange("p a d -> p (a d)"), par("ident")).then_inc(setup_pe, 1)
            pe.wait_ge(setup_v, marks["total"])
            with pe.Fori(0, N) as i:
                for s in STREAMS:
                    wait_load(pe, h_in[s], i)
                    nc.tensor.matmul(ps[s][0][:, :], par("cen2"), h[s][:, :], start=True, stop=True).then_inc(TE[s].mark("center"), 1)
                for s in STREAMS:
                    wait_now(pe, S[s], i, "square")
                    nc.tensor.matmul(ps[s][1][:, :], par("avg2"), sq[s][:, :], start=True, stop=True).then_inc(TE[s].mark("var"), 1)
                for q in range(2):
                    for s in STREAMS:
                        wait_now(pe, V[s], i, "norm")
                        for k in range(2):
                            last = nc.tensor.matmul(ps[s][2 * q + k][:, :], bt[D * q:D * (q + 1), k, :], xn[s][D * q:D * (q + 1), :], start=True, stop=True)
                        last.then_inc(TE[s].mark(f"bu{q}"), 1)
                for s in STREAMS:
                    wait_now(pe, G[s], i, "back_sin1")
                    for q in range(2):
                        nc.tensor.matmul(ps[s][0][D * q:D * (q + 1), :], c1[:, :], u1[s][:, q, :], start=True, stop=False)
                        last = nc.tensor.matmul(ps[s][0][D * q:D * (q + 1), :], c2[:, :], u2[s][:, q, :], start=False, stop=True)
                    last.then_inc(TE[s].mark("y"), 1)



def causal_stage(nc, dram):
    NPAIR, NSEQ = 2, 4
    R = NSEQ * NH2
    VR = 2 * HD2
    VW = P + VR
    NT = TB
    PREP, POST = 10, 2
    USES = NPAIR * PREP + NSEQ * POST
    starts = (2, 11)
    plan = [[] for _ in range(R + 2)]
    for n in range(NPAIR):
        at = starts[n]
        plan[at].append(("ms", n + 1, 0, 0))
        for q in range(2):
            for half in range(2):
                plan[at + 1 + 2 * q + half] += [("proj", n + 1, q, 2 * half), ("proj", n + 1, q, 2 * half + 1)]
        plan[at + 5].append(("v", n + 1, 0, 0))
    for m in range(NSEQ):
        plan[min(4 * m + 5, R + 1)].append(("sums", m, 0, 0))
        plan[min(4 * m + 6, R + 1)].append(("out", m, 0, 0))
    uses, u = [], 0
    for step in plan:
        uses.append([(u + k, *what) for k, what in enumerate(step)])
        u += len(step)
    assert u == USES
    first = [(k - PREP, *what) for k, what in enumerate(
        [("ms", 0, 0, 0)] + [("proj", 0, q, w) for q in range(2) for w in range(4)] + [("v", 0, 0, 0)])]

    with ExitStack() as ctx:
        def one(name, shape, dt=F32):
            return ctx.enter_context(nc.sbuf_tensor(f"causal_{name}", shape, dt))

        def sb(name, shape, dt=F32):
            return [one(f"{name}{k}", shape, dt) for k in range(2)]

        def sem(name):
            return nc.alloc_semaphore(f"causal_{name}")

        def bank(name):
            return ctx.enter_context(nc.psum_tensor(f"causal_{name}", [P, T], F32))

        params, par, params_loaded = load_params(nc, ctx, "causal", dram)
        h = sb("h", [P, T])
        sq, rs = one("sq", [P, T]), one("rs", [P, T])
        xn = sb("xn", [P, T])
        xs = one("xs", [P, 2, T], F32R)
        projections = ("wq", "wqr", "wk", "wkr")
        wh, wl = (one(f"projections_{part}", [P, 4 * P], F32R) for part in ("high", "low"))
        qt, kt = sb("qt", [P, 2, T]), sb("kt", [P, 2, T])
        qh = sb("qh", [P, 2, NH2, T])
        ident_b, mask_b = one("ident_bf16", [P, P], mybir.dt.bfloat16), one("mask_bf16", [P, P], mybir.dt.bfloat16)
        rot = sb("rot", [P, T])
        vp = sb("value_parts", [P, NT, 2, NH2 * VW], F32R)
        prob = sb("prob", [P, NT, T])
        pt_hi, pt_lo = ([one(f"turned_{part}{k}", [P, NT, T], F32R) for k in range(2)] for part in ("high", "low"))
        nmax = one("nmax", [P, 2, NT])
        rsum = sb("rsum", [P, NT, NH2])
        rsx = one("rsum_inverse", [P, NT, NH2, VR])
        rinv, on = one("rsum_turned", [P, T]), one("on", [P, T])
        ho = sb("ho", [P, T])
        lb = [bank(f"logits{k}") for k in range(3)]
        tb_ = [bank(f"turned{k}") for k in range(3)]
        X, values_bank = bank("spare"), bank("values")
        L_TILES, T_TILES, NU = ((3,), (0, 2), (1,)), ((0,), (1, 3), (2,)), 3
        L = [lb[1][:, 3 * P:4 * P], lb[2][:, 0:2 * P], lb[1][:, 0:3 * P], lb[0][:, :]]
        PT = [tb_[0][:, :], tb_[1][:, 0:3 * P], tb_[2][:, 0:2 * P], tb_[1][:, 3 * P:4 * P]]
        O = values_bank

        h_in, stored, extra = [sem(f"h_in{k}") for k in range(2)], [sem(f"stored{k}") for k in range(2)], sem("extra_copied")
        cleared, weighted = sem("zeros_set"), sem("weights_normed")

        def count(name, per_round):
            return Count(sem(name), per_round)

        logits, maxes, exps = count("logits", R * NU), count("maxes", R * NU), count("exps", R * NU)
        turned, turned_high, turned_low = (count(n, R * NU) for n in ("turned", "turned_high_made", "turned_low_made"))
        values = count("values", R)
        used, read = count("spare_written", USES), count("spare_read", USES)
        squared, logged, rstd, normed_h = (count(n, NPAIR) for n in ("squared", "logged", "rstd", "h_normed"))
        roped = count("roped", NPAIR * 4)
        split_high, split_low = count("xs_high", NPAIR * 2), count("xs_low", NPAIR * 2)
        masked, v_high = count("queries_apart", NPAIR * 2), count("values_high", NPAIR)
        inverted, weighed = count("sums_inverted", 2 * NSEQ), count("values_normed", NSEQ)
        block = ctx.enter_context(nc.Block())
        N = PAIRS // NPAIR

        def wait(eng, c, i, j):
            eng.wait_ge(c.sem, c.value(i, j))

        def prime(eng, *counts):
            for c in counts:
                eng.sem_inc(c.sem, c.per_round)

        def last_use(kind, n, q=0, w=0):
            for step in [first] + uses:
                for u, *what in step:
                    if what == [kind, n, q, w]:
                        return u

        def placed(n, q, rep, part):
            heads = vp[n % 2][:, :, q, :].rearrange("p t (k c) -> p t k c", c=2 * VW)
            return heads[:, :, :, rep * VW + part * HD2:rep * VW + (part + 1) * HD2]

        def made_values(q):
            return X[:, :].rearrange("p (t c) -> p t c", c=P)[:, :, q * NKV2 * HD2:(q + 1) * NKV2 * HD2].rearrange("p t (k d) -> p t k d", d=HD2)

        @block.sync
        def _(sp):
            sp.dma_start(params[:, :], dram["params_causal"]).then_inc(params_loaded, 16)
            sp.dma_start(dram["x3"][PAIRS], dram["x3"][0]).then_inc(extra, 16)
            sp.dma_start(h[0][:, :], dram["x3"][0]).then_inc(h_in[0], 16)
            sp.wait_ge(extra, 16)
            with sp.Fori(0, N) as i:
                for n in range(NPAIR):
                    wait(sp, read, i, last_use("out", 1) if n else last_use("out", 3) - USES)
                    sp.dma_start(h[(n + 1) % 2][:, :], dram["x3"][bass.ds(i * 2 + n + 1, 1), :, :].rearrange("a p t -> (a p) t")
                                 ).then_inc(h_in[(n + 1) % 2], 16)
                    wait(sp, read, i, last_use("out", 2 * n + 1))
                    sp.dma_start(dram["h4"][bass.ds(i * 2 + n, 1), :, :].rearrange("a p t -> (a p) t"), ho[n][:, :]).then_inc(stored[n], 16)
            for n in range(NPAIR):
                sp.wait_ge(stored[n], 16 * N)

        def landed(eng, i, n):
            eng.wait_ge(h_in[n % 2], i * 16 + 16 * (n // 2 + 1))

        @block.gpsimd
        def _(pool):
            prime(nc.gpsimd, roped)
            for k in range(2):
                last = nc.gpsimd.memset(vp[k][:, :, :, :].bitcast(F32), 0.0)
            last.then_inc(cleared, 1)

            def add_turned(i, n, q, w):
                dst = (qt, kt)[w // 2][n % 2][:, q, :]
                wait(pool, read, i, last_use("proj", n, q, w))
                nc.gpsimd.tensor_tensor(dst, dst, rot[w // 2][:, :], ALU.add).then_inc(roped.sem, 1)

            for q in range(2):
                for w in (1, 3):
                    add_turned(0, 0, q, w)
            with pool.Fori(0, N) as i:
                for step in uses:
                    for _, kind, n, q, w in step:
                        if kind == "proj" and w % 2:
                            add_turned(i, n, q, w)

        @block.scalar
        def _(act):
            prime(nc.scalar, exps, squared, logged, rstd, split_high, masked, v_high, turned_high)
            act.wait_ge(params_loaded, 16)
            act.wait_ge(cleared, 1)

            def norm(i, n):
                landed(act, i, n)
                wait(act, used, i, last_use("ms", n - 1) if n else -PREP - 1)
                nc.scalar.activation(sq[:, :], h[n % 2][:, :], ACT.Square).then_inc(squared.sem, 1)

            def root(i, n):
                wait(act, read, i, last_use("ms", n))
                nc.scalar.activation(rs[:, :], rs[:, :], ACT.Ln).then_inc(logged.sem, 1)
                wait(act, logged, i, n)
                nc.scalar.activation(rs[:, :], rs[:, :], ACT.Exp, scale=-0.5).then_inc(rstd.sem, 1)
                for q in range(2):
                    wait(act, normed_h, i, n)
                    rows = slice(D * q, D * (q + 1))
                    nc.scalar.activation(xs[rows, q, :], xn[n % 2][rows, :], ACT.Copy).then_inc(split_high.sem, 1)

            def queries_apart(i, n, q):
                wait(act, roped, i, n * 4 + q * 2)
                wait(act, logits, i, (n - 1) * 2 * NH2 * NU - 1)
                for hh in range(NH2):
                    last = nc.scalar.activation(qh[n % 2][:, q, hh, :], qt[n % 2][:, q, :], ACT.Copy, scale=par.cols("heads", hh, hh + 1))
                last.then_inc(masked.sem, 1)

            def values_high(i, n):
                wait(act, used, i, last_use("v", n))
                wait(act, values, i, (n - 1) * 2 * NH2 - 1)
                for q in range(2):
                    for rep in range(2):
                        last = nc.scalar.activation(placed(n, q, rep, 0), made_values(q), ACT.Copy)
                last.then_inc(v_high.sem, 1)

            norm(0, 0)
            root(0, 0)
            queries_apart(0, 0, 0)
            queries_apart(0, 0, 1)
            values_high(0, 0)
            def step(i, g):
                s = g // NH2
                for k, n in enumerate((1, 2)):
                    if g == starts[k]:
                        norm(i, n)
                wait(act, turned, i, (g - 2) * NU + NU - 1)
                for k, n in enumerate((1, 2)):
                    for q in range(2):
                        if g == starts[k] + 2 + 2 * q:
                            queries_apart(i, n, q)
                for u, tiles in enumerate(L_TILES):
                    if g >= 1:
                        if u == 0:
                            wait(act, values, i, g - 3)
                        wait(act, turned, i, (g - 1) * NU + u)
                        for t in T_TILES[u]:
                            last = nc.scalar.activation(pt_hi[(g - 1) % 2][:, t, t * P:T], PT[t], ACT.Copy)
                        last.then_inc(turned_high.sem, 1)
                    wait(act, maxes, i, g * NU + u)
                    for t in tiles:
                        last = nc.scalar.activation(prob[g % 2][:, t, 0:(t + 1) * P], L[t], ACT.Exp, bias=nmax[:, g % 2, t:t + 1],
                                                    accum_out=rsum[s % 2][:, t, g % NH2:g % NH2 + 1])
                    last.then_inc(exps.sem, 1)
                for k, n in enumerate((1, 2)):
                    if g == starts[k]:
                        root(i, n)
                    if g == starts[k] + 5:
                        values_high(i, n)

            step(0, 0)
            step(0, 1)
            with act.Fori(0, N) as i:
                for g in range(2, R + 2):
                    step(i, g)

        @block.vector
        def _(dve):
            prime(nc.vector, maxes, turned_low, normed_h, split_low, inverted, weighed)
            nc.vector.sem_inc(read.sem, USES - PREP)
            dve.wait_ge(params_loaded, 16)
            for k, w in enumerate(("wq", "wqr", "wk", "wkr", "wv")):
                last = nc.vector.tensor_scalar(par(w), par(w), par("ln"), None, ALU.mult)
            nc.vector.tensor_copy(ident_b[:, :], par("ident"))
            nc.vector.tensor_copy(mask_b[:, :], par("mask"))
            last.then_inc(weighted, 1)
            dve.wait_ge(weighted, 1)
            for k, w in enumerate(projections):
                last = nc.vector.tensor_copy(wh[:, k * P:(k + 1) * P], par(w))
            last.then_inc(weighted, 1)
            dve.wait_ge(weighted, 2)
            for k, w in enumerate(projections):
                last = nc.vector.tensor_tensor(wl[:, k * P:(k + 1) * P], par(w), wh[:, k * P:(k + 1) * P].bitcast(F32), ALU.subtract)
            last.then_inc(weighted, 1)

            def spare(i, u, kind, n, q, w):
                x = X
                if kind == "ms":
                    wait(dve, used, i, u)
                    wait(dve, normed_h, i, n - 1)
                    nc.vector.tensor_scalar(rs[:, :], x[:, :], par("eps"), None, ALU.add).then_inc(read.sem, 1)
                    wait(dve, rstd, i, n)
                    wait(dve, used, i, last_use("v", n - 1) if n else -PREP - 1)
                    nc.vector.tensor_tensor(xn[n % 2][:, :], h[n % 2][:, :], rs[:, :], ALU.mult).then_inc(normed_h.sem, 1)
                    for q in range(2):
                        own, other = slice(D * q, D * (q + 1)), slice(D * (1 - q), D * (2 - q))
                        wait(dve, split_high, i, 2 * n + q)
                        nc.vector.tensor_tensor(xs[other, q, :], xn[n % 2][own, :], xs[own, q, :].bitcast(F32), ALU.subtract).then_inc(split_low.sem, 1)
                elif kind == "proj":
                    wait(dve, used, i, u)
                    if w % 2 == 0:
                        wait(dve, logits, i, (n - 1) * 2 * NH2 * NU - 1)
                    else:
                        wait(dve, roped, i, n * 4 + q * 2 + w // 2 - 2)
                    dst = (qt, kt)[w // 2][n % 2][:, q, :] if w % 2 == 0 else rot[w // 2][:, :]
                    nc.vector.scalar_tensor_tensor(dst, x[:, :], HD2 ** -0.5 if w < 2 else 1.0, par("sin" if w % 2 else "cos"),
                                                   ALU.mult, ALU.mult).then_inc(read.sem, 1)
                elif kind == "v":
                    wait(dve, used, i, u)
                    wait(dve, v_high, i, n)
                    for q in range(2):
                        for rep in range(2):
                            last = nc.vector.tensor_tensor(placed(n, q, rep, 1), made_values(q), placed(n, q, rep, 0).bitcast(F32), ALU.subtract)
                    last.then_inc(read.sem, 1)
                elif kind == "sums":
                    wait(dve, used, i, u)
                    wait(dve, weighed, i, n - 1)
                    nc.vector.tensor_copy(rinv[:, :], x[:, :]).then_inc(read.sem, 1)
                    wait(dve, read, i, u)
                    wait(dve, values, i, n * NH2 + NH2 - 1)
                    nc.vector.tensor_tensor(on[:, :], O[:, :], rinv[:, :], ALU.mult).then_inc(weighed.sem, 1)
                else:
                    wait(dve, used, i, u)
                    rows = slice(D * (n % 2), D * (n % 2) + D)
                    if n % 2 == 0:
                        dve.wait_ge(stored[n // 2], i * 16)
                    nc.vector.tensor_tensor(ho[n // 2][rows, :], x[rows, :], h[n // 2][rows, :], ALU.add).then_inc(read.sem, 1)

            def sums_inverted(i, m):
                wait(dve, exps, i, m * NH2 * NU + NH2 * NU - 1)
                nc.vector.reciprocal(rsum[m % 2][:, :, :], rsum[m % 2][:, :, :]).then_inc(inverted.sem, 1)
                wait(dve, inverted, i, 2 * m)
                wait(dve, used, i, last_use("sums", m - 1) if m else last_use("sums", NSEQ - 1) - USES)
                nc.vector.tensor_copy(rsx[:, :, :, :], rsum[m % 2][:, :, :].rearrange("p t (h o) -> p t h o", o=1
                                                                                   ).to_broadcast((P, NT, NH2, VR))).then_inc(inverted.sem, 1)

            for u, kind, n, q, w in first:
                spare(0, u, kind, n, q, w)

            def step(i, g):
                for u in range(NU):
                    wait(dve, logits, i, g * NU + u)
                    wait(dve, exps, i, (g - 2) * NU + u)
                    for t in L_TILES[u]:
                        last = nc.vector.tensor_reduce(nmax[:, g % 2, t:t + 1], L[t], AX, ALU.max, negate=True)
                    last.then_inc(maxes.sem, 1)
                    if g >= 1:
                        wait(dve, turned_high, i, (g - 1) * NU + u)
                        for t in T_TILES[u]:
                            last = nc.vector.tensor_tensor(pt_lo[(g - 1) % 2][:, t, t * P:T], PT[t], pt_hi[(g - 1) % 2][:, t, t * P:T].bitcast(F32),
                                                           ALU.subtract)
                        last.then_inc(turned_low.sem, 1)
                if g >= NH2 and g % NH2 == 0:
                    sums_inverted(i, g // NH2 - 1)
                for u, kind, n, q, w in uses[g]:
                    spare(i, u, kind, n, q, w)

            step(0, 0)
            step(0, 1)
            with dve.Fori(0, N) as i:
                for g in range(2, R + 2):
                    step(i, g)

        @block.tensor
        def _(pe):
            prime(nc.tensor, logits, turned, values)
            nc.tensor.sem_inc(used.sem, USES - PREP)
            pe.wait_ge(params_loaded, 16)
            pe.wait_ge(weighted, 3)
            pe.wait_ge(cleared, 1)

            def spare(i, u, kind, n, q, w):
                x = X
                wait(pe, read, i, u - 1)
                if kind == "ms":
                    wait(pe, squared, i, n)
                    last = nc.tensor.matmul(x[:, :], par("avg2"), sq[:, :], start=True, stop=True)
                elif kind == "proj":
                    wait(pe, split_low, i, 2 * n + q)
                    for part in (wh, wl):
                        last = nc.tensor.matmul(x[:, :], part[:, w * P:(w + 1) * P], xs[:, q, :], start=part is wh, stop=part is wl)
                elif kind == "v":
                    for t in range(NT):
                        last = nc.tensor.matmul(x[:, t * P:(t + 1) * P], xn[n % 2][:, t * P:(t + 1) * P], par("wv"), start=True, stop=True)
                elif kind == "sums":
                    wait(pe, inverted, i, 2 * n + 1)
                    for t in range(NT):
                        last = nc.tensor.transpose(x[:, t * P:(t + 1) * P], rsx[:, t, :, :].rearrange("p h r -> p (h r)"), par("ident"))
                else:
                    wait(pe, weighed, i, n)
                    last = nc.tensor.matmul(x[:, :], par("wo"), on[:, :], start=True, stop=True)
                last.then_inc(used.sem, 1)

            for u, kind, n, q, w in first:
                spare(0, u, kind, n, q, w)

            def step(i, g):
                s = g // NH2
                for u in range(NU):
                    if u == 0:
                        wait(pe, roped, i, s * 2 + 1)
                        if g % NH2 == 0:
                            wait(pe, masked, i, s)
                    wait(pe, exps, i, (g - 1) * NU + u)
                    for t in L_TILES[u]:
                        nc.tensor.matmul(L[t], qh[s // 2 % 2][:, s % 2, g % NH2, t * P:(t + 1) * P], kt[s // 2 % 2][:, s % 2, 0:(t + 1) * P],
                                         start=True, stop=False)
                        last = nc.tensor.matmul(L[t][:, t * P:(t + 1) * P], ident_b[:, :], mask_b[:, :], start=False, stop=True)
                    last.then_inc(logits.sem, 1)
                    if g >= 1:
                        if u == 0:
                            wait(pe, exps, i, (g - 1) * NU + NU - 1)
                        wait(pe, turned_low, i, (g - 2) * NU + u)
                        for mt in T_TILES[u]:
                            for t in range(mt, NT):
                                last = nc.tensor.transpose(PT[mt][:, (t - mt) * P:(t - mt + 1) * P], prob[(g - 1) % 2][:, t, mt * P:(mt + 1) * P],
                                                           par("ident"))
                        last.then_inc(turned.sem, 1)
                if g >= 2:
                    v = g - 2
                    wait(pe, turned_low, i, v * NU + NU - 1)
                    if v % NH2 == 0:
                        wait(pe, weighed, i, v // NH2 - 1)
                    if v % (2 * NH2) == 0:
                        wait(pe, read, i, last_use("v", 1) if v else last_use("v", 2) - USES)
                    hh, sv = v % NH2, v // NH2
                    for mt in range(NT):
                        for part in (pt_hi, pt_lo):
                            last = nc.tensor.matmul(O[:, mt * P:T], vp[sv // 2][:, mt, sv % 2, hh * P:(hh + 1) * P], part[v % 2][:, mt, mt * P:T],
                                                    start=hh == 0 and mt == 0 and part is pt_hi,
                                                    stop=hh == NH2 - 1 and mt == NT - 1 and part is pt_lo)
                    last.then_inc(values.sem, 1)
                for u, kind, n, q, w in uses[g]:
                    spare(i, u, kind, n, q, w)

            wait(pe, read, 0, -1)
            step(0, 0)
            step(0, 1)
            with pe.Fori(0, N) as i:
                for g in range(2, R + 2):
                    step(i, g)



def norm_stage(nc, dram):
    VS, SSN, TS = ["norm"], ["square", "log", "rstd"], ["center", "var"]
    with ExitStack() as ctx:
        def sb(name, shape):
            return [ctx.enter_context(nc.sbuf_tensor(f"norm_{name}{s}", shape, F32)) for s in STREAMS]

        def sem(name):
            return nc.alloc_semaphore(f"norm_{name}")

        params, par, params_loaded = load_params(nc, ctx, "norm", dram)
        h, sq, xn = sb("h", [P, T]), sb("sq", [P, T]), sb("xn", [P, T])
        ps = [[ctx.enter_context(nc.psum_tensor(f"norm_ps{s}{k}", [P, T], F32)) for k in range(2)] for s in STREAMS]
        h_in, stored = ([sem(f"{n}{s}") for s in STREAMS] for n in ("h_in", "stored"))
        V = [Steps(sem(f"vector_steps{s}"), VS) for s in STREAMS]
        S = [Steps(sem(f"scalar_steps{s}"), SSN) for s in STREAMS]
        TE = [Steps(sem(f"tensor_steps{s}"), TS) for s in STREAMS]
        block = ctx.enter_context(nc.Block())
        N = PAIRS // 2

        @block.sync
        def _(sp):
            sp.dma_start(params[:, :], dram["params_norm"]).then_inc(params_loaded, 16)
            with sp.Fori(0, N) as i:
                for s in STREAMS:
                    wait_before(sp, TE[s], i, "center")
                    sp.dma_start(h[s][:, :], dram["h3"][bass.ds(i * 2 + s, 1), :, :].rearrange("a p t -> (a p) t")).then_inc(h_in[s], 16)
                for s in STREAMS:
                    wait_now(sp, V[s], i, "norm")
                    sp.dma_start(dram["x3"][bass.ds(i * 2 + s, 1), :, :].rearrange("a p t -> (a p) t"), xn[s][:, :]).then_inc(stored[s], 16)
            for s in STREAMS:
                sp.wait_ge(stored[s], 16 * N)

        @block.vector
        def _(dve):
            for s in STREAMS:
                nc.vector.sem_inc(V[s].sem, len(VS))
            with dve.Fori(0, N) as i:
                for s in STREAMS:
                    wait_now(dve, S[s], i, "rstd")
                    dve.wait_ge(stored[s], i * 16)
                    nc.vector.tensor_tensor(xn[s][:, :], ps[s][0][:, :], sq[s][:, :], ALU.mult).then_inc(V[s].mark("norm"), 1)

        @block.scalar
        def _(act):
            for s in STREAMS:
                nc.scalar.sem_inc(S[s].sem, len(SSN))
            act.wait_ge(params_loaded, 16)
            with act.Fori(0, N) as i:
                for s in STREAMS:
                    wait_now(act, TE[s], i, "center")
                    nc.scalar.activation(sq[s][:, :], ps[s][0][:, :], ACT.Square).then_inc(S[s].mark("square"), 1)
                for s in STREAMS:
                    wait_now(act, TE[s], i, "var")
                    nc.scalar.activation(sq[s][:, :], ps[s][1][:, :], ACT.Ln, bias=par("eps")).then_inc(S[s].mark("log"), 1)
                for s in STREAMS:
                    wait_now(act, S[s], i, "log")
                    nc.scalar.activation(sq[s][:, :], sq[s][:, :], ACT.Exp, scale=-0.5).then_inc(S[s].mark("rstd"), 1)

        @block.tensor
        def _(pe):
            for s in STREAMS:
                nc.tensor.sem_inc(TE[s].sem, len(TS))
            pe.wait_ge(params_loaded, 16)
            with pe.Fori(0, N) as i:
                for s in STREAMS:
                    wait_load(pe, h_in[s], i)
                    wait_before(pe, V[s], i, "norm")
                    nc.tensor.matmul(ps[s][0][:, :], par("cen2"), h[s][:, :], start=True, stop=True).then_inc(TE[s].mark("center"), 1)
                for s in STREAMS:
                    wait_now(pe, S[s], i, "square")
                    nc.tensor.matmul(ps[s][1][:, :], par("avg2"), sq[s][:, :], start=True, stop=True).then_inc(TE[s].mark("var"), 1)



def swiglu_stage(nc, dram):
    NT = NE + NE // 2
    QT = [(q, t) for q in range(2) for t in range(TB)]
    hidden0, hidden1 = ([f"hidden{q}_{k}" for k in range(NT)] for q in range(2))
    summed0, summed1 = ([f"{a}{q}{t}" for t in range(TB) for a in ("weighed", "summed")] for q in range(2))
    VS = (["norm", "low0", "low1", "both"] + hidden0
          + ["max", "shift", "sum", "invert", "probs", "compare", "lower", "above", "rank", "mask", "picked",
             "total", "guarded", "inverse", "weights"] + summed0 + hidden1 + summed1 + ["out"])
    silu, up, down = ([[f"{n}{k}" for k in range(count)] for n in names] for names, count in
                      ((("silu0_", "silu1_"), NT), (("up0_", "up1_"), NT), (("down0", "down1"), TB)))
    SSN = ["square", "log", "rstd", "high0", "high1"] + silu[0] + ["exp"] + silu[1]
    TS = ["ms"] + up[0] + ["score"] + down[0] + up[1] + down[1] + ["turn"]
    with ExitStack() as ctx:
        def sb(name, shape, dt=F32):
            return [ctx.enter_context(nc.sbuf_tensor(f"swiglu_{name}{s}", shape, dt)) for s in STREAMS]

        def sem(name):
            return nc.alloc_semaphore(f"swiglu_{name}")

        params, par, params_loaded = load_params(nc, ctx, "swiglu", dram)
        h, x = sb("h", [P, T]), sb("x", [P, T])
        sq, xn = sb("sq", [P, T]), sb("xn", [P, T])
        N8 = 2 * TB
        score, prob, mask = sb("score", [P, N8, NE]), sb("prob", [P, N8, NE]), sb("mask", [P, N8, NE])
        pick, small = sb("pick", [P, N8, NE]), sb("small", [P, 3, N8])
        ge, gt = sb("ge", [P, N8, NE, NE]), sb("gt", [P, N8, NE, NE])
        gate, hid = sb("gate", [P, 2, T]), sb("hid", [P, NT, T])
        xs = sb("xs", [P, 2, T], F32R)
        wh, wl = ([ctx.enter_context(nc.sbuf_tensor(f"swiglu_{n}_{part}", [P, NT * P], F32R)) for n in ("w1", "w3")]
                  for part in ("high", "low"))
        ym, z, o = sb("ym", [P, 2, NE, D]), sb("z", [P, TB, 2, D]), sb("o", [P, TB, 2, D])
        ps = [[ctx.enter_context(nc.psum_tensor(f"swiglu_ps{s}{k}", [P, T], F32)) for k in range(4)] for s in STREAMS]
        in_h, in_x, stored = ([sem(f"{n}{s}") for s in STREAMS] for n in ("h_in", "x_in", "stored"))
        scaled = sem("weights_scaled")
        V = [Steps(sem(f"vector_steps{s}"), VS) for s in STREAMS]
        S = [Steps(sem(f"scalar_steps{s}"), SSN) for s in STREAMS]
        TE = [Steps(sem(f"tensor_steps{s}"), TS) for s in STREAMS]
        block = ctx.enter_context(nc.Block())
        N = PAIRS // 2

        @block.sync
        def _(sp):
            sp.dma_start(params[:, :], dram["params_swiglu"]).then_inc(params_loaded, 16)
            with sp.Fori(0, N) as i:
                for s in STREAMS:
                    wait_before(sp, TE[s], i, "turn")
                    sp.dma_start(x[s][:, :], dram["h4"][bass.ds(i * 2 + s, 1), :, :].rearrange("a p t -> (a p) t")).then_inc(in_x[s], 16)
                    sp.dma_start(h[s][:, :], dram["h3"][bass.ds(i * 2 + s, 1), :, :].rearrange("a p t -> (a p) t")).then_inc(in_h[s], 16)
                for s in STREAMS:
                    wait_now(sp, V[s], i, "out")
                    for q in range(2):
                        sp.dma_start(dram["out"][bass.ds(i * 4 + 2 * s + q, 1), :, :].rearrange("a (t p) d -> (a p) t d", p=P), o[s][:, :, q, :]
                                     ).then_inc(stored[s], 16)
            for s in STREAMS:
                sp.wait_ge(stored[s], 32 * N)

        @block.vector
        def _(dve):
            for s in STREAMS:
                nc.vector.sem_inc(V[s].sem, len(VS))
            dve.wait_ge(params_loaded, 16)
            for name in ("router", "w1", "w3"):
                last = nc.vector.tensor_scalar(par(name), par(name), par("ln"), None, ALU.mult)
            last.then_inc(scaled, 1)
            dve.wait_ge(scaled, 1)
            for k, name in enumerate(("w1", "w3")):
                last = nc.vector.tensor_copy(wh[k][:, :], par(name))
            last.then_inc(scaled, 1)
            dve.wait_ge(scaled, 2)
            for k, name in enumerate(("w1", "w3")):
                last = nc.vector.tensor_tensor(wl[k][:, :], par(name), wh[k][:, :].bitcast(F32), ALU.subtract)
            last.then_inc(scaled, 1)
            with dve.Fori(0, N) as i:
                def each(name, op, *waits):
                    for s in STREAMS:
                        for steps, what in waits:
                            wait_now(dve, steps[s], i, what)
                        op(s).then_inc(V[s].mark(name), 1)

                def over(a):
                    return a.rearrange("p (n o) -> p n o", o=1).to_broadcast((P, N8, NE))

                tt, red = nc.vector.tensor_tensor, nc.vector.tensor_reduce
                each("norm", lambda s: tt(xn[s][:, :], x[s][:, :], sq[s][:, :], ALU.mult), (S, "rstd"))

                for q in range(2):
                    own, other = slice(D * q, D * (q + 1)), slice(D * (1 - q), D * (2 - q))
                    each(f"low{q}", lambda s: tt(xs[s][other, q, :], xn[s][own, :], xs[s][own, q, :].bitcast(F32), ALU.subtract),
                         (S, f"high{q}"))

                for s in STREAMS:
                    wait_load(dve, in_h[s], i)
                each("both", lambda s: tt(h[s][:, :], h[s][:, :], x[s][:, :], ALU.add))
                def logits(s):
                    return ps[s][1][:, 0:N8 * NE].rearrange("p (n e) -> p n e", e=NE)

                for q in range(2):
                    for k in range(NT):
                        each(f"hidden{q}_{k}", lambda s: tt(hid[s][:, k, :], ps[s][2 * (k % 2) + 1][:, :], gate[s][:, k % 2, :], ALU.mult),
                             (S, f"silu{q}_{k}"), *([(TE, f"down0{TB - 1}")] if (q, k) == (1, 0) else []))
                    if q == 0:
                        each("max", lambda s: red(small[s][:, 0, :], logits(s), AX, ALU.max), (TE, "score"))
                        each("shift", lambda s: tt(score[s][:, :, :], logits(s), over(small[s][:, 0, :]), ALU.subtract), (V, "max"))
                        each("sum", lambda s: red(small[s][:, 1, :], prob[s][:, :, :], AX, ALU.add), (S, "exp"))
                        each("invert", lambda s: nc.vector.reciprocal(small[s][:, 1, :], small[s][:, 1, :]), (V, "sum"))
                        each("probs", lambda s: tt(score[s][:, :, :], prob[s][:, :, :], over(small[s][:, 1, :]), ALU.mult), (V, "invert"))
                        for s in STREAMS:
                            wait_now(dve, V[s], i, "probs")
                            top2(nc, V[s], lambda name, s=s: wait_now(dve, V[s], i, name), score[s], ge[s], gt[s], mask[s], par("tri"))
                        each("picked", lambda s: tt(pick[s][:, :, :], score[s][:, :, :], mask[s][:, :, :], ALU.mult), (V, "mask"))
                        each("total", lambda s: red(small[s][:, 2, :], pick[s][:, :, :], AX, ALU.add), (V, "picked"))
                        each("guarded", lambda s: nc.vector.tensor_scalar(small[s][:, 2, :], small[s][:, 2, :], 1e-9, None, ALU.add), (V, "total"))
                        each("inverse", lambda s: nc.vector.reciprocal(small[s][:, 2, :], small[s][:, 2, :]), (V, "guarded"))
                        each("weights", lambda s: tt(mask[s][:, :, :], pick[s][:, :, :], over(small[s][:, 2, :]), ALU.mult), (V, "inverse"))
                    for t in range(TB):
                        before = QT[q * TB + t - 2] if q * TB + t >= 2 else None
                        each(f"weighed{q}{t}", lambda s: tt(
                            ym[s][:, t % 2], ps[s][2 + t % 2][:, :].rearrange("p (e d) -> p e d", e=NE),
                            mask[s][:, 2 * t + q, :].rearrange("p (e o) -> p e o", o=1).to_broadcast((P, NE, D)), ALU.mult),
                            (TE, f"down{q}{t}"), (V, "summed%d%d" % before if before else "weights"))
                        each(f"summed{q}{t}", lambda s: red(z[s][:, t, q, :], ym[s][:, t % 2].rearrange("p e d -> p d e"), AX, ALU.add),
                             (V, f"weighed{q}{t}"))
                for s in STREAMS:
                    wait_now(dve, TE[s], i, "turn")
                    wait_now(dve, V[s], i, f"summed1{TB - 1}")
                    dve.wait_ge(stored[s], i * 32)
                    tt(o[s][:].rearrange("p t q d -> p (t q d)"), ps[s][0][:, :], z[s][:].rearrange("p t q d -> p (t q d)"), ALU.add
                       ).then_inc(V[s].mark("out"), 1)

        @block.scalar
        def _(act):
            for s in STREAMS:
                nc.scalar.sem_inc(S[s].sem, len(SSN))
            act.wait_ge(params_loaded, 16)
            with act.Fori(0, N) as i:
                for s in STREAMS:
                    wait_load(act, in_x[s], i)
                    nc.scalar.activation(sq[s][:, :], x[s][:, :], ACT.Square).then_inc(S[s].mark("square"), 1)
                for s in STREAMS:
                    wait_now(act, TE[s], i, "ms")
                    nc.scalar.activation(sq[s][:, :], ps[s][0][:, :], ACT.Ln, bias=par("eps")).then_inc(S[s].mark("log"), 1)
                for s in STREAMS:
                    wait_now(act, S[s], i, "log")
                    nc.scalar.activation(sq[s][:, :], sq[s][:, :], ACT.Exp, scale=-0.5).then_inc(S[s].mark("rstd"), 1)
                for q in range(2):
                    for s in STREAMS:
                        wait_now(act, V[s], i, "norm")
                        nc.scalar.activation(xs[s][D * q:D * (q + 1), q, :], xn[s][D * q:D * (q + 1), :], ACT.Copy
                                             ).then_inc(S[s].mark(f"high{q}"), 1)
                for q in range(2):
                    for k in range(NT):
                        for s in STREAMS:
                            wait_now(act, TE[s], i, f"up{q}_{k}")
                            nc.scalar.activation(gate[s][:, k % 2, :], ps[s][2 * (k % 2)][:, :], ACT.Silu).then_inc(S[s].mark(f"silu{q}_{k}"), 1)
                    for s in STREAMS:
                        if q == 0:
                            wait_now(act, V[s], i, "shift")
                            nc.scalar.activation(prob[s][:, :, :], score[s][:, :, :], ACT.Exp).then_inc(S[s].mark("exp"), 1)

        @block.tensor
        def _(pe):
            for s in STREAMS:
                nc.tensor.sem_inc(TE[s].sem, len(TS))
            pe.wait_ge(params_loaded, 16)
            pe.wait_ge(scaled, 3)
            with pe.Fori(0, N) as i:
                for s in STREAMS:
                    wait_now(pe, S[s], i, "square")
                    wait_before(pe, V[s], i, "out")
                    nc.tensor.matmul(ps[s][0][:, :], par("avg2"), sq[s][:, :], start=True, stop=True).then_inc(TE[s].mark("ms"), 1)
                for q in range(2):
                    for k in range(NT):
                        for s in STREAMS:
                            if k >= 2:
                                wait_now(pe, V[s], i, f"hidden{q}_{k - 2}")
                            elif k == 1 and q == 1:
                                wait_now(pe, V[s], i, f"weighed0{TB - 1}")
                            elif k == 0 and q == 0:
                                wait_now(pe, V[s], i, "low1")
                            elif k == 0:
                                wait_now(pe, V[s], i, "shift")
                            for w in range(2):
                                for part in (wh, wl):
                                    last = nc.tensor.matmul(ps[s][2 * (k % 2) + w][:, :], part[w][:, k * P:(k + 1) * P], xs[s][:, q, :],
                                                            start=part is wh, stop=part is wl)
                            last.then_inc(TE[s].mark(f"up{q}_{k}"), 1)
                    for s in STREAMS:
                        if q == 0:
                            wait_now(pe, V[s], i, f"hidden0_{NT - 2}")
                            for t in range(TB):
                                last = nc.tensor.matmul(ps[s][1][:, t * 2 * NE:(t + 1) * 2 * NE], xn[s][:, t * P:(t + 1) * P], par("router"),
                                                        start=True, stop=True)
                            last.then_inc(TE[s].mark("score"), 1)
                    for t in range(TB):
                        for s in STREAMS:
                            if t == 0:
                                wait_now(pe, V[s], i, f"hidden{q}_{NT - 1}")
                            elif t >= 2:
                                wait_now(pe, V[s], i, f"weighed{q}{t - 2}")
                            for j in range(NE // 2):
                                cols = slice(t * P, (t + 1) * P)
                                nc.tensor.matmul(ps[s][2 + t % 2][:, 2 * j * D:2 * (j + 1) * D], hid[s][:, NE + j, cols],
                                                 par.cols("w2r", 2 * j * D, 2 * (j + 1) * D), start=True, stop=False)
                                for e in (2 * j, 2 * j + 1):
                                    last = nc.tensor.matmul(ps[s][2 + t % 2][:, 2 * j * D:2 * (j + 1) * D], hid[s][:, e, cols],
                                                            par.cols("w2", e * P, (e + 1) * P), start=False, stop=e % 2 == 1)
                            last.then_inc(TE[s].mark(f"down{q}{t}"), 1)
                for s in STREAMS:
                    wait_now(pe, V[s], i, f"hidden1_{NT - 1}")
                    for t in range(TB):
                        last = nc.tensor.transpose(ps[s][0][:, t * P:(t + 1) * P], h[s][:, t * P:(t + 1) * P], par("ident"))
                    last.then_inc(TE[s].mark("turn"), 1)


def build(nc, dram, run=None):
    scratch = {"match": (B, len(MATCH), T), "h0": (PAIRS, P, T), "h1": (PAIRS, P, T), "h2": (PAIRS, P, T),
               "h3": (PAIRS, P, T), "x3": (PAIRS + 1, P, T), "h4": (PAIRS, P, T), "tokens": (B + 1, P, TB, 3 * D), "gram": (B, P, P),
               "blocks": (B + 1, D, D)}
    for name, shape in scratch.items():
        if name not in dram:
            dram[name] = nc.dram_tensor(name, shape, F32, kind="Internal").ap()
    dram["index"] = nc.dram_tensor("index_rows", (P, PAIRS * NSCALE * TB * 2), I32, kind="Internal").ap()
    for stage in (hash_stage, token_stage, qkv_stage, qr_stage, attention_stage, gelu_stage, ssm_stage, norm_stage,
                  causal_stage, swiglu_stage):
        if run is None or stage.__name__ in run:
            with nc.cleanup_on_exit():
                stage(nc, dram)



def pad_rows(a, rows=P):
    out = np.zeros((rows, a.shape[1]), np.float32)
    out[:a.shape[0]] = a
    return out


def col(a):
    return a.reshape(-1, 1)


def two(a):
    return np.concatenate([a, a], axis=0)


def apart(a):
    zero = np.zeros_like(a)
    return np.concatenate([np.concatenate([a, zero], axis=1), np.concatenate([zero, a], axis=1)])


def rows_of(a, n=P):
    return np.broadcast_to(a.reshape(1, -1), (n, a.size))


def cols_of(a):
    return a.transpose(1, 0, 2).reshape(a.shape[1], -1)


def beside(a):
    out = np.zeros((a.shape[1], NE, 2, D), np.float32)
    for e in range(NE):
        out[:, e, e % 2] = a[e]
    return out.reshape(a.shape[1], -1)


def for_outputs(w, heads):
    out = np.broadcast_to(w.reshape(heads, 1, D // heads, 1, D), (heads, 2, D // heads, 2, D))
    return out.reshape(P, P)


def feature_rows():
    quad_b, quad_c, const = np.zeros((24, 3 * P)), np.zeros((24, 3 * P)), np.zeros((24, P))
    for h in range(HEADS):
        for m, (i, j) in enumerate(mono_pairs()):
            quad_b[HEADS + h, h * MONO + m] = 1 if i == j else 2
            quad_c[2 * HEADS + h, h * MONO + m] = 1 if i == j else 2
        quad_b[h, NQUAD + h * HD:NQUAD + (h + 1) * HD] = 1
    const[:, NFEAT - 1 - 2 * P] = 1
    return quad_b.astype(np.float32), quad_c.astype(np.float32), const.astype(np.float32)


def rope_tables():
    inv_freq = 1.0 / 10000.0 ** (np.arange(0, HD2, 2, dtype=np.float32) / HD2)
    freqs = np.outer(np.arange(T, dtype=np.float32), inv_freq)
    emb = np.concatenate([freqs, freqs], axis=-1).T
    sign = np.where(np.arange(HD2) < HD2 // 2, -1, 1)[:, None]
    cos, sin = np.zeros((P, T), np.float32), np.zeros((P, T), np.float32)
    for h in range(NH2):
        cos[32 * h:32 * h + HD2] = np.cos(emb)
        sin[32 * h:32 * h + HD2] = np.sin(emb) * sign
    return cos, sin


def heads_apart(w, rep, turned):
    out = np.zeros((D, P), np.float32)
    for h in range(NH2):
        rows = w[(h // rep) * HD2:(h // rep + 1) * HD2]
        if turned:
            rows = np.concatenate([rows[HD2 // 2:], rows[:HD2 // 2]], axis=0)
        out[:, 32 * h:32 * h + HD2] = rows.T
    return out


def hidden_tiles(w):
    out = np.zeros((D, 12, P), np.float32)
    for e in range(NE):
        out[:, e] = w[e, :P].T
        out[:, NE + e // 2, 64 * (e % 2):64 * (e % 2) + REST] = w[e, P:].T
    return out.reshape(D, 12 * P)


def lay_out(a):
    t = {k[7:]: v for k, v in a.items() if k.startswith("L0_tok_")}
    n = {k[8:]: v for k, v in a.items() if k.startswith("L0_attn_")}
    g = {k[7:]: v for k, v in a.items() if k.startswith("L0_ffn_")}
    s = {k[8:]: v for k, v in a.items() if k.startswith("L1_attn_")}
    m = {k[7:]: v for k, v in a.items() if k.startswith("L1_ffn_")}
    eye = np.eye(P, dtype=np.float32)
    halves = np.kron(np.eye(2), np.ones((D, D))).astype(np.float32)
    quad_b, quad_c, const = feature_rows()
    cos, sin = rope_tables()
    start = np.broadcast_to((np.arange(T) % CHUNK == 0).astype(np.float32), (2 * SS, T))
    tri = np.broadcast_to((np.arange(NE)[:, None] > np.arange(NE)[None]).astype(np.float32).reshape(1, -1), (P, NE * NE))
    rest = np.zeros((P, NE, D), np.float32)
    for e in range(NE):
        rest[64 * (e % 2):64 * (e % 2) + REST, e] = m["w2"][e, :, P:].T
    eps5 = np.full((P, 1), 1e-5, np.float32)
    half = np.where(np.arange(P)[:, None] < D, 1, -1).astype(np.float32)
    parts = {
        "token": dict(
            embT=np.concatenate([t["emb_byte"].T, t["emb_byte"].T], axis=1), wq=t["Wq"], bq=rows_of(t["bq"]),
            win_e=t["Win"][:D], w1a=two(t["Win"][D:2 * D]), w1b=two(t["Win"][D:2 * D]), wmf=pad_rows(t["Win"][2 * D:]),
            b_in=col(t["b_in"]), wg=t["Wg"], wi=t["Wi"], bg=two(col(t["bg"])), bi=two(col(t["bi"])),
            woT=np.concatenate([t["Wo"].T, t["Wo"].T], axis=1), bo=col(t["bo"]), ln_g=col(t["ln_g"]),
            ln_b=col(t["ln_b"]), mlp_w=cols_of(t["mlp_w"]), mlp_b=t["mlp_b"].T, wout=t["Wout"],
            bout=two(col(t["bout"])), conv_w=two(t["conv_w"].reshape(D, 4)), conv_b=two(col(t["conv_b"])),
            cen=eye - np.float32(1 / H), avg=np.full((P, P), 1 / H, np.float32), ident=eye,
            iota=two(col(np.arange(VOCAB, dtype=np.float32))), first=start, rest=1 - start, eps=eps5),
        "qkv": dict(cen2=eye - halves / D, avg2=halves / D, wqkv=two(n["w_qkv"].T), bqkv=rows_of(n["b_qkv"]),
                    eps=eps5),
        "qr": dict(eye=rows_of(np.tile(np.eye(HD, dtype=np.float32), (4, 1)))),
        "attn": dict(
            ident=eye, convT=n["conv_w"].T, gamma=col(n["bn_gamma"]), beta=col(n["bn_beta"]),
            mean=col(n["bn_mean"]), var=col(n["bn_var"]),
            scales=col(np.concatenate([np.broadcast_to(n[k].reshape(1), (HEADS,)) for k in
                                       ("scale", "riem_scale", "grassman_scale")])),
            conv_b=rows_of(n["conv_b"]), sel_b=quad_b, sel_c=quad_c, sel_1=const,
            last=col(np.arange(P) == NFEAT - 1 - 2 * P).astype(np.float32),
            wproj=for_outputs(n["w_proj"].T, HEADS), bproj=two(col(n["b_proj"])),
            eps=eps5[:24]),
        "gelu": dict(cen2=eye - halves / D, avg2=halves / D, ident=eye, wg=apart(g["Wg"]), bg=rows_of(g["bg"]),
                     w1=two(cols_of(g["W1"])), b1=g["b1"].T, w2=beside(g["W2"]), b2=pad_rows(g["b2"]), tri=tri, eps=eps5),
        "ssm": dict(
            cen2=eye - halves / D, avg2=halves / D, lre=two(col(s["Lambda_re"])), lim=two(col(s["Lambda_im"])),
            lstep=two(col(s["log_step"])), b_mine=np.concatenate([s["B_re"], s["B_im"]]),
            b_other=np.concatenate([s["B_im"], s["B_re"]]), sgn=-half,
            c1=np.concatenate([s["C_re"].T, s["C_im"].T]), c2=np.concatenate([s["C_im"].T, s["C_re"].T]),
            neg1=half, neg2=-np.ones((P, 1), np.float32), ident=eye, eps=eps5),
        "norm": dict(cen2=eye - halves / D, avg2=halves / D, eps=eps5),
        "causal": dict(
            avg2=halves / D, ident=eye, ln=two(col(m["ln1_w"])), wq=two(heads_apart(m["wq"], 1, False)),
            wqr=two(heads_apart(m["wq"], 1, True)), wk=two(heads_apart(m["wk"], 2, False)),
            wkr=two(heads_apart(m["wk"], 2, True)), wv=np.concatenate([apart(m["wv"].T), np.zeros((P, D), np.float32)], axis=1),
            heads=(np.arange(P)[:, None] // 32 == np.arange(NH2)[None]).astype(np.float32),
            wo=for_outputs(m["wo"].T, NH2), cos=cos, sin=sin,
            mask=np.where(np.arange(P)[:, None] >= np.arange(P)[None], 0, -1e30).astype(np.float32),
            eps=np.full((P, 1), 1e-6, np.float32)),
        "swiglu": dict(avg2=halves / D, ident=eye, ln=two(col(m["ln2_w"])), router=apart(m["router_w"].T),
                       w1=two(hidden_tiles(m["w1"])), w3=two(hidden_tiles(m["w3"])),
                       w2=beside(m["w2"][:, :, :P].transpose(0, 2, 1)), w2r=rest.reshape(P, NE * D),
                       tri=tri, eps=np.full((P, 1), 1e-6, np.float32)),
    }
    out = {}
    for stage in STAGES:
        where, width = spec(stage)
        whole = np.zeros((P, width), np.float32)
        assert set(where) == set(parts[stage]), (stage, set(where) ^ set(parts[stage]))
        for name, (rows, at, cols) in where.items():
            part = parts[stage][name]
            assert part.shape == (rows, cols), (name, part.shape, rows, cols)
            whole[:rows, at:at + cols] = part
        out[f"params_{stage}"] = whole
    out["x"] = a["x"]
    out["hash_tables"] = t["hash_tables"].reshape(NSCALE * HASH_MOD, D)
    return out


def kernel(**inputs):
    import concourse.bacc as bacc
    from concourse.bass_utils import run_bass_kernel_spmd

    arrays = {k: np.ascontiguousarray(v) for k, v in lay_out({k: np.asarray(v) for k, v in inputs.items()}).items()}
    nc = bacc.Bacc("TRN2", target_bir_lowering=False, num_devices=1)
    dram = {k: nc.dram_tensor(k, v.shape, mybir.dt.from_np(v.dtype), kind="ExternalInput").ap() for k, v in arrays.items()}
    dram["out"] = nc.dram_tensor("out", (B, T, D), F32, kind="ExternalOutput").ap()
    build(nc, dram)
    result = run_bass_kernel_spmd(nc, [arrays], core_ids=[0])
    return result.results[0]["out"]
```
